# Optimizing a Trainium2 kernel written in Bass

```python
import numpy as np
import jax
import jax.numpy as jnp

def _softmax(x, axis=-1):
    return jax.nn.softmax(x, axis=axis)

def _gelu(x):
    return jax.nn.gelu(x, approximate=True)

def _silu(x):
    return jax.nn.silu(x)

def _sigmoid(x):
    return jax.nn.sigmoid(x)

def _layernorm(x, axis=-1, eps=1e-05):
    m = jnp.mean(x, axis=axis, keepdims=True)
    v = jnp.var(x, axis=axis, keepdims=True)
    return (x - m) / jnp.sqrt(v + eps)

def _scatter_add(tgt, idx, src, axis=0):
    return tgt.at[idx].add(src)

def _segment_sum(src, seg, n):
    return jax.ops.segment_sum(src, seg, n)
kernel_name = 'mk_xattn_ffn_d2_seqx_r8_e7f5ba'

def setup_inputs(seed: int=0):
    np.random.seed(seed)
    _w = jnp.asarray

    def _rec_inputs():
        import jax
        import jax.numpy as jnp
        _rk = jax.random.key(seed)
        x = 0.0003765 + 1 * jax.random.normal(jax.random.fold_in(_rk, 1), (16, 128, 256), jnp.float32)
        _lenS = 128 - jax.random.randint(jax.random.fold_in(_rk, 7), (16,), 0, max(1, 128 // 4) + 1, jnp.int32)
        _lenS2 = 128 - jax.random.randint(jax.random.fold_in(_rk, 8), (16,), 0, max(1, 128 // 4) + 1, jnp.int32)
        _ctx_2048P = jax.random.normal(jax.random.fold_in(_rk, 11), (16, 16, 256), jnp.float32)
        _ctx_2048c = jax.random.dirichlet(jax.random.fold_in(_rk, 511), 0.3 * jnp.ones((16,), jnp.float32), (16, 128))
        _ctx_2048t = jnp.einsum('bsk,bkd->bsd', _ctx_2048c, _ctx_2048P)
        _ctx_2048t = _ctx_2048t * jax.lax.rsqrt(jnp.mean(jnp.square(_ctx_2048t)) + 1e-12) * 0.953939
        ctx_2048 = -0.000292821 + 1.00034 * (_ctx_2048t + 0.3 * jax.random.normal(jax.random.fold_in(_rk, 611), (16, 128, 256), jnp.float32))
        _validS = jnp.arange(128)[None, :] < _lenS[:, None]
        _validS2 = jnp.arange(128)[None, :] < _lenS2[:, None]
        _causal = jnp.tril(jnp.ones((128, 128), dtype=bool))
        mask_Bx1x2048_fk1 = jnp.where(jnp.ones((16, 1, 256), dtype=bool), 1.0, 0.0).astype(jnp.float32)
        return (x, ctx_2048, mask_Bx1x2048_fk1)
    x, ctx_2048, mask_Bx1x2048_fk1 = _rec_inputs()

    def _L0_xattn_setup():
        import jax, jax.numpy as jnp
        import numpy as np
        key = jax.random.key(seed)
        k1, k2, k3, k4, k5 = jax.random.split(key, 5)
        B, D_MODEL, L = (2, 128, 256)
        HEAD_DIM = 8
        H = D_MODEL // HEAD_DIM
        return {'k': jax.random.normal(k1, (B, D_MODEL, L), dtype=jnp.float32), 'v': jax.random.normal(k2, (B, D_MODEL, L), dtype=jnp.float32), 'q': jax.random.normal(k3, (B, D_MODEL, L), dtype=jnp.float32), 'ssm_kernel': jax.random.normal(k4, (H, L), dtype=jnp.float32), 'D': jax.random.normal(k5, (H,), dtype=jnp.float32), 'head_dim': HEAD_DIM}
    _L0_xattn_all = _L0_xattn_setup()
    _L0_xattn_in = {k: v for k, v in _L0_xattn_all.items() if k in ('ssm_kernel', 'D')}
    del _L0_xattn_all

    def _L0_ffn_setup():
        import jax, jax.numpy as jnp
        import numpy as np
        D_MODEL = 256
        HIDDEN = 4 * D_MODEL
        B, S = (2, 512)

        def bit_linear(x, w, b):
            gamma_x = jnp.clip(jnp.max(jnp.abs(x), axis=-1, keepdims=True), 1e-05, None)
            scale_x = 127.0 / gamma_x
            x_dq = jnp.clip(jnp.round(x * scale_x), -128.0, 127.0) / scale_x
            x_ste = x + jax.lax.stop_gradient(x_dq - x)
            gamma_w = jnp.clip(jnp.mean(jnp.abs(w)), 1e-05, None)
            w_dq = jnp.clip(jnp.round(w / gamma_w), -1.0, 1.0) * gamma_w
            w_ste = w + jax.lax.stop_gradient(w_dq - w)
            return jnp.einsum('bsd,hd->bsh', x_ste, w_ste) + b
        key = jax.random.key(seed)
        ks = jax.random.split(key, 7)
        std = 0.02
        return {'x': jax.random.normal(ks[0], (B, S, D_MODEL), dtype=jnp.float32), 'gate_w': jax.random.normal(ks[1], (HIDDEN, D_MODEL), dtype=jnp.float32) * std, 'gate_b': jnp.zeros((HIDDEN,), dtype=jnp.float32), 'val_w': jax.random.normal(ks[2], (HIDDEN, D_MODEL), dtype=jnp.float32) * std, 'val_b': jnp.zeros((HIDDEN,), dtype=jnp.float32), 'out_w': jax.random.normal(ks[3], (D_MODEL, HIDDEN), dtype=jnp.float32) * std, 'out_b': jnp.zeros((D_MODEL,), dtype=jnp.float32)}
    _L0_ffn_all = _L0_ffn_setup()
    _L0_ffn_in = {k: v for k, v in _L0_ffn_all.items() if k in ('gate_w', 'gate_b', 'val_w', 'val_b', 'out_w', 'out_b')}
    del _L0_ffn_all

    def _L1_xattn_setup():
        import math
        import jax, jax.numpy as jnp
        import numpy as np
        SIZE = 128
        HEADS = 16
        HEAD_DIM = SIZE // HEADS
        B, T, S = (2, 256, 256)
        NEG = 1000000.0
        key = jax.random.key(seed)
        ks = jax.random.split(key, 10)
        target = jax.random.normal(ks[0], (B, SIZE, T), dtype=jnp.float32)
        source = jax.random.normal(ks[1], (B, SIZE, S), dtype=jnp.float32)
        target_mask = (jax.random.uniform(ks[2], (B, 1, T)) > 0.1).astype(jnp.float32)
        source_mask = (jax.random.uniform(ks[3], (B, 1, S)) > 0.1).astype(jnp.float32)
        scale = 1.0 / math.sqrt(SIZE)
        Wq = jax.random.normal(ks[4], (SIZE, SIZE), dtype=jnp.float32) * scale
        Wk = jax.random.normal(ks[5], (SIZE, SIZE), dtype=jnp.float32) * scale
        Wv = jax.random.normal(ks[6], (SIZE, SIZE), dtype=jnp.float32) * scale
        bq = jax.random.normal(ks[7], (SIZE,), dtype=jnp.float32) * 0.01
        bk = jax.random.normal(ks[8], (SIZE,), dtype=jnp.float32) * 0.01
        bv = jax.random.normal(ks[9], (SIZE,), dtype=jnp.float32) * 0.01
        return {'target': target, 'source': source, 'target_mask': target_mask, 'source_mask': source_mask, 'Wq': Wq, 'bq': bq, 'Wk': Wk, 'bk': bk, 'Wv': Wv, 'bv': bv}
    _L1_xattn_all = _L1_xattn_setup()
    _L1_xattn_in = {k: v for k, v in _L1_xattn_all.items() if k in ('Wq', 'bq', 'Wk', 'bk', 'Wv', 'bv')}
    del _L1_xattn_all

    def _L1_ffn_setup():
        import jax, jax.numpy as jnp
        import numpy as np
        N_ACTIVE = 32
        key = jax.random.key(seed)
        ks = jax.random.split(key, 6)
        B, T, D, G, GD = (4, 256, 256, 512, 32)
        x = jax.random.normal(ks[0], (B, T, D), jnp.float32)
        Wc = jax.random.normal(ks[1], (G, D), jnp.float32) * D ** (-0.5)
        temperature = jnp.array(1.0, jnp.float32)
        genes = jax.random.normal(ks[2], (G, GD), jnp.float32) * 0.02
        Wd = jax.random.normal(ks[3], (D, GD), jnp.float32) * GD ** (-0.5)
        Wu = jax.random.normal(ks[4], (D, GD), jnp.float32) * 0.02
        norm_w = jnp.ones((D,), jnp.float32)
        scale = jnp.array(0.1, jnp.float32)
        return {'x': x, 'Wc': Wc, 'temperature': temperature, 'genes': genes, 'Wd': Wd, 'Wu': Wu, 'norm_w': norm_w, 'scale': scale}
    _L1_ffn_all = _L1_ffn_setup()
    _L1_ffn_in = {k: v for k, v in _L1_ffn_all.items() if k in ('Wc', 'temperature', 'genes', 'Wd', 'Wu', 'norm_w', 'scale')}
    del _L1_ffn_all
    return {'x': x, 'ctx_2048': ctx_2048, 'mask_Bx1x2048_fk1': mask_Bx1x2048_fk1, 'L0_xattn_ssm_kernel': _L0_xattn_in['ssm_kernel'], 'L0_xattn_D': _L0_xattn_in['D'], 'L0_ffn_gate_w': _L0_ffn_in['gate_w'], 'L0_ffn_gate_b': _L0_ffn_in['gate_b'], 'L0_ffn_val_w': _L0_ffn_in['val_w'], 'L0_ffn_val_b': _L0_ffn_in['val_b'], 'L0_ffn_out_w': _L0_ffn_in['out_w'], 'L0_ffn_out_b': _L0_ffn_in['out_b'], 'L1_xattn_Wq': _L1_xattn_in['Wq'], 'L1_xattn_bq': _L1_xattn_in['bq'], 'L1_xattn_Wk': _L1_xattn_in['Wk'], 'L1_xattn_bk': _L1_xattn_in['bk'], 'L1_xattn_Wv': _L1_xattn_in['Wv'], 'L1_xattn_bv': _L1_xattn_in['bv'], 'L1_ffn_Wc': _L1_ffn_in['Wc'], 'L1_ffn_temperature': _L1_ffn_in['temperature'], 'L1_ffn_genes': _L1_ffn_in['genes'], 'L1_ffn_Wd': _L1_ffn_in['Wd'], 'L1_ffn_Wu': _L1_ffn_in['Wu'], 'L1_ffn_norm_w': _L1_ffn_in['norm_w'], 'L1_ffn_scale': _L1_ffn_in['scale']}

def reference(x, ctx_2048, mask_Bx1x2048_fk1, L0_xattn_ssm_kernel, L0_xattn_D, L0_ffn_gate_w, L0_ffn_gate_b, L0_ffn_val_w, L0_ffn_val_b, L0_ffn_out_w, L0_ffn_out_b, L1_xattn_Wq, L1_xattn_bq, L1_xattn_Wk, L1_xattn_bk, L1_xattn_Wv, L1_xattn_bv, L1_ffn_Wc, L1_ffn_temperature, L1_ffn_genes, L1_ffn_Wd, L1_ffn_Wu, L1_ffn_norm_w, L1_ffn_scale):
    import jax
    import jax.numpy as jnp

    def _L0_xattn_ref(k, v, q, ssm_kernel, D, head_dim):
        import jax, jax.numpy as jnp
        import numpy as np
        B, HD, L = k.shape
        H = HD // head_dim
        fft_size = 2 * L
        k_ = k.reshape(B, H, head_dim, L)
        v_ = v.reshape(B, H, head_dim, L)
        q_ = q.reshape(B, H, head_dim, L)
        kv = jnp.einsum('bhil,bhjl->bijhl', k_, v_)
        kv_f = jnp.fft.rfft(kv, n=fft_size)
        kernel_f = jnp.fft.rfft(ssm_kernel, n=fft_size)
        y = jnp.fft.irfft(kv_f * kernel_f, n=fft_size)[..., :L]
        out = y + kv * D[None, None, None, :, None]
        out = jnp.einsum('bijhl,bhil->bjhl', out, q_)
        out = jnp.transpose(out, (0, 2, 1, 3)).reshape(B, H * head_dim, L)
        return out.astype(k.dtype)

    def _L0_ffn_ref(x, gate_w, gate_b, val_w, val_b, out_w, out_b):
        import jax, jax.numpy as jnp
        import numpy as np
        D_MODEL = 256
        HIDDEN = 4 * D_MODEL
        B, S = (2, 512)

        def bit_linear(x, w, b):
            gamma_x = jnp.clip(jnp.max(jnp.abs(x), axis=-1, keepdims=True), 1e-05, None)
            scale_x = 127.0 / gamma_x
            x_dq = jnp.clip(jnp.round(x * scale_x), -128.0, 127.0) / scale_x
            x_ste = x + jax.lax.stop_gradient(x_dq - x)
            gamma_w = jnp.clip(jnp.mean(jnp.abs(w)), 1e-05, None)
            w_dq = jnp.clip(jnp.round(w / gamma_w), -1.0, 1.0) * gamma_w
            w_ste = w + jax.lax.stop_gradient(w_dq - w)
            return jnp.einsum('bsd,hd->bsh', x_ste, w_ste) + b
        gate = jax.nn.silu(bit_linear(x, gate_w, gate_b))
        val = bit_linear(x, val_w, val_b)
        return bit_linear(gate * val, out_w, out_b)

    def _L1_xattn_ref(target, source, target_mask, source_mask, Wq, bq, Wk, bk, Wv, bv):
        import math
        import jax, jax.numpy as jnp
        import numpy as np
        SIZE = 128
        HEADS = 16
        HEAD_DIM = SIZE // HEADS
        B, T, S = (2, 256, 256)
        NEG = 1000000.0
        b, _, t = target.shape
        s = source.shape[-1]
        q = jnp.einsum('oc,bct->bot', Wq, target) + bq[None, :, None]
        k = jnp.einsum('oc,bcs->bos', Wk, source) + bk[None, :, None]
        v = jnp.einsum('oc,bcs->bos', Wv, source) + bv[None, :, None]
        q = q.reshape(b, HEADS, HEAD_DIM, t)
        k = k.reshape(b, HEADS, HEAD_DIM, s)
        v = v.reshape(b, HEADS, HEAD_DIM, s)
        dot = jnp.einsum('bhdt,bhds->bhts', q, k) / math.sqrt(HEAD_DIM)
        mask = target_mask[:, :, :, None] * source_mask[:, :, None, :]
        dot = mask * dot - (1.0 - mask) * NEG
        amap = jax.nn.softmax(dot, axis=-1) * mask
        out = jnp.einsum('bhts,bhds->bhdt', amap, v)
        return out.reshape(b, HEADS * HEAD_DIM, t)

    def _L1_ffn_ref(x, Wc, temperature, genes, Wd, Wu, norm_w, scale):
        import jax, jax.numpy as jnp
        import numpy as np
        N_ACTIVE = 32
        eps = jnp.finfo(x.dtype).eps
        xn = x * jax.lax.rsqrt(jnp.mean(x * x, axis=-1, keepdims=True) + eps) * norm_w
        logits = jnp.einsum('btd,gd->btg', xn, Wc) / jnp.clip(temperature, 0.1)
        top_vals, top_idx = jax.lax.top_k(logits, N_ACTIVE)
        expr_w = jax.nn.softmax(top_vals, axis=-1)
        expressed = jnp.einsum('btk,btkc->btc', expr_w, genes[top_idx])
        down = jnp.tanh(jnp.einsum('btc,dc->btd', expressed, Wd))
        up = jnp.einsum('btc,dc->btd', expressed, Wu)
        return down * xn * up * scale
    x = x + _L0_xattn_ref(ctx_2048, ctx_2048, _layernorm(x, axis=-1), L0_xattn_ssm_kernel, L0_xattn_D, 8)
    x = x + _L0_ffn_ref(_layernorm(x, axis=-1), L0_ffn_gate_w, L0_ffn_gate_b, L0_ffn_val_w, L0_ffn_val_b, L0_ffn_out_w, L0_ffn_out_b)
    x = x + _L1_xattn_ref(_layernorm(x, axis=-1), ctx_2048, mask_Bx1x2048_fk1, mask_Bx1x2048_fk1, L1_xattn_Wq, L1_xattn_bq, L1_xattn_Wk, L1_xattn_bk, L1_xattn_Wv, L1_xattn_bv)
    x = x + _L1_ffn_ref(_layernorm(x, axis=-1), L1_ffn_Wc, L1_ffn_temperature, L1_ffn_genes, L1_ffn_Wd, L1_ffn_Wu, L1_ffn_norm_w, L1_ffn_scale)
    return x

_drawn_inputs = setup_inputs


def setup_inputs(seed=0):
    import zlib

    import numpy as np

    out = dict(_drawn_inputs(seed))
    spreads = {'L0_ffn_gate_b': (0.0, 0.8),
     'L0_ffn_val_b': (0.0, 0.8),
     'L0_ffn_out_b': (0.0, 2.0),
     'L1_ffn_norm_w': (1.0, 0.6)}
    factors = {'L0_ffn_gate_w': 8.0,
     'L0_ffn_val_w': 8.0,
     'L0_ffn_out_w': 8.0,
     'L1_xattn_Wq': 6.039,
     'L1_xattn_bq': 30.182,
     'L1_xattn_Wk': 6.712,
     'L1_xattn_bk': 200.0,
     'L1_xattn_Wv': 6.589,
     'L1_xattn_bv': 197.338,
     'L1_ffn_Wc': 64.0,
     'L1_ffn_genes': 64.0,
     'L1_ffn_Wd': 64.0,
     'L1_ffn_Wu': 64.0}
    for name, (base, spread) in spreads.items():
        noise = np.random.default_rng([zlib.crc32(name.encode()), seed]).standard_normal(out[name].shape)
        drawn = base * np.exp(spread * noise) if base else spread * noise
        out[name] = jnp.asarray(drawn.astype(out[name].dtype))
    for name, factor in factors.items():
        out[name] = (out[name] * factor).astype(out[name].dtype)
    return out
```

```python
from contextlib import ExitStack

import concourse.bass as bass
from concourse import mybir

F32 = mybir.dt.float32
BF16 = mybir.dt.bfloat16
U32 = mybir.dt.uint32
ALU = mybir.AluOpType
ACT = mybir.ActivationFunctionType
AX = mybir.AxisListType

P = 128
MAGIC = 12582912.0
LN_EPS = 1e-5
RMS_EPS = 1.1920928955078125e-07
NEG = 1000000.0
GONE = -3.0e38
TOPK = 32


def split3(eng, whole, rest, parts):
    eng.tensor_copy(parts[0], whole)
    eng.drain()
    eng.tensor_tensor(rest, whole, parts[0], ALU.subtract)
    eng.drain()
    eng.tensor_copy(parts[1], rest)
    eng.drain()
    eng.tensor_tensor(parts[2], rest, parts[1], ALU.subtract)


def build(nc, a, out):
    B, C, L = a["x"].shape
    H, HD = a["ssm"].shape[0], C // a["ssm"].shape[0]
    HID = a["gate_w"].shape[0]
    G, GD = a["genes"].shape
    KL, KH, KG = L // P, HID // P, G // P
    QK_SCALE = 1.0 / float(HD) ** 0.5
    TERM_Q, TERM_K = (0, 0, 0, 1, 1, 2), (0, 1, 2, 0, 1, 0)
    NT = len(TERM_Q)
    ROWS, GRP = 2 * HD * NT, H // 2
    ROW_MASK, ROW_MAX = ROWS, ROWS + NT
    K_MAX, K_ALL = ROWS + NT, ROWS + NT + 6
    assert C == P and L == 2 * P and HD == 8 and K_ALL <= P

    scr_toep = nc.dram_tensor("scr_toep", [H, P + L], F32, kind="Internal").ap()
    scr_toeps = nc.dram_tensor("scr_toeps", [H, P, L], F32, kind="Internal").ap()
    scr_q = nc.dram_tensor("scr_q", [2, ROWS, GRP, L], BF16, kind="Internal").ap()
    scr_k = nc.dram_tensor("scr_k", [2, ROWS, GRP, L], BF16, kind="Internal").ap()
    scr_mask = nc.dram_tensor("scr_mask", [B, 2, NT, L], BF16, kind="Internal").ap()
    scr_o = nc.dram_tensor("scr_o", [2, H, HD + 1, L], F32, kind="Internal").ap()

    with ExitStack() as ctx:
        def sb(name, shape, dt=F32):
            return ctx.enter_context(nc.sbuf_tensor(name, shape, dt))

        def sem(name):
            return ctx.enter_context(nc.semaphore(name))

        banks = [ctx.enter_context(nc.psum_tensor(f"bank{i}", [P, 512], F32)) for i in range(8)]

        ident = sb("ident", [P, P])
        ident16 = sb("ident16", [P, P], BF16)
        half_neg = sb("half_neg", [P, 16])
        wgvT = sb("wgvT", [P, KL, 2 * HID], BF16)
        woT = sb("woT", [P, KH, L], BF16)
        wqkvT = sb("wqkvT", [P, 3, P])
        wcT = sb("wcT", [P, KL, G])
        wduT = sb("wduT", [P, 2 * L])
        genes = sb("genes", [P, KG, P])
        b6 = sb("b6", [P, 2 * HID], BF16)
        gammas = sb("gammas", [P, 3])
        inv_gammas = sb("inv_gammas", [P, 3])
        out_b = sb("out_b", [P, L])
        norm_w = sb("norm_w", [P, L])
        bv = sb("bv", [P, C])
        bqk = sb("bqk", [P, 2])
        temp_scale = sb("temp_scale", [P, 2])
        mask_cols = sb("mask_cols", [P, B, KL])
        yT = sb("yT", [P, KL, B, C])

        w_raw = sb("w_raw", [P, 3, KH * L])
        w_int = sb("w_int", [P, KH * L], BF16)
        small_raw = sb("small_raw", [P, 3, P])
        wc_raw = sb("wc_raw", [P, KG, L])
        wdu_raw = sb("wdu_raw", [P, 2, 2, GD])
        bias_row = sb("bias_row", [1, 2, HID])
        bias_parts = w_raw[0:1].rearrange("p a n -> p (a n)")[:, KH * L:KH * L + 3 * HID].bitcast(BF16).rearrange(
            "p (n h) -> p n h", n=3)
        toep_row = sb("toep_row", [H, P + L])
        d_col = sb("d_col", [H, 1])
        mask_nat = sb("mask_nat", [2 * B, P])
        mask_rows = sb("mask_rows", [B, L])
        aug = sb("aug", [B, 2, L])
        aug_rest = sb("aug_rest", [B, 2, L])
        aug_parts = sb("aug_parts", [B, 2, 3, L], BF16)
        aug_terms = sb("aug_terms", [B, 2, NT, L], BF16)
        abs_sum = sb("abs_sum", [P, 3])
        one_rows = sb("one_rows", [6, H, L], BF16)
        ctx_in = [sb(f"ctx_in{k}", [P, L]) for k in range(2)]
        x_in = [sb(f"x_in{k}", [P, L]) for k in range(2)]
        xn_in = [sb(f"xn_in{k}", [P, L]) for k in range(2)]
        stat6 = sb("stat6", [P, 6])
        stat2 = sb("stat2", [P, 2])
        mv_all = sb("mv_all", [P, B, 2])
        rstd_all = sb("rstd_all", [P, B])
        cT = sb("cT", [P, KL, B, C])
        qT = sb("qT", [P, KL, B, C])
        toep = [sb(f"toep{k}", [P, L]) for k in range(2)]
        kv = [sb(f"kv{k}", [P, KL * B, HD, HD]) for k in range(2)]
        prod = w_raw[:].rearrange("p a n -> p (a n)")[:, 0:KL * B * HD * HD].rearrange(
            "p (s j i) -> p s j i", j=HD, i=HD)

        spare = {"cT": cT[:].rearrange("p s b c -> p (s b c)"), "qT": qT[:].rearrange("p s b c -> p (s b c)"),
                 "kv0": kv[0][:].rearrange("p s j i -> p (s j i)"), "kv1": kv[1][:].rearrange("p s j i -> p (s j i)")}
        used = dict.fromkeys(spare, 0)

        def inside(tile, shape, dt=F32):
            n = 1
            for m in shape[1:]:
                n *= m
            words = n if dt == F32 else n // 2
            view = spare[tile][:, used[tile]:used[tile] + words]
            used[tile] += words
            assert used[tile] <= spare[tile].shape[1]
            view = view if dt == F32 else view.bitcast(dt)
            names = "abc"[:len(shape) - 1]
            if len(names) == 1:
                return view
            return view.rearrange(f"p ({' '.join(names)}) -> p {' '.join(names)}", **dict(zip(names, shape[1:])))

        x1 = sb("x1", [P, L])
        x1b = sb("x1b", [P, L])
        x2 = sb("x2", [P, L])
        x3 = sb("x3", [P, L])
        xn = sb("xn", [P, L])
        xr = sb("xr", [P, L])
        st6 = sb("st6", [P, 6])
        st = sb("st", [P, 24])
        xqT = sb("xqT", [P, KL, P], BF16)
        s6 = sb("s6", [P, P], BF16)
        s6T = sb("s6T", [P, P], BF16)
        tanh_g = sb("tanh_g", [P, 512])
        u_g = sb("u_g", [P, 512])
        hid = inside("qT", [P, HID])
        hqT = sb("hqT", [P, KH, P], BF16)
        x_b = sb("x_b", [P, L])
        ctx_b = sb("ctx_b", [P, L])
        y_in = sb("y_in", [P, KL, P])
        mask_b = sb("mask_b", [P, L])
        mask_q = sb("mask_q", [P, L])
        ctx_m = sb("ctx_m", [P, L])
        qk = inside("kv1", [P, 2, L])
        qk_rest = inside("kv1", [P, 2, L])
        qk_parts = inside("kv1", [P, 3, 2, L], BF16)
        v_aug = sb("v_aug", [P, KL, H, 32])
        QS = inside("kv0", [P, GRP, L], BF16)
        KS = sb("KS", [P, H, L], BF16)
        neg_max = sb("neg_max", [P, KL, H])
        nm_rest = sb("nm_rest", [P, KL, H])
        nm_parts = sb("nm_parts", [P, KL, 2, 3, GRP], BF16)
        nm_rows = sb("nm_rows", [6 * GRP, L], BF16)
        probs = [inside("cT", [P, L * KL]) for k in range(8)]
        o_quad = inside("kv0", [P, 4, L])
        o_nat = sb("o_nat", [P, L])
        o_den = sb("o_den", [P, L])
        xrT = inside("kv1", [P, KL, P])
        logits = inside("qT", [P, G])
        left = inside("qT", [P, G])
        best = sb("best", [P, 8])
        top1 = sb("top1", [P, 2])
        e_all = inside("qT", [P, G])
        w_top = inside("qT", [P, G])
        w_sum = sb("w_sum", [P, 2])
        wT = inside("qT", [P, KG, P])
        exprT = sb("exprT", [P, P])
        down = sb("down", [P, L])
        dx = sb("dx", [P, L])
        res = sb("res", [P, L])


        made = {}

        def s(name):
            if name not in made:
                made[name] = ctx.enter_context(nc.semaphore(name))
            return made[name]

        MEAN, VAR, RSTD, QX, SX, SG, KAPPA, QH, SH, SO, SQ, RR, NB, WS, RS, RSS, R0 = range(17)

        def col(n, m=1):
            return st[:, n:n + m]

        bank16 = [b[:].bitcast(BF16) for b in banks]
        M, SC, O, X = banks[0:2], banks[2:4], banks[4], banks[5:8]
        heads = [4 * jj + q for q in range(4) for jj in range(4)]

        def collect_o(act, q):
            act.wait_ge(s("o_bank_ready"), 1)
            act.sem_inc(s("o_bank_ready"), -1)
            act.wait_ge(s("o_quad_free"), 1)
            act.sem_inc(s("o_quad_free"), -1)
            act.activation(o_quad[:, q, :], O[:, 0:L], ACT.Copy)
            act.drain().then_inc(s("o_bank_free"), 1)
            act.sem_inc(s("o_quad_ready"), 1)

        block = ctx.enter_context(nc.Block())

        @block.sync
        def _(sp):
            for name in ("qk_parts_free", "res_free"):
                sp.sem_inc(s(name), 1)
            sp.sem_inc(s("o_quad_free"), 4)
            for n, w in enumerate((a["gate_w"], a["val_w"])):
                sp.dma_start(w_raw[:, n, :].rearrange("p (k d) -> p k d", d=L),
                             w.rearrange("(k p) d -> p k d", p=P)).then_inc(s("weights_in"), 16)
            sp.dma_start(w_raw[:, 2, :].rearrange("p (k d) -> p k d", d=HID),
                         a["out_w"].rearrange("(k p) d -> p k d", p=P)).then_inc(s("weights_in"), 16)
            for n, w in enumerate((a["wq"], a["wk"], a["wv"])):
                sp.dma_start(small_raw[:, n, :], w).then_inc(s("small_in"), 16)
            sp.dma_start(wc_raw[:], a["wc"].rearrange("(k p) d -> p k d", p=P)).then_inc(s("small_in"), 16)
            for n, w in enumerate((a["wd"], a["wu"])):
                sp.dma_start(wdu_raw[:, n, :, :], w.rearrange("(k p) g -> p k g", p=P)).then_inc(s("small_in"), 16)
            sp.dma_start(bias_row[:, 0, :], a["gate_b"].rearrange("(o n) -> o n", o=1)).then_inc(s("bias_in"), 16)
            sp.dma_start(bias_row[:, 1, :], a["val_b"].rearrange("(o n) -> o n", o=1)).then_inc(s("bias_in"), 16)
            sp.dma_start(mask_nat[:], a["mask"].rearrange("b o (k l) -> (b o k) l", l=P)).then_inc(s("mask_nat_in"), 16)
            sp.dma_start(mask_rows[:], a["mask"].rearrange("b o l -> (b o) l")).then_inc(s("mask_rows_in"), 16)
            sp.dma_start(toep_row[:], a["ssm"]).then_inc(s("toep_row_in"), 16)
            sp.dma_start(d_col[:], a["d"].rearrange("(h o) -> h o", o=1)).then_inc(s("toep_row_in"), 16)
            for tile, src in ((out_b, a["out_b"]), (norm_w, a["norm_w"]), (bv, a["bv"])):
                n = src.shape[0]
                sp.dma_start(tile[:], bass.AP(src.tensor, 0, [[0, P], [1, n]])).then_inc(s("vectors_in"), 16)
            for n, src in enumerate((a["bq"], a["bk"])):
                sp.dma_start(bqk[:, n:n + 1], src.rearrange("(p o) -> p o", o=1)).then_inc(s("vectors_in"), 16)
            for n, src in enumerate((a["temperature"], a["scale"])):
                sp.dma_start(temp_scale[:, n:n + 1], bass.AP(src.tensor, 0, [[0, P], [1, 1]])).then_inc(s("vectors_in"), 16)
            sp.wait_ge(s("genes_clear"), 1)
            sp.sem_inc(s("genes_clear"), -1)
            sp.dma_start(genes[:, :, 0:GD], a["genes"].rearrange("(k p) c -> p k c", p=P)).then_inc(s("genes_in"), 16)
            sp.wait_ge(s("toep_row_ready"), 1)
            sp.sem_inc(s("toep_row_ready"), -1)
            sp.dma_start(scr_toep, toep_row[:]).then_inc(s("toep_written"), 16)
            sp.wait_ge(s("toep_written"), 16)
            sp.sem_inc(s("toep_written"), -16)
            sp.dma_start(scr_toeps, bass.AP(scr_toep.tensor, P, [[P + L, H], [-1, P], [1, L]])).then_inc(
                s("toeps_written"), 16)

            with sp.Fori(0, B // 2) as i:
                for k in range(2):
                    sp.wait_ge(s(f"x_in{k}_free"), 1)
                    sp.sem_inc(s(f"x_in{k}_free"), -1)
                    sp.dma_start(x_in[k][:], a["x"][2 * i + k]).then_inc(s(f"x_in{k}_loaded"), 16)
            with sp.Fori(0, B // 2) as i:
                for k in range(2):
                    sp.wait_ge(s(f"x_in{k}_free"), 1)
                    sp.sem_inc(s(f"x_in{k}_free"), -1)
                    sp.dma_start(x_in[k][:], a["x"][2 * i + k]).then_inc(s(f"x_in{k}_loaded"), 16)
                    sp.wait_ge(s(f"ctx_in{k}_free"), 1)
                    sp.sem_inc(s(f"ctx_in{k}_free"), -1)
                    sp.dma_start(ctx_in[k][:], a["ctx"][2 * i + k]).then_inc(s(f"ctx_in{k}_loaded"), 16)
            sp.wait_ge(s("toeps_written"), 16)
            sp.sem_inc(s("toeps_written"), -16)
            with sp.Fori(0, H // 2) as i:
                for k in range(2):
                    sp.wait_ge(s(f"toep{k}_free"), 1)
                    sp.sem_inc(s(f"toep{k}_free"), -1)
                    sp.dma_start(toep[k][:], scr_toeps[2 * i + k]).then_inc(s(f"toep{k}_loaded"), 16)
            sp.wait_ge(s("clear_sp"), 1)
            sp.sem_inc(s("clear_sp"), -1)
            sp.wait_ge(s("bias_parts_ready"), 1)
            sp.sem_inc(s("bias_parts_ready"), -1)
            for r in range(NT):
                sp.dma_start(b6[r:r + 1, :], bias_parts[0:1, TERM_K[r], :]).then_inc(s("b6_ready"), 16)
            sp.wait_ge(s("mask_terms_ready"), 1)
            sp.sem_inc(s("mask_terms_ready"), -1)
            sp.dma_start(scr_mask.rearrange("b w t l -> b (w t l)"), aug_terms[:].rearrange("b w t l -> b (w t l)")
                         ).then_inc(s("mask_terms_written"), 16)
            sp.dma_start(KS[ROW_MAX:ROW_MAX + 6, :, :], one_rows[:]).then_inc(s("ks_ones_in"), 16)
            sp.wait_ge(s("mask_terms_written"), 16)
            sp.sem_inc(s("mask_terms_written"), -16)
            sp.wait_ge(s("ks_ones_in"), 16)
            sp.sem_inc(s("ks_ones_in"), -16)
            sp.wait_ge(s("y_all_ready"), 1)
            sp.sem_inc(s("y_all_ready"), -1)

            with sp.Fori(0, B) as b:
                sp.wait_ge(s("y_in_free"), 1)
                sp.sem_inc(s("y_in_free"), -1)
                sp.dma_start(y_in[:], yT[:, :, b, :]).then_inc(s("y_in_loaded"), 16)
                sp.wait_ge(s("x_b_free"), 1)
                sp.sem_inc(s("x_b_free"), -1)
                sp.dma_start(x_b[:], a["x"][b]).then_inc(s("x_b_loaded"), 16)
                sp.wait_ge(s("ctx_b_free"), 1)
                sp.sem_inc(s("ctx_b_free"), -1)
                sp.dma_start(ctx_b[:], a["ctx"][b]).then_inc(s("ctx_b_loaded"), 16)
                sp.wait_ge(s("mask_b_free"), 1)
                sp.sem_inc(s("mask_b_free"), -1)
                sp.dma_start(mask_b[:], bass.AP(a["mask"].tensor, b * L, [[0, P], [1, L]])).then_inc(s("mask_b_loaded"), 16)
                sp.wait_ge(s("qs_free"), 1)
                sp.sem_inc(s("qs_free"), -1)
                sp.dma_start(QS[ROW_MASK:ROW_MASK + NT, :, :],
                             bass.AP(scr_mask.tensor, b * (2 * NT * L), [[L, NT], [0, GRP], [1, L]])).then_inc(s("qs_loaded"), 16)
                sp.dma_start(KS[ROW_MASK:ROW_MASK + NT, :, :],
                             bass.AP(scr_mask.tensor, b * (2 * NT * L) + NT * L, [[L, NT], [0, H], [1, L]])
                             ).then_inc(s("qs_loaded"), 16)
                sp.wait_ge(s("qk_parts_ready"), 1)
                sp.sem_inc(s("qk_parts_ready"), -1)
                for t in range(NT):
                    for w, (scr, part) in enumerate(((scr_q, TERM_Q[t]), (scr_k, TERM_K[t]))):
                        dst = bass.AP(scr.tensor, t * GRP * L, [[L, GRP], [NT * GRP * L, 2 * HD], [1, L]])
                        sp.dma_start(dst, qk_parts[:, part, w, :]).then_inc(s("parts_written"), 16)
                sp.wait_ge(s("parts_written"), 16 * 2 * NT)
                sp.sem_inc(s("parts_written"), -(16 * 2 * NT))
                sp.sem_inc(s("qk_parts_free"), 1)
                sp.dma_start(QS[0:ROWS, :, :], scr_q[0]).then_inc(s("qs_loaded"), 16)
                for j in range(2):
                    half = ROWS // 2
                    sp.dma_start(KS[half * j:half * (j + 1), :, :].rearrange("r (g j) l -> r g j l", j=2)[:, :, j, :],
                                 scr_k[0, half * j:half * (j + 1)]).then_inc(s("qs_loaded"), 16)
                sp.wait_ge(s("max_rows_ready"), 1)
                sp.sem_inc(s("max_rows_ready"), -1)
                sp.dma_start(QS[ROW_MAX:ROW_MAX + 6, :, :], nm_rows[:]).then_inc(s("max_rows_loaded"), 16)
                sp.wait_ge(s("o_quad_ready"), 4)
                sp.sem_inc(s("o_quad_ready"), -4)
                for jj in range(4):
                    sp.dma_start(scr_o[0, 4 * jj:4 * jj + 4].rearrange("q d l -> d q l"),
                                 o_quad[32 * jj:32 * jj + HD + 1, :, :]).then_inc(s("o_written"), 16)
                sp.wait_ge(s("o_written"), 64)
                sp.sem_inc(s("o_written"), -64)
                sp.sem_inc(s("o_quad_free"), 4)
                sp.wait_ge(s("o_nat_free"), 1)
                sp.sem_inc(s("o_nat_free"), -1)
                sp.dma_start(o_nat[:], scr_o[0, :, 0:HD, :]).then_inc(s("o_nat_loaded"), 16)
                sp.dma_start(o_den[:], bass.AP(scr_o.tensor, HD * L, [[(HD + 1) * L, H], [0, HD], [1, L]])
                             ).then_inc(s("o_nat_loaded"), 16)
                sp.wait_ge(s("res_ready"), 1)
                sp.sem_inc(s("res_ready"), -1)
                sp.dma_start(out[b], res[:]).then_inc(s("res_out"), 16)
                sp.wait_ge(s("res_out"), 16)
                sp.sem_inc(s("res_out"), -16)
                sp.sem_inc(s("res_free"), 1)

        @block.gpsimd
        def _(pool):
            pool.memset(ident[:], 0.0)
            pool.memset(ident16[:], 0.0)
            pool.memset(genes[:], 0.0)
            pool.memset(half_neg[:], -0.5)
            pool.memset(one_rows[:], 1.0)
            pool.drain().then_inc(s("genes_clear"), 1)
            for m in (ident, ident16):
                pool.affine_select(out=m[:], in_=m[:], compare_op=ALU.not_equal, fill=1.0, base=0,
                                   pattern=[[-1, P]], channel_multiplier=1)
            rows = one_rows[:].rearrange("r (g j) l -> r g j l", j=2)
            pool.affine_select(out=rows[:, :, 0, :], in_=rows[:, :, 0, :], compare_op=ALU.is_ge, fill=0.0, base=2,
                               pattern=[[0, GRP], [0, L]], channel_multiplier=-1)
            pool.affine_select(out=rows[:, :, 1, :], in_=rows[:, :, 1, :], compare_op=ALU.is_ge, fill=0.0, base=-3,
                               pattern=[[0, GRP], [0, L]], channel_multiplier=1)
            pool.drain().then_inc(s("ident_ready"), 1)
            pool.memset(KS[:].bitcast(U32), 0)
            pool.memset(v_aug[:], 0.0)
            pool.memset(s6[:], 0.0)
            pool.memset(b6[:], 0.0)
            pool.memset(wduT[:], 0.0)
            pool.drain()
            pool.memset(v_aug[:, :, :, HD:HD + 1], 1.0)
            pool.drain().then_inc(s("clear_act"), 1)
            pool.sem_inc(s("clear_dve"), 1)
            pool.sem_inc(s("clear_sp"), 1)
            pool.sem_inc(s("ctx_b_free"), 1)
            pool.wait_ge(s("toep_row_in"), 32)
            pool.sem_inc(s("toep_row_in"), -32)
            pool.tensor_tensor(toep_row[:, P:P + 1], toep_row[:, P:P + 1], d_col[:], ALU.add).then_inc(
                s("toep_row_ready"), 1)
            pool.wait_ge(s("abs_sum_ready"), 1)
            pool.sem_inc(s("abs_sum_ready"), -1)
            pool.partition_all_reduce(gammas[:], abs_sum[:], P, bass.bass_isa.ReduceOp.add).then_inc(
                s("gamma_sum_ready"), 1)

            pool.wait_ge(s("var_all_ready"), 1)
            pool.sem_inc(s("var_all_ready"), -1)
            pool.tensor_scalar(rstd_all[:], mv_all[:, :, 1], LN_EPS, 1.0, ALU.add, ALU.mult)
            pool.drain()
            pool.tensor_tensor(rstd_all[:], rstd_all[:], half_neg[:], ALU.pow).then_inc(s("rstd_all_ready"), 1)
            pool.wait_ge(s("seq_all_ready"), 1)
            pool.sem_inc(s("seq_all_ready"), -1)
            with pool.Fori(0, H // 2) as i:
                for k in range(2):
                    pool.wait_ge(s(f"kv{k}_free"), 1)
                    pool.sem_inc(s(f"kv{k}_free"), -1)
                    kh = cT[:].rearrange("p s b c -> p (s b) c")[:, :, bass.ds((2 * i + k) * HD, HD)]
                    shape = [P, KL * B, HD, HD]
                    pool.tensor_tensor(kv[k][:], kh.unsqueeze(3).broadcast_to(shape),
                                       kh.unsqueeze(2).broadcast_to(shape), ALU.mult).then_inc(s(f"kv{k}_ready"), 1)

            pool.wait_ge(s("mask_rows_in"), 16)
            pool.sem_inc(s("mask_rows_in"), -16)
            pool.tensor_scalar(aug[:, 0, :], mask_rows[:], -NEG, 0.0, ALU.mult, ALU.add)
            pool.tensor_scalar(aug[:, 1, :], mask_rows[:], -1.0, 1.0, ALU.mult, ALU.add)
            pool.drain()
            split3(pool, aug[:], aug_rest[:], [aug_parts[:, :, n, :] for n in range(3)])
            pool.drain()
            for t in range(NT):
                pool.tensor_copy(aug_terms[:, 0, t, :], aug_parts[:, 0, TERM_Q[t], :])
                pool.tensor_copy(aug_terms[:, 1, t, :], aug_parts[:, 1, TERM_K[t], :])
            pool.drain().then_inc(s("mask_terms_ready"), 1)
            pool.wait_ge(s("bias_in"), 32)
            pool.sem_inc(s("bias_in"), -32)
            pool.wait_ge(s("gammas_ready"), 1)
            pool.sem_inc(s("gammas_ready"), -1)
            for n in range(2):
                pool.tensor_scalar(bias_row[:, n, :], bias_row[:, n, :], inv_gammas[0:1, n:n + 1], 1.0, ALU.mult, ALU.mult)
            pool.drain()
            flat = bias_row[:].rearrange("p n h -> p (n h)")
            pool.wait_ge(s("weights_done"), 1)
            pool.sem_inc(s("weights_done"), -1)
            split3(pool, flat, flat, [bias_parts[:, n, :] for n in range(3)])
            pool.drain().then_inc(s("bias_parts_ready"), 1)

            def rstd_of(eps=LN_EPS):
                pool.wait_ge(s("var_ready"), 1)
                pool.sem_inc(s("var_ready"), -1)
                pool.tensor_scalar(col(RSTD), col(VAR), eps, 1.0, ALU.add, ALU.mult)
                pool.drain()
                pool.tensor_tensor(col(RSTD), col(RSTD), half_neg[:, 0:1], ALU.pow).then_inc(s("rstd_ready"), 1)

            with pool.Fori(0, B) as b:
                pool.wait_ge(s("x1_ready"), 1)
                pool.sem_inc(s("x1_ready"), -1)
                pool.tensor_tensor(x1b[:], x1[:], out_b[:], ALU.add).then_inc(s("x1b_ready"), 1)
                rstd_of()
                pool.wait_ge(s("sx_ready"), 1)
                pool.sem_inc(s("sx_ready"), -1)
                pool.tensor_copy(s6[:, 0:3], col(SX).broadcast_to([P, 3]))
                pool.drain()
                pool.tensor_tensor(col(R0), col(SX), s6[:, 0:1], ALU.subtract)
                pool.drain()
                pool.tensor_copy(s6[:, 3:5], col(R0).broadcast_to([P, 2]))
                pool.drain()
                pool.tensor_tensor(s6[:, 5:6], col(R0), s6[:, 3:4], ALU.subtract).then_inc(s("s6_ready"), 1)
                pool.wait_ge(s("ctx_b_loaded"), 16)
                pool.sem_inc(s("ctx_b_loaded"), -16)
                pool.wait_ge(s("mask_b_loaded"), 16)
                pool.sem_inc(s("mask_b_loaded"), -16)
                pool.wait_ge(s("ctx_m_free"), 1)
                pool.sem_inc(s("ctx_m_free"), -1)
                pool.tensor_tensor(ctx_m[:], ctx_b[:], mask_b[:], ALU.mult)
                pool.tensor_scalar(mask_q[:], mask_b[:], QK_SCALE, 1.0, ALU.mult, ALU.mult)
                pool.drain().then_inc(s("ctx_m_ready"), 1)
                pool.sem_inc(s("mask_q_ready"), 1)
                pool.sem_inc(s("ctx_b_free"), 1)
                rstd_of()
                pool.wait_ge(s("qk_ready"), 1)
                pool.sem_inc(s("qk_ready"), -1)
                pool.wait_ge(s("qk_parts_free"), 1)
                pool.sem_inc(s("qk_parts_free"), -1)
                split3(pool, qk[:], qk_rest[:], [qk_parts[:, n, :, :] for n in range(3)])
                pool.drain().then_inc(s("qk_parts_ready"), 1)
                pool.wait_ge(s("neg_max_ready"), 1)
                pool.sem_inc(s("neg_max_ready"), -1)
                nm = neg_max[:].rearrange("p t (g j) -> p t j g", j=2)
                nr = nm_rest[:].rearrange("p t (g j) -> p t j g", j=2)
                split3(pool, nm, nr, [nm_parts[:, :, :, n, :] for n in range(3)])
                pool.drain().then_inc(s("nm_parts_ready"), 1)
                rstd_of()
                pool.wait_ge(s("sq_ready"), 1)
                pool.sem_inc(s("sq_ready"), -1)
                pool.tensor_scalar(col(RR), col(SQ), 1.0 / L, RMS_EPS, ALU.mult, ALU.add)
                pool.drain()
                pool.tensor_tensor(col(RR), col(RR), half_neg[:, 0:1], ALU.pow).then_inc(s("rr_ready"), 1)

        @block.scalar
        def _(act):
            for name in ("seq_T0_taken", "seq_T1_taken", "scores0_free", "scores1_free", "o_bank_free", "bank_x0_free",
                         "bank_x1_free", "bank_x2_free"):
                act.sem_inc(s(name), 1)
            act.wait_ge(s("clear_act"), 1)
            act.sem_inc(s("clear_act"), -1)
            for n in range(3):
                for half in range(2):
                    act.wait_ge(s("w_T_ready"), 1)
                    act.sem_inc(s("w_T_ready"), -1)
                    src = bank16[half][:, :].rearrange("p (k c) -> p k c", c=P)
                    if n < 2:
                        for dk in range(KL):
                            dst = wgvT[:, dk, HID * n + 512 * half:HID * n + 512 * (half + 1)]
                            act.activation(dst.rearrange("p (k c) -> p k c", c=P), src[:, 4 * dk:4 * dk + 4, :], ACT.Copy)
                    else:
                        dst = woT[:, 4 * half:4 * half + 4, :].rearrange("p k (o c) -> p (k o) c", c=P)
                        act.activation(dst, src, ACT.Copy)
                    act.drain().then_inc(s("w_T_taken"), 1)
            act.wait_ge(s("small_T_ready"), 1)
            act.sem_inc(s("small_T_ready"), -1)
            act.activation(wqkvT[:].rearrange("p n c -> p (n c)"), banks[2][:, 0:3 * P], ACT.Copy)
            for dk in range(KL):
                act.activation(wcT[:, dk, :], banks[3 + dk][:], ACT.Copy)
            act.activation(wduT[0:GD, :], banks[5][0:GD, :], ACT.Copy)
            act.drain().then_inc(s("small_T_taken"), 1)
            with act.Fori(0, B // 2) as i:
                for k in range(2):
                    act.wait_ge(s(f"seq_T{k}_ready"), 1)
                    act.sem_inc(s(f"seq_T{k}_ready"), -1)
                    src = banks[6 + k][:].rearrange("p (w s c) -> p w s c", w=2, c=C)
                    act.activation(cT[:, :, 2 * i + k, :], src[:, 0], ACT.Copy)
                    act.activation(qT[:, :, 2 * i + k, :], src[:, 1], ACT.Copy)
                    act.drain().then_inc(s(f"seq_T{k}_taken"), 1)
            act.sem_inc(s("seq_all_ready"), 1)
            act.sem_inc(s("seq_all_dve"), 1)

            with act.Fori(0, B) as b:
                act.wait_ge(s("xq_T_ready"), 1)
                act.sem_inc(s("xq_T_ready"), -1)
                act.activation(xqT[:].rearrange("p k t -> p (k t)"), X[1][:, 0:L], ACT.Copy, bias=-MAGIC).then_inc(
                    s("xqT_ready"), 1)
                act.wait_ge(s("s6_T_ready"), 1)
                act.sem_inc(s("s6_T_ready"), -1)
                act.activation(s6T[:], bank16[7][:, 0:P], ACT.Copy)
                act.drain().then_inc(s("s6T_ready"), 1)
                for half in range(2):
                    act.wait_ge(s("gates_ready"), 1)
                    act.sem_inc(s("gates_ready"), -1)
                    act.wait_ge(s("tanh_free"), 1)
                    act.sem_inc(s("tanh_free"), -1)
                    if half == 0:
                        act.wait_ge(s("sg_ready"), 1)
                        act.sem_inc(s("sg_ready"), -1)
                    act.activation(tanh_g[:], X[0][:], ACT.Tanh, scale=col(SG)).then_inc(s("tanh_ready"), 1)
                for half in range(2):
                    act.wait_ge(s("hid_T_ready"), 1)
                    act.sem_inc(s("hid_T_ready"), -1)
                    act.activation(hqT[:, 4 * half:4 * half + 4, :].rearrange("p k t -> p (k t)"), X[half][:], ACT.Copy,
                                   bias=-MAGIC).then_inc(s("hqT_ready"), 1)
                act.wait_ge(s("nm_T_ready"), 1)
                act.sem_inc(s("nm_T_ready"), -1)
                act.activation(nm_rows[:], bank16[7][0:6 * GRP, 0:L], ACT.Copy)
                act.drain().then_inc(s("max_rows_ready"), 1)
                act.sem_inc(s("bank_x2_free"), 1)
                for n in range(H):
                    act.wait_ge(s(f"scores{n % 2}_ready"), 1)
                    act.sem_inc(s(f"scores{n % 2}_ready"), -1)
                    act.wait_ge(s("probs_free"), 1)
                    act.sem_inc(s("probs_free"), -1)
                    act.activation(probs[n % 8][:], SC[n % 2][:], ACT.Exp)
                    act.drain().then_inc(s(f"scores{n % 2}_free"), 1)
                    act.sem_inc(s("probs_ready"), 1)
                    if n % 4 == 1 and n > 4:
                        collect_o(act, n // 4 - 1)
                collect_o(act, 3)
                act.wait_ge(s("xn3_ready"), 1)
                act.sem_inc(s("xn3_ready"), -1)
                act.activation(down[:], xn[:], ACT.Square, accum_out=col(SQ))
                act.drain().then_inc(s("sq_ready"), 1)
                act.wait_ge(s("xr_T_ready"), 1)
                act.sem_inc(s("xr_T_ready"), -1)
                act.activation(xrT[:].rearrange("p k t -> p (k t)"), X[0][:, 0:L], ACT.Copy)
                act.drain().then_inc(s("xrT_ready"), 1)
                act.sem_inc(s("bank_x0_free"), 1)
                act.wait_ge(s("logit_bank_ready"), 1)
                act.sem_inc(s("logit_bank_ready"), -1)
                act.activation(logits[:], X[1][:], ACT.Copy)
                act.drain().then_inc(s("logits_ready"), 1)
                act.sem_inc(s("bank_x1_free"), 1)
                act.wait_ge(s("nb_ready"), 1)
                act.sem_inc(s("nb_ready"), -1)
                act.activation(e_all[:], logits[:], ACT.Exp, bias=col(NB), scale=temp_scale[:, 0:1]).then_inc(
                    s("e_ready"), 1)
                act.wait_ge(s("w_T_bank_ready"), 1)
                act.sem_inc(s("w_T_bank_ready"), -1)
                act.activation(wT[:].rearrange("p k t -> p (k t)"), X[2][:], ACT.Copy)
                act.drain().then_inc(s("wT_ready"), 1)
                act.sem_inc(s("bank_x2_free"), 1)
                act.wait_ge(s("expr_ready"), 1)
                act.sem_inc(s("expr_ready"), -1)
                act.activation(exprT[:], X[0][:, 0:P], ACT.Copy)
                act.drain().then_inc(s("exprT_ready"), 1)
                act.sem_inc(s("bank_x0_free"), 1)
                act.wait_ge(s("du_ready"), 1)
                act.sem_inc(s("du_ready"), -1)
                act.wait_ge(s("rs_ready"), 1)
                act.sem_inc(s("rs_ready"), -1)
                act.activation(down[:], X[1][:, 0:L], ACT.Tanh, scale=col(RS)).then_inc(s("down_ready"), 1)

        @block.tensor
        def _(pe):
            for name in ("ctx_in0_free", "ctx_in1_free", "xn_in0_free", "xn_in1_free", "toep0_free", "toep1_free", "kv0_free",
                         "kv1_free", "y_in_free", "qs_free", "ctx_m_free", "v_aug_free"):
                pe.sem_inc(s(name), 1)
            pe.sem_inc(s("probs_free"), 8)
            pe.wait_ge(s("ident_ready"), 1)
            pe.sem_inc(s("ident_ready"), -1)
            for n in range(3):
                pe.wait_ge(s("w_int_ready"), 1)
                pe.sem_inc(s("w_int_ready"), -1)
                for half in range(2):
                    if n > 0:
                        pe.wait_ge(s("w_T_taken"), 1)
                        pe.sem_inc(s("w_T_taken"), -1)
                    for m in range(8):
                        if n < 2:
                            src = w_int[:, (4 * half + m % 4) * L + (m // 4) * P:(4 * half + m % 4) * L + (m // 4 + 1) * P]
                        else:
                            at = (m % 2) * HID + (4 * half + m // 2) * P
                            src = w_int[:, at:at + P]
                        mm = pe.transpose(bank16[half][:, m * P:(m + 1) * P], src, ident16[:])
                    mm.then_inc(s("w_T_ready"), 1)
                pe.drain().then_inc(s("w_int_free"), 1)
            pe.wait_ge(s("w_T_taken"), 2)
            pe.sem_inc(s("w_T_taken"), -2)
            pe.wait_ge(s("small_in"), 16 * 6)
            pe.sem_inc(s("small_in"), -(16 * 6))
            for n in range(3):
                pe.transpose(banks[2][:, n * P:(n + 1) * P], small_raw[:, n, :], ident[:])
            for dk in range(KL):
                for k in range(KG):
                    pe.transpose(banks[3 + dk][:, k * P:(k + 1) * P], wc_raw[:, k, dk * P:(dk + 1) * P], ident[:])
            for n in range(2):
                for k in range(2):
                    mm = pe.transpose(banks[5][0:GD, (2 * n + k) * P:(2 * n + k + 1) * P], wdu_raw[:, n, k, :], ident[:])
            mm.then_inc(s("small_T_ready"), 1)
            with pe.Fori(0, B // 2) as i:
                for k in range(2):
                    pe.wait_ge(s(f"seq_T{k}_taken"), 1)
                    pe.sem_inc(s(f"seq_T{k}_taken"), -1)
                    pe.wait_ge(s(f"ctx_in{k}_loaded"), 16)
                    pe.sem_inc(s(f"ctx_in{k}_loaded"), -16)
                    for sh in range(KL):
                        pe.transpose(banks[6 + k][:, sh * P:(sh + 1) * P], ctx_in[k][:, sh * P:(sh + 1) * P], ident[:])
                    pe.wait_ge(s(f"xn_in{k}_ready"), 1)
                    pe.sem_inc(s(f"xn_in{k}_ready"), -1)
                    for sh in range(KL):
                        mm = pe.transpose(banks[6 + k][:, (2 + sh) * P:(3 + sh) * P], xn_in[k][:, sh * P:(sh + 1) * P], ident[:])
                    mm.then_inc(s(f"seq_T{k}_ready"), 1)
                    pe.drain().then_inc(s(f"ctx_in{k}_free"), 1)
                    pe.sem_inc(s(f"xn_in{k}_free"), 1)
            for k in range(2):
                pe.wait_ge(s(f"seq_T{k}_taken"), 1)
                pe.sem_inc(s(f"seq_T{k}_taken"), -1)
            pe.wait_ge(s("small_T_taken"), 1)
            pe.sem_inc(s("small_T_taken"), -1)
            with pe.Fori(0, H // 2) as i:
                for k in range(2):
                    pe.wait_ge(s(f"toep{k}_loaded"), 16)
                    pe.sem_inc(s(f"toep{k}_loaded"), -16)
                    pe.wait_ge(s(f"kv{k}_ready"), 1)
                    pe.sem_inc(s(f"kv{k}_ready"), -1)
                    pe.wait_ge(s(f"conv{k}_free"), 1)
                    pe.sem_inc(s(f"conv{k}_free"), -1)
                    rhs = kv[k][:].rearrange("p (s b) j i -> p s (b j i)", b=B)
                    for lh in range(KL):
                        for bh in range(2):
                            cols = slice(512 * bh, 512 * (bh + 1))
                            for sh in range(lh + 1):
                                mm = pe.matmul(banks[4 * k + 2 * lh + bh][:], toep[k][:, (lh - sh) * P:(lh - sh + 1) * P],
                                               rhs[:, sh, cols], start=(sh == 0), stop=(sh == lh))
                    mm.then_inc(s(f"conv{k}_ready"), 1)
                    pe.drain().then_inc(s(f"toep{k}_free"), 1)
                    pe.sem_inc(s(f"kv{k}_free"), 1)
            for k in range(2):
                pe.wait_ge(s(f"conv{k}_free"), 1)
                pe.sem_inc(s(f"conv{k}_free"), -1)
            pe.wait_ge(s("mask_nat_in"), 16)
            pe.sem_inc(s("mask_nat_in"), -16)
            pe.transpose(banks[5][:, 0:KL * B], mask_nat[:], ident[0:KL * B, 0:KL * B]).then_inc(s("mask_T_ready"), 1)
            pe.wait_ge(s("mask_T_taken"), 1)
            pe.sem_inc(s("mask_T_taken"), -1)
            pe.wait_ge(s("b6_ready"), 16 * NT)
            pe.sem_inc(s("b6_ready"), -(16 * NT))
            pe.wait_ge(s("genes_in"), 16)
            pe.sem_inc(s("genes_in"), -16)

            with pe.Fori(0, B) as b:
                pe.wait_ge(s("y_in_loaded"), 16)
                pe.sem_inc(s("y_in_loaded"), -16)
                pe.wait_ge(s("bank_x0_free"), 1)
                pe.sem_inc(s("bank_x0_free"), -1)
                for sh in range(KL):
                    mm = pe.transpose(X[0][:, sh * P:(sh + 1) * P], y_in[:, sh, :], ident[:])
                mm.then_inc(s("y_T_ready"), 1)
                pe.drain().then_inc(s("y_in_free"), 1)
                pe.wait_ge(s("xq_ready"), 1)
                pe.sem_inc(s("xq_ready"), -1)
                pe.wait_ge(s("bank_x1_free"), 1)
                pe.sem_inc(s("bank_x1_free"), -1)
                for k in range(KL):
                    mm = pe.transpose(X[1][:, k * P:(k + 1) * P], xn[:, k * P:(k + 1) * P], ident[:])
                mm.then_inc(s("xq_T_ready"), 1)
                pe.wait_ge(s("s6_ready"), 1)
                pe.sem_inc(s("s6_ready"), -1)
                pe.wait_ge(s("bank_x2_free"), 1)
                pe.sem_inc(s("bank_x2_free"), -1)
                pe.transpose(bank16[7][:, 0:P], s6[:], ident16[:]).then_inc(s("s6_T_ready"), 1)
                pe.wait_ge(s("xqT_ready"), 1)
                pe.sem_inc(s("xqT_ready"), -1)
                pe.wait_ge(s("s6T_ready"), 1)
                pe.sem_inc(s("s6T_ready"), -1)
                pe.wait_ge(s("bank_x0_free"), 1)
                pe.sem_inc(s("bank_x0_free"), -1)
                for half in range(2):
                    if half == 1:
                        pe.wait_ge(s("gate_bank_free"), 1)
                        pe.sem_inc(s("gate_bank_free"), -1)
                        pe.wait_ge(s("val_bank_free"), 1)
                        pe.sem_inc(s("val_bank_free"), -1)
                    for n in range(2):
                        at = HID * n + 512 * half
                        for k in range(KL):
                            pe.matmul(X[n][:], xqT[:, k, :], wgvT[:, k, at:at + 512], start=(k == 0), stop=False)
                        mm = pe.matmul(X[n][:], s6T[:], b6[:, at:at + 512], start=False, stop=True)
                    mm.then_inc(s("gates_ready"), 1)
                pe.wait_ge(s("gate_bank_free"), 1)
                pe.sem_inc(s("gate_bank_free"), -1)
                pe.wait_ge(s("val_bank_free"), 1)
                pe.sem_inc(s("val_bank_free"), -1)
                pe.wait_ge(s("hq_ready"), 1)
                pe.sem_inc(s("hq_ready"), -1)
                for half in range(2):
                    for m in range(4):
                        n = 4 * half + m
                        mm = pe.transpose(X[half][:, m * P:(m + 1) * P], hid[:, n * P:(n + 1) * P], ident[:])
                    mm.then_inc(s("hid_T_ready"), 1)
                pe.wait_ge(s("hqT_ready"), 2)
                pe.sem_inc(s("hqT_ready"), -2)
                for k in range(KH):
                    mm = pe.matmul(X[2][:, 0:L], hqT[:, k, :], woT[:, k, :], start=(k == 0), stop=(k == KH - 1))
                mm.then_inc(s("ffn_ready"), 1)
                pe.wait_ge(s("ctx_m_ready"), 1)
                pe.sem_inc(s("ctx_m_ready"), -1)
                pe.matmul(X[1][:, 0:L], wqkvT[:, 1, :], ctx_m[:], start=True, stop=True)
                for sh in range(KL):
                    mm = pe.matmul(X[1][:, L + sh * P:L + (sh + 1) * P], ctx_m[:, sh * P:(sh + 1) * P], wqkvT[:, 2, :],
                                   start=True, stop=True)
                mm.then_inc(s("kv_bank_ready"), 1)
                pe.wait_ge(s("xn2_ready"), 1)
                pe.sem_inc(s("xn2_ready"), -1)
                pe.matmul(X[0][:, 0:L], wqkvT[:, 0, :], xn[:], start=True, stop=True).then_inc(s("q_bank_ready"), 1)
                pe.drain().then_inc(s("ctx_m_free"), 1)
                pe.wait_ge(s("qs_loaded"), 16 * 5)
                pe.sem_inc(s("qs_loaded"), -(16 * 5))
                for h in range(H):
                    pe.wait_ge(s(f"max{h % 2}_free"), 1)
                    pe.sem_inc(s(f"max{h % 2}_free"), -1)
                    for th in range(KL):
                        mm = pe.matmul(M[h % 2][:, th * L:(th + 1) * L], QS[0:K_MAX, h // 2, th * P:(th + 1) * P],
                                       KS[0:K_MAX, h, :], start=True, stop=True)
                    mm.then_inc(s(f"max{h % 2}_ready"), 1)
                pe.wait_ge(s("nm_parts_ready"), 1)
                pe.sem_inc(s("nm_parts_ready"), -1)
                pe.wait_ge(s("bank_x2_free"), 1)
                pe.sem_inc(s("bank_x2_free"), -1)
                for th in range(KL):
                    mm = pe.transpose(bank16[7][0:6 * GRP, th * P:(th + 1) * P],
                                      nm_parts[:, th].rearrange("p j n g -> p (j n g)"), ident16[:])
                mm.then_inc(s("nm_T_ready"), 1)
                pe.wait_ge(s("max_rows_loaded"), 16)
                pe.sem_inc(s("max_rows_loaded"), -16)

                def scores(n):
                    h = heads[n]
                    pe.wait_ge(s(f"scores{n % 2}_free"), 1)
                    pe.sem_inc(s(f"scores{n % 2}_free"), -1)
                    for sh in range(KL):
                        mm = pe.matmul(SC[n % 2][:, sh * L:(sh + 1) * L], KS[0:K_ALL, h, sh * P:(sh + 1) * P],
                                       QS[0:K_ALL, h // 2, :], start=True, stop=True)
                    mm.then_inc(s(f"scores{n % 2}_ready"), 1)

                def values(q):
                    if q == 0:
                        pe.wait_ge(s("v_aug_ready"), 1)
                        pe.sem_inc(s("v_aug_ready"), -1)
                    pe.wait_ge(s("probs_ready"), 4)
                    pe.sem_inc(s("probs_ready"), -4)
                    pe.wait_ge(s("o_bank_free"), 1)
                    pe.sem_inc(s("o_bank_free"), -1)
                    for sh in range(KL):
                        for jj in range(4):
                            mm = pe.matmul(O[32 * jj:32 * jj + 32, 0:L], v_aug[:, sh, heads[4 * q + jj], :],
                                           probs[(4 * q + jj) % 8][:, sh * L:(sh + 1) * L], start=(sh == 0), stop=(sh == 1))
                    mm.then_inc(s("o_bank_ready"), 1)
                    pe.drain().then_inc(s("probs_free"), 4)

                for n in range(H):
                    scores(n)
                    if n % 4 == 1 and n > 4:
                        values(n // 4 - 1)
                pe.drain().then_inc(s("qs_free"), 1)
                values(3)
                pe.sem_inc(s("v_aug_free"), 1)
                pe.wait_ge(s("xr_ready"), 1)
                pe.sem_inc(s("xr_ready"), -1)
                pe.wait_ge(s("bank_x0_free"), 1)
                pe.sem_inc(s("bank_x0_free"), -1)
                for k in range(KL):
                    mm = pe.transpose(X[0][:, k * P:(k + 1) * P], xr[:, k * P:(k + 1) * P], ident[:])
                mm.then_inc(s("xr_T_ready"), 1)
                pe.wait_ge(s("xrT_ready"), 1)
                pe.sem_inc(s("xrT_ready"), -1)
                pe.wait_ge(s("bank_x1_free"), 1)
                pe.sem_inc(s("bank_x1_free"), -1)
                for k in range(KL):
                    mm = pe.matmul(X[1][:], xrT[:, k, :], wcT[:, k, :], start=(k == 0), stop=(k == KL - 1))
                mm.then_inc(s("logit_bank_ready"), 1)
                pe.wait_ge(s("w_top_ready"), 1)
                pe.sem_inc(s("w_top_ready"), -1)
                pe.wait_ge(s("bank_x2_free"), 1)
                pe.sem_inc(s("bank_x2_free"), -1)
                for k in range(KG):
                    mm = pe.transpose(X[2][:, k * P:(k + 1) * P], w_top[:, k * P:(k + 1) * P], ident[:])
                mm.then_inc(s("w_T_bank_ready"), 1)
                pe.wait_ge(s("wT_ready"), 1)
                pe.sem_inc(s("wT_ready"), -1)
                pe.wait_ge(s("bank_x0_free"), 1)
                pe.sem_inc(s("bank_x0_free"), -1)
                for k in range(KG):
                    mm = pe.matmul(X[0][:, 0:P], genes[:, k, :], wT[:, k, :], start=(k == 0), stop=(k == KG - 1))
                mm.then_inc(s("expr_ready"), 1)
                pe.wait_ge(s("exprT_ready"), 1)
                pe.sem_inc(s("exprT_ready"), -1)
                pe.wait_ge(s("bank_x1_free"), 1)
                pe.sem_inc(s("bank_x1_free"), -1)
                pe.matmul(X[1][:], exprT[:], wduT[:], start=True, stop=True).then_inc(s("du_ready"), 1)

        @block.vector
        def _(dve):
            for name in ("conv0_free", "conv1_free", "x_b_free", "mask_b_free", "o_nat_free", "tanh_free", "max0_free",
                         "max1_free"):
                dve.sem_inc(s(name), 1)
            dve.wait_ge(s("weights_in"), 48)
            dve.sem_inc(s("weights_in"), -48)
            for n in range(3):
                dve.tensor_reduce(abs_sum[:, n:n + 1], w_raw[:, n, :], AX.X, ALU.add, apply_absolute_value=True)
            dve.drain().then_inc(s("abs_sum_ready"), 1)
            for k in range(2):
                dve.sem_inc(s(f"x_in{k}_free"), 1)
            dve.wait_ge(s("gamma_sum_ready"), 1)
            dve.sem_inc(s("gamma_sum_ready"), -1)
            dve.tensor_scalar(gammas[:], gammas[:], 1.0 / (HID * L), 1e-5, ALU.mult, ALU.max)
            dve.drain()
            dve.reciprocal(inv_gammas[:], gammas[:])
            dve.drain().then_inc(s("gammas_ready"), 1)
            for n in range(3):
                dve.tensor_scalar(w_raw[:, n, :], w_raw[:, n, :], inv_gammas[:, n:n + 1], 1.0, ALU.mult, ALU.min)
                dve.drain()
                dve.tensor_scalar(w_raw[:, n, :], w_raw[:, n, :], -1.0, MAGIC, ALU.max, ALU.add)
                dve.drain()
                if n > 0:
                    dve.wait_ge(s("w_int_free"), 1)
                    dve.sem_inc(s("w_int_free"), -1)
                dve.tensor_scalar(w_int[:], w_raw[:, n, :], -MAGIC, None, ALU.add).then_inc(s("w_int_ready"), 1)
            dve.drain().then_inc(s("weights_done"), 1)
            dve.wait_ge(s("vectors_in"), 16 * 7)
            dve.sem_inc(s("vectors_in"), -(16 * 7))
            dve.tensor_scalar(temp_scale[:, 0:1], temp_scale[:, 0:1], 0.1, None, ALU.max)
            dve.drain()
            dve.reciprocal(temp_scale[:, 0:1], temp_scale[:, 0:1])
            with dve.Fori(0, B // 2) as i:
                for k in range(2):
                    dve.wait_ge(s(f"x_in{k}_loaded"), 16)
                    dve.sem_inc(s(f"x_in{k}_loaded"), -16)
                    dve.bn_stats(stat6[:], x_in[k][:])
                    dve.drain().then_inc(s(f"x_in{k}_free"), 1)
                    dve.bn_aggr(stat2[:], stat6[:])
                    dve.drain()
                    dve.tensor_copy(mv_all[:, 2 * i + k, :], stat2[:])
            dve.drain().then_inc(s("var_all_ready"), 1)
            dve.wait_ge(s("rstd_all_ready"), 1)
            dve.sem_inc(s("rstd_all_ready"), -1)
            with dve.Fori(0, B // 2) as i:
                for k in range(2):
                    dve.wait_ge(s(f"x_in{k}_loaded"), 16)
                    dve.sem_inc(s(f"x_in{k}_loaded"), -16)
                    dve.wait_ge(s(f"xn_in{k}_free"), 1)
                    dve.sem_inc(s(f"xn_in{k}_free"), -1)
                    dve.tensor_scalar(xn_in[k][:], x_in[k][:], mv_all[:, 2 * i + k, 0:1], rstd_all[:, bass.ds(2 * i + k, 1)],
                                      ALU.subtract, ALU.mult).then_inc(s(f"xn_in{k}_ready"), 1)
                    dve.drain().then_inc(s(f"x_in{k}_free"), 1)
            dve.wait_ge(s("seq_all_dve"), 1)
            dve.sem_inc(s("seq_all_dve"), -1)
            with dve.Fori(0, H // 2) as i:
                for k in range(2):
                    dve.wait_ge(s(f"conv{k}_ready"), 1)
                    dve.sem_inc(s(f"conv{k}_ready"), -1)
                    q = qT[:].rearrange("p s b c -> p (s b) c")[:, :, bass.ds((2 * i + k) * HD, HD)]
                    n = 2 * k
                    for lh in range(KL):
                        for bh in range(2):
                            r = slice(lh * B + bh * (B // 2), lh * B + (bh + 1) * (B // 2))
                            dve.tensor_tensor(prod[:, r], banks[4 * k + 2 * lh + bh][:].rearrange("p (b j i) -> p b j i", j=HD, i=HD),
                                              q[:, r, :].unsqueeze(2).broadcast_to([P, B // 2, HD, HD]), ALU.mult)
                    dve.drain().then_inc(s(f"conv{k}_free"), 1)
                    dve.tensor_reduce(yT[:].rearrange("p s b c -> p (s b) c")[:, :, bass.ds((2 * i + k) * HD, HD)], prod,
                                      AX.X, ALU.add)
                    dve.drain()
            dve.sem_inc(s("y_all_ready"), 1)
            dve.wait_ge(s("clear_dve"), 1)
            dve.sem_inc(s("clear_dve"), -1)
            dve.wait_ge(s("mask_T_ready"), 1)
            dve.sem_inc(s("mask_T_ready"), -1)
            dve.tensor_copy(mask_cols[:].rearrange("p b k -> p (b k)"), banks[5][:, 0:KL * B])
            dve.drain().then_inc(s("mask_T_taken"), 1)

            def layer_norm(src, done):
                dve.bn_stats(st6[:], src)
                dve.drain()
                dve.bn_aggr(col(MEAN, 2), st6[:]).then_inc(s("var_ready"), 1)
                dve.wait_ge(s("rstd_ready"), 1)
                dve.sem_inc(s("rstd_ready"), -1)
                dve.tensor_scalar(xn[:], src, col(MEAN), col(RSTD), ALU.subtract, ALU.mult)
                dve.drain()
                if done:
                    dve.sem_inc(s(done), 1)

            with dve.Fori(0, B) as b:
                dve.wait_ge(s("y_T_ready"), 1)
                dve.sem_inc(s("y_T_ready"), -1)
                dve.wait_ge(s("x_b_loaded"), 16)
                dve.sem_inc(s("x_b_loaded"), -16)
                dve.tensor_tensor(x1[:], X[0][:, 0:L], x_b[:], ALU.add)
                dve.drain().then_inc(s("bank_x0_free"), 1)
                dve.sem_inc(s("x_b_free"), 1)
                dve.sem_inc(s("x1_ready"), 1)
                layer_norm(x1[:], None)
                dve.tensor_reduce(col(QX), xn[:], AX.X, ALU.max, apply_absolute_value=True)
                dve.drain()
                dve.tensor_scalar(col(QX), col(QX), 1e-5, 1.0 / 127.0, ALU.max, ALU.mult)
                dve.drain()
                dve.reciprocal(col(SX), col(QX))
                dve.drain().then_inc(s("sx_ready"), 1)
                dve.tensor_scalar(xn[:], xn[:], col(SX), MAGIC, ALU.mult, ALU.add).then_inc(s("xq_ready"), 1)
                dve.tensor_scalar(col(SG), col(QX), gammas[:, 0:1], 0.5, ALU.mult, ALU.mult)
                dve.tensor_scalar(col(KAPPA), col(QX), gammas[:, 1:2], None, ALU.mult)
                dve.drain().then_inc(s("sg_ready"), 1)
                dve.tensor_tensor(col(KAPPA), col(KAPPA), col(SG), ALU.mult)
                for half in range(2):
                    dve.wait_ge(s("tanh_ready"), 1)
                    dve.sem_inc(s("tanh_ready"), -1)
                    dve.scalar_tensor_tensor(u_g[:], tanh_g[:], 1.0, X[0][:], ALU.add, ALU.mult)
                    dve.drain().then_inc(s("gate_bank_free"), 1)
                    dve.sem_inc(s("tanh_free"), 1)
                    dve.tensor_tensor(hid[:, 512 * half:512 * (half + 1)], u_g[:], X[1][:], ALU.mult)
                    dve.drain().then_inc(s("val_bank_free"), 1)
                dve.tensor_reduce(col(QH), hid[:], AX.X, ALU.max, apply_absolute_value=True)
                dve.drain()
                dve.tensor_scalar(col(QH), col(QH), col(KAPPA), 1e-5, ALU.mult, ALU.max)
                dve.drain()
                dve.tensor_scalar(col(QH), col(QH), 1.0 / 127.0, None, ALU.mult)
                dve.drain()
                dve.reciprocal(col(SH), col(QH))
                dve.tensor_scalar(col(SO), col(QH), gammas[:, 2:3], None, ALU.mult)
                dve.drain()
                dve.tensor_scalar(col(SH), col(SH), col(KAPPA), None, ALU.mult)
                dve.drain()
                dve.tensor_scalar(hid[:], hid[:], col(SH), MAGIC, ALU.mult, ALU.add).then_inc(s("hq_ready"), 1)
                dve.wait_ge(s("ffn_ready"), 1)
                dve.sem_inc(s("ffn_ready"), -1)
                dve.wait_ge(s("x1b_ready"), 1)
                dve.sem_inc(s("x1b_ready"), -1)
                dve.scalar_tensor_tensor(x2[:], X[2][:, 0:L], col(SO), x1b[:], ALU.mult, ALU.add)
                dve.drain().then_inc(s("bank_x2_free"), 1)
                layer_norm(x2[:], "xn2_ready")
                dve.wait_ge(s("kv_bank_ready"), 1)
                dve.sem_inc(s("kv_bank_ready"), -1)
                dve.wait_ge(s("mask_q_ready"), 1)
                dve.sem_inc(s("mask_q_ready"), -1)
                dve.wait_ge(s("v_aug_free"), 1)
                dve.sem_inc(s("v_aug_free"), -1)
                dve.scalar_tensor_tensor(qk[:, 1, :], mask_b[:], bqk[:, 1:2], X[1][:, 0:L], ALU.mult, ALU.add)
                for sh in range(KL):
                    dve.scalar_tensor_tensor(v_aug[:, sh, :, 0:HD], bv[:].rearrange("p (h d) -> p h d", d=HD),
                                             mask_cols[:, b, sh:sh + 1],
                                             X[1][:, L + sh * P:L + (sh + 1) * P].rearrange("p (h d) -> p h d", d=HD),
                                             ALU.mult, ALU.add)
                dve.drain().then_inc(s("bank_x1_free"), 1)
                dve.sem_inc(s("v_aug_ready"), 1)
                dve.wait_ge(s("q_bank_ready"), 1)
                dve.sem_inc(s("q_bank_ready"), -1)
                dve.scalar_tensor_tensor(qk[:, 0, :], X[0][:, 0:L], bqk[:, 0:1], mask_q[:], ALU.add, ALU.mult)
                dve.drain().then_inc(s("bank_x0_free"), 1)
                dve.sem_inc(s("qk_ready"), 1)
                for h in range(H):
                    dve.wait_ge(s(f"max{h % 2}_ready"), 1)
                    dve.sem_inc(s(f"max{h % 2}_ready"), -1)
                    dve.tensor_reduce(neg_max[:, :, h:h + 1], M[h % 2][:].rearrange("p (t s) -> p t s", s=L), AX.X,
                                      ALU.max, negate=True).then_inc(s(f"max{h % 2}_free"), 1)
                dve.drain().then_inc(s("neg_max_ready"), 1)
                dve.wait_ge(s("o_nat_loaded"), 32)
                dve.sem_inc(s("o_nat_loaded"), -32)
                dve.reciprocal(o_den[:], o_den[:])
                dve.tensor_tensor(o_nat[:], o_nat[:], mask_b[:], ALU.mult)
                dve.drain().then_inc(s("mask_b_free"), 1)
                dve.tensor_tensor(o_nat[:], o_nat[:], o_den[:], ALU.mult)
                dve.drain()
                dve.tensor_tensor(x3[:], x2[:], o_nat[:], ALU.add)
                dve.drain().then_inc(s("o_nat_free"), 1)
                layer_norm(x3[:], "xn3_ready")
                dve.wait_ge(s("rr_ready"), 1)
                dve.sem_inc(s("rr_ready"), -1)
                dve.scalar_tensor_tensor(xr[:], xn[:], col(RR), norm_w[:], ALU.mult, ALU.mult).then_inc(s("xr_ready"), 1)
                dve.wait_ge(s("logits_ready"), 1)
                dve.sem_inc(s("logits_ready"), -1)
                dve.max(best[:], logits[:])
                dve.drain()
                dve.tensor_scalar(col(NB), best[:, 0:1], temp_scale[:, 0:1], -1.0, ALU.mult, ALU.mult).then_inc(
                    s("nb_ready"), 1)
                dve.match_replace(left[:], best[:], logits[:], GONE)
                for _ in range(TOPK // 8 - 1):
                    dve.drain()
                    dve.max(best[:], left[:])
                    dve.drain()
                    dve.match_replace(left[:], best[:], left[:], GONE)
                dve.drain()
                dve.wait_ge(s("e_ready"), 1)
                dve.sem_inc(s("e_ready"), -1)
                dve.scalar_tensor_tensor(w_top[:], left[:], GONE, e_all[:], ALU.is_equal, ALU.mult)
                dve.drain().then_inc(s("w_top_ready"), 1)
                dve.tensor_reduce(col(WS), w_top[:], AX.X, ALU.add)
                dve.drain()
                dve.reciprocal(col(RS), col(WS))
                dve.drain().then_inc(s("rs_ready"), 1)
                dve.tensor_scalar(col(RSS), col(RS), temp_scale[:, 1:2], None, ALU.mult)
                dve.wait_ge(s("down_ready"), 1)
                dve.sem_inc(s("down_ready"), -1)
                dve.tensor_tensor(dx[:], down[:], xr[:], ALU.mult)
                dve.drain()
                dve.scalar_tensor_tensor(dx[:], X[1][:, L:2 * L], col(RSS), dx[:], ALU.mult, ALU.mult)
                dve.drain().then_inc(s("bank_x1_free"), 1)
                dve.wait_ge(s("res_free"), 1)
                dve.sem_inc(s("res_free"), -1)
                dve.tensor_tensor(res[:], dx[:], x3[:], ALU.add).then_inc(s("res_ready"), 1)
                dve.drain()


_IN = dict(x="x", ctx_2048="ctx", mask_Bx1x2048_fk1="mask", L0_xattn_ssm_kernel="ssm", L0_xattn_D="d",
           L0_ffn_gate_w="gate_w", L0_ffn_gate_b="gate_b", L0_ffn_val_w="val_w", L0_ffn_val_b="val_b",
           L0_ffn_out_w="out_w", L0_ffn_out_b="out_b", L1_xattn_Wq="wq", L1_xattn_bq="bq", L1_xattn_Wk="wk",
           L1_xattn_bk="bk", L1_xattn_Wv="wv", L1_xattn_bv="bv", L1_ffn_Wc="wc", L1_ffn_temperature="temperature",
           L1_ffn_genes="genes", L1_ffn_Wd="wd", L1_ffn_Wu="wu", L1_ffn_norm_w="norm_w", L1_ffn_scale="scale")


def kernel(**inputs):
    import numpy as np
    import concourse.bacc as bacc
    from concourse.bass_utils import run_bass_kernel_spmd

    nc = bacc.Bacc("TRN2", target_bir_lowering=False, num_devices=1)
    arrays, aps = {}, {}
    for name, short in _IN.items():
        v = np.ascontiguousarray(inputs[name])
        if v.ndim == 0:
            v = v.reshape(1)
        if short == "ssm":
            v = np.concatenate([np.zeros((v.shape[0], P), v.dtype), v], axis=1)
        arrays["in_" + short] = v
        aps[short] = nc.dram_tensor("in_" + short, v.shape, mybir.dt.from_np(v.dtype), kind="ExternalInput").ap()
    shape = inputs["x"].shape
    out = nc.dram_tensor("out_x", shape, F32, kind="ExternalOutput").ap()
    build(nc, aps, out)
    r = run_bass_kernel_spmd(nc, [arrays], core_ids=[0])
    return r.results[0]["out_x"]
```

```python
from contextlib import ExitStack

import concourse.bass as bass
from concourse import mybir

F32 = mybir.dt.float32
BF16 = mybir.dt.bfloat16
U32 = mybir.dt.uint32
ALU = mybir.AluOpType
ACT = mybir.ActivationFunctionType
AX = mybir.AxisListType

P = 128
MAGIC = 12582912.0
LN_EPS = 1e-5
RMS_EPS = 1.1920928955078125e-07
NEG = 1000000.0
GONE = -3.0e38
TOPK = 32


def split3(eng, whole, rest, parts):
    eng.tensor_copy(parts[0], whole)
    eng.drain()
    eng.tensor_tensor(rest, whole, parts[0], ALU.subtract)
    eng.drain()
    eng.tensor_copy(parts[1], rest)
    eng.drain()
    eng.tensor_tensor(parts[2], rest, parts[1], ALU.subtract)


def build(nc, a, out):
    B, C, L = a["x"].shape
    H, HD = a["ssm"].shape[0], C // a["ssm"].shape[0]
    HID = a["gate_w"].shape[0]
    G, GD = a["genes"].shape
    KL, KH, KG = L // P, HID // P, G // P
    QK_SCALE = 1.0 / float(HD) ** 0.5
    TERM_Q, TERM_K = (0, 0, 0, 1, 1, 2), (0, 1, 2, 0, 1, 0)
    NT = len(TERM_Q)
    ROWS, GRP = 2 * HD * NT, H // 2
    ROW_MASK, ROW_MAX = ROWS, ROWS + NT
    K_MAX, K_ALL = ROWS + NT, ROWS + NT + 6
    assert C == P and L == 2 * P and HD == 8 and K_ALL <= P

    scr_toep = nc.dram_tensor("scr_toep", [H, P + L], F32, kind="Internal").ap()
    scr_toeps = nc.dram_tensor("scr_toeps", [H, P, L], F32, kind="Internal").ap()
    scr_q = nc.dram_tensor("scr_q", [2, ROWS, GRP, L], BF16, kind="Internal").ap()
    scr_k = nc.dram_tensor("scr_k", [2, ROWS, GRP, L], BF16, kind="Internal").ap()
    scr_mask = nc.dram_tensor("scr_mask", [B, 2, NT, L], BF16, kind="Internal").ap()
    scr_o = nc.dram_tensor("scr_o", [2, H, HD + 1, L], F32, kind="Internal").ap()
    scr_r = nc.dram_tensor("scr_r", [2, H, L], F32, kind="Internal").ap()

    with ExitStack() as ctx:
        def sb(name, shape, dt=F32):
            return ctx.enter_context(nc.sbuf_tensor(name, shape, dt))

        def sem(name):
            return ctx.enter_context(nc.semaphore(name))

        banks = [ctx.enter_context(nc.psum_tensor(f"bank{i}", [P, 512], F32)) for i in range(8)]

        ident = sb("ident", [P, P])
        ident16 = sb("ident16", [P, P], BF16)
        half_neg = sb("half_neg", [P, 16])
        wgvT = sb("wgvT", [P, KL, 2 * HID], BF16)
        woT = sb("woT", [P, KH, L], BF16)
        wqkvT = sb("wqkvT", [P, 3, P])
        wcT = sb("wcT", [P, KL, G])
        wduT = sb("wduT", [P, 2 * L])
        genes = sb("genes", [P, KG, P])
        b6 = sb("b6", [P, 2 * HID], BF16)
        gammas = sb("gammas", [P, 3])
        inv_gammas = sb("inv_gammas", [P, 3])
        out_b = sb("out_b", [P, L])
        norm_w = sb("norm_w", [P, L])
        bv = sb("bv", [P, C])
        bqk = sb("bqk", [P, 2])
        temp_scale = sb("temp_scale", [P, 2])
        mask_cols = sb("mask_cols", [P, B, KL])
        yT = sb("yT", [P, KL, B, C])

        w_raw = sb("w_raw", [P, 3, KH * L])
        w_int = sb("w_int", [P, KH * L], BF16)
        small_raw = sb("small_raw", [P, 3, P])
        wc_raw = sb("wc_raw", [P, KG, L])
        wdu_raw = sb("wdu_raw", [P, 2, 2, GD])
        bias_row = sb("bias_row", [1, 2, HID])
        bias_parts = w_raw[0:1].rearrange("p a n -> p (a n)")[:, KH * L:KH * L + 3 * HID].bitcast(BF16).rearrange(
            "p (n h) -> p n h", n=3)
        toep_row = sb("toep_row", [H, P + L])
        d_col = sb("d_col", [H, 1])
        mask_nat = sb("mask_nat", [2 * B, P])
        mask_rows = sb("mask_rows", [B, L])
        aug = sb("aug", [B, 2, L])
        aug_rest = sb("aug_rest", [B, 2, L])
        aug_parts = sb("aug_parts", [B, 2, 3, L], BF16)
        aug_terms = sb("aug_terms", [B, 2, NT, L], BF16)
        abs_sum = sb("abs_sum", [P, 3])
        one_rows = sb("one_rows", [6, H, L], BF16)
        ctx_in = [sb(f"ctx_in{k}", [P, L]) for k in range(2)]
        x_in = [sb(f"x_in{k}", [P, L]) for k in range(2)]
        xn_in = [sb(f"xn_in{k}", [P, L]) for k in range(2)]
        stat6 = sb("stat6", [P, 6])
        stat2 = sb("stat2", [P, 2])
        mv_all = sb("mv_all", [P, B, 2])
        rstd_all = sb("rstd_all", [P, B])
        cT = sb("cT", [P, KL, B, C])
        qT = sb("qT", [P, KL, B, C])
        toep = [sb(f"toep{k}", [P, L]) for k in range(2)]
        kv = [sb(f"kv{k}", [P, KL * B, HD, HD]) for k in range(2)]
        prod = w_raw[:].rearrange("p a n -> p (a n)")[:, 0:KL * B * HD * HD].rearrange(
            "p (s j i) -> p s j i", j=HD, i=HD)

        spare = {"w_raw": w_raw[:].rearrange("p a n -> p (a n)"), "cT": cT[:].rearrange("p s b c -> p (s b c)"),
                 "qT": qT[:].rearrange("p s b c -> p (s b c)"),
                 "kv0": kv[0][:].rearrange("p s j i -> p (s j i)"), "kv1": kv[1][:].rearrange("p s j i -> p (s j i)")}
        used = dict.fromkeys(spare, 0)

        def inside(tile, shape, dt=F32):
            n = 1
            for m in shape[1:]:
                n *= m
            words = n if dt == F32 else n // 2
            view = spare[tile][:, used[tile]:used[tile] + words]
            used[tile] += words
            assert used[tile] <= spare[tile].shape[1]
            view = view if dt == F32 else view.bitcast(dt)
            names = "abc"[:len(shape) - 1]
            if len(names) == 1:
                return view
            return view.rearrange(f"p ({' '.join(names)}) -> p {' '.join(names)}", **dict(zip(names, shape[1:])))

        x_b = sb("x_b", [P, L])
        y_in = sb("y_in", [P, KL, P])
        x1 = inside("qT", [P, L])
        x1b = inside("qT", [P, L])
        xq = inside("qT", [P, L])
        xqT = inside("qT", [P, KL, P], BF16)
        st6 = sb("st6", [P, 6])
        st = sb("st", [P, 24])
        s6 = sb("s6", [P, P], BF16)
        s6T = inside("qT", [P, P], BF16)
        tanh_g = inside("qT", [P, 512])
        u_g = inside("qT", [P, 512])
        hid = inside("w_raw", [P, HID])
        hqT = inside("w_raw", [P, KH, P], BF16)
        xn2 = inside("qT", [P, L])
        ctx_b = sb("ctx_b", [P, L])
        mask_b = sb("mask_b", [P, L])
        mask_q = sb("mask_q", [P, L])
        ctx_m = sb("ctx_m", [P, L])
        qk = inside("kv1", [P, 2, L])
        qk_rest = inside("kv1", [P, 2, L])
        qk_parts = inside("kv1", [P, 3, 2, L], BF16)
        v_aug = [sb(f"v_aug{k}", [P, KL, H, 32]) for k in range(2)]
        QS = [inside("w_raw", [P, GRP, L], BF16) for k in range(2)]
        KS = [sb(f"KS{k}", [P, H, L], BF16) for k in range(2)]
        neg_max = sb("neg_max", [P, KL, H])
        nm_rest = sb("nm_rest", [P, KL, H])
        nm_parts = sb("nm_parts", [P, KL, 2, 3, GRP], BF16)
        nm_rows = sb("nm_rows", [6 * GRP, L], BF16)
        probs = [inside("cT", [P, L * KL]) for k in range(8)]
        o_quad = inside("kv0", [P, 4, L])
        o_nat = inside("kv0", [P, L])
        o_den = inside("kv0", [P, L])
        attn = inside("kv0", [P, L])
        den32 = sb("den32", [P, 32])
        mask32 = sb("mask32", [P, 32])
        x3 = inside("qT", [P, L])
        xn3 = inside("qT", [P, L])
        xn3_sq = inside("w_raw", [P, L])
        xr = inside("qT", [P, L])
        xrT = inside("kv0", [P, KL, P])
        logits = inside("w_raw", [P, G])
        left = inside("w_raw", [P, G])
        best = sb("best", [P, 8])
        e_all = inside("w_raw", [P, G])
        w_top = inside("qT", [P, G])
        wT = inside("w_raw", [P, KG, P])
        exprT = inside("qT", [P, P])
        down = inside("kv1", [P, L])
        dx = inside("qT", [P, L])
        res = sb("res", [P, L])

        made = {}

        def s(name):
            if name not in made:
                made[name] = ctx.enter_context(nc.semaphore(name))
            return made[name]

        (MEAN1, VAR1, RSTD1, MEAN2, VAR2, RSTD2, MEAN3, VAR3, RSTD3, QX, SX, SG, KAPPA, QH, RH, SH, SO, SQ, RR, NB, WS, RS,
         RSS, R0) = range(24)

        def col(n, m=1):
            return st[:, n:n + m]

        bank16 = [b[:].bitcast(BF16) for b in banks]
        M, SC, O, X5, X6, X7 = banks[0:2], banks[2:4], banks[4], banks[5], banks[6], banks[7]
        x2_all = yT

        FFN0, PROJ, MAXIMA, PROBS, FFN1 = 4, 3, 2, 1, 0
        STAGES = (FFN0, PROJ, MAXIMA, PROBS, FFN1)

        def runs(iteration, eng):
            for d in range(-FFN0, 0):
                iteration(d, d % 2, {g for g in STAGES if 0 <= d + g < B})
            with eng.Fori(0, (B - FFN0) // 2) as i:
                for k in range(2):
                    iteration(2 * i + k, k, set(STAGES))
            for d in range(B - FFN0, B):
                iteration(d, d % 2, {g for g in STAGES if 0 <= d + g < B})

        heads = [4 * jj + q for q in range(4) for jj in range(4)]

        block = ctx.enter_context(nc.Block())

        @block.sync
        def _(sp):
            sp.sem_inc(s("qk_parts_free"), 1)
            sp.sem_inc(s("o_quad_free"), 1)
            for n, w in enumerate((a["gate_w"], a["val_w"])):
                sp.dma_start(w_raw[:, n, :].rearrange("p (k d) -> p k d", d=L),
                             w.rearrange("(k p) d -> p k d", p=P)).then_inc(s("weights_in"), 16)
            sp.dma_start(w_raw[:, 2, :].rearrange("p (k d) -> p k d", d=HID),
                         a["out_w"].rearrange("(k p) d -> p k d", p=P)).then_inc(s("weights_in"), 16)
            for n, w in enumerate((a["wq"], a["wk"], a["wv"])):
                sp.dma_start(small_raw[:, n, :], w).then_inc(s("small_in"), 16)
            sp.dma_start(wc_raw[:], a["wc"].rearrange("(k p) d -> p k d", p=P)).then_inc(s("small_in"), 16)
            for n, w in enumerate((a["wd"], a["wu"])):
                sp.dma_start(wdu_raw[:, n, :, :], w.rearrange("(k p) g -> p k g", p=P)).then_inc(s("small_in"), 16)
            sp.dma_start(bias_row[:, 0, :], a["gate_b"].rearrange("(o n) -> o n", o=1)).then_inc(s("bias_in"), 16)
            sp.dma_start(bias_row[:, 1, :], a["val_b"].rearrange("(o n) -> o n", o=1)).then_inc(s("bias_in"), 16)
            sp.dma_start(mask_nat[:], a["mask"].rearrange("b o (k l) -> (b o k) l", l=P)).then_inc(s("mask_nat_in"), 16)
            sp.dma_start(mask_rows[:], a["mask"].rearrange("b o l -> (b o) l")).then_inc(s("mask_rows_in"), 16)
            sp.dma_start(toep_row[:], a["ssm"]).then_inc(s("toep_row_in"), 16)
            sp.dma_start(d_col[:], a["d"].rearrange("(h o) -> h o", o=1)).then_inc(s("toep_row_in"), 16)
            for tile, src in ((out_b, a["out_b"]), (norm_w, a["norm_w"]), (bv, a["bv"])):
                n = src.shape[0]
                sp.dma_start(tile[:], bass.AP(src.tensor, 0, [[0, P], [1, n]])).then_inc(s("vectors_in"), 16)
            for n, src in enumerate((a["bq"], a["bk"])):
                sp.dma_start(bqk[:, n:n + 1], src.rearrange("(p o) -> p o", o=1)).then_inc(s("vectors_in"), 16)
            for n, src in enumerate((a["temperature"], a["scale"])):
                sp.dma_start(temp_scale[:, n:n + 1], bass.AP(src.tensor, 0, [[0, P], [1, 1]])).then_inc(s("vectors_in"), 16)
            sp.wait_ge(s("genes_clear"), 1)
            sp.sem_inc(s("genes_clear"), -1)
            sp.dma_start(genes[:, :, 0:GD], a["genes"].rearrange("(k p) c -> p k c", p=P)).then_inc(s("genes_in"), 16)
            sp.wait_ge(s("toep_row_ready"), 1)
            sp.sem_inc(s("toep_row_ready"), -1)
            sp.dma_start(scr_toep, toep_row[:]).then_inc(s("toep_written"), 16)
            sp.wait_ge(s("toep_written"), 16)
            sp.sem_inc(s("toep_written"), -16)
            sp.dma_start(scr_toeps, bass.AP(scr_toep.tensor, P, [[P + L, H], [-1, P], [1, L]])).then_inc(
                s("toeps_written"), 16)

            with sp.Fori(0, B // 2) as i:
                for k in range(2):
                    sp.wait_ge(s(f"x_in{k}_free"), 1)
                    sp.sem_inc(s(f"x_in{k}_free"), -1)
                    sp.dma_start(x_in[k][:], a["x"][2 * i + k]).then_inc(s(f"x_in{k}_loaded"), 16)
            with sp.Fori(0, B // 2) as i:
                for k in range(2):
                    sp.wait_ge(s(f"x_in{k}_free"), 1)
                    sp.sem_inc(s(f"x_in{k}_free"), -1)
                    sp.dma_start(x_in[k][:], a["x"][2 * i + k]).then_inc(s(f"x_in{k}_loaded"), 16)
                    sp.wait_ge(s(f"ctx_in{k}_free"), 1)
                    sp.sem_inc(s(f"ctx_in{k}_free"), -1)
                    sp.dma_start(ctx_in[k][:], a["ctx"][2 * i + k]).then_inc(s(f"ctx_in{k}_loaded"), 16)
            sp.wait_ge(s("toeps_written"), 16)
            sp.sem_inc(s("toeps_written"), -16)
            with sp.Fori(0, H // 2) as i:
                for k in range(2):
                    sp.wait_ge(s(f"toep{k}_free"), 1)
                    sp.sem_inc(s(f"toep{k}_free"), -1)
                    sp.dma_start(toep[k][:], scr_toeps[2 * i + k]).then_inc(s(f"toep{k}_loaded"), 16)
            sp.wait_ge(s("clear_sp"), 1)
            sp.sem_inc(s("clear_sp"), -1)
            sp.wait_ge(s("bias_parts_ready"), 1)
            sp.sem_inc(s("bias_parts_ready"), -1)
            for r in range(NT):
                sp.dma_start(b6[r:r + 1, :], bias_parts[0:1, TERM_K[r], :]).then_inc(s("b6_loaded"), 16)
            sp.wait_ge(s("mask_terms_ready"), 1)
            sp.sem_inc(s("mask_terms_ready"), -1)
            sp.dma_start(scr_mask.rearrange("b w t l -> b (w t l)"), aug_terms[:].rearrange("b w t l -> b (w t l)")
                         ).then_inc(s("mask_terms_written"), 16)
            for k in range(2):
                sp.dma_start(KS[k][ROW_MAX:ROW_MAX + 6, :, :], one_rows[:]).then_inc(s("ks_ones_in"), 16)
            sp.wait_ge(s("mask_terms_written"), 16)
            sp.sem_inc(s("mask_terms_written"), -16)
            sp.wait_ge(s("ks_ones_in"), 32)
            sp.sem_inc(s("ks_ones_in"), -32)
            sp.wait_ge(s("b6_loaded"), 16 * NT)
            sp.sem_inc(s("b6_loaded"), -(16 * NT))
            sp.sem_inc(s("b6_ready"), 1)
            sp.wait_ge(s("y_all_ready"), 1)
            sp.sem_inc(s("y_all_ready"), -1)

            def iteration(d, p, on):
                if FFN0 in on:
                    b = d + FFN0
                    sp.wait_ge(s("x_b_free"), 1)
                    sp.sem_inc(s("x_b_free"), -1)
                    sp.dma_start(x_b[:], a["x"][b]).then_inc(s("x_b_loaded"), 16)
                    sp.wait_ge(s("y_in_free"), 1)
                    sp.sem_inc(s("y_in_free"), -1)
                    sp.dma_start(y_in[:], yT[:, :, b, :]).then_inc(s("y_in_loaded"), 16)
                if PROBS in on:
                    sp.wait_ge(s("mask32_free"), 1)
                    sp.sem_inc(s("mask32_free"), -1)
                    sp.dma_start(mask32[:], bass.AP(a["mask"].tensor, (d + PROBS) * L, [[0, H], [32, L // 32], [1, 32]])
                                 ).then_inc(s("den_loaded"), 16)
                if FFN0 in on:
                    sp.wait_ge(s("ctx_b_free"), 1)
                    sp.sem_inc(s("ctx_b_free"), -1)
                    sp.dma_start(ctx_b[:], a["ctx"][b]).then_inc(s("ctx_b_loaded"), 16)
                    sp.wait_ge(s("mask_b_free"), 1)
                    sp.sem_inc(s("mask_b_free"), -1)
                    sp.dma_start(mask_b[:], bass.AP(a["mask"].tensor, b * L, [[0, P], [1, L]])).then_inc(
                        s("mask_b_loaded"), 16)
                if PROJ in on:
                    sp.wait_ge(s("qk_parts_ready"), 1)
                    sp.sem_inc(s("qk_parts_ready"), -1)
                    for t in range(NT):
                        for w, (scr, part) in enumerate(((scr_q, TERM_Q[t]), (scr_k, TERM_K[t]))):
                            at = (1 - p) * ROWS * GRP * L + t * GRP * L
                            dst = bass.AP(scr.tensor, at, [[L, GRP], [NT * GRP * L, 2 * HD], [1, L]])
                            sp.dma_start(dst, qk_parts[:, part, w, :]).then_inc(s("parts_written"), 16)
                if PROBS in on:
                    sp.wait_ge(s("o_written"), 64)
                    sp.sem_inc(s("o_written"), -64)
                    sp.sem_inc(s("o_quad_free"), 1)
                    at = (1 - p) * H * (HD + 1) * L + HD * L
                    sp.dma_start(den32[:], bass.AP(scr_o.tensor, at, [[(HD + 1) * L, H], [32, L // 32], [1, 32]])
                                 ).then_inc(s("den_loaded"), 16)
                    sp.wait_ge(s("o_nat_free"), 1)
                    sp.sem_inc(s("o_nat_free"), -1)
                    sp.dma_start(o_nat[:], scr_o[1 - p, :, 0:HD, :]).then_inc(s("o_nat_loaded"), 16)
                if PROJ in on:
                    sp.wait_ge(s("parts_written"), 16 * 2 * NT)
                    sp.sem_inc(s("parts_written"), -(16 * 2 * NT))
                    sp.sem_inc(s("qk_parts_free"), 1)
                    sp.wait_ge(s("qs_free"), 1)
                    sp.sem_inc(s("qs_free"), -1)
                    at = (d + PROJ) * (2 * NT * L)
                    sp.dma_start(QS[1 - p][ROW_MASK:ROW_MASK + NT, :, :],
                                 bass.AP(scr_mask.tensor, at, [[L, NT], [0, GRP], [1, L]])).then_inc(s("qs_loaded"), 16)
                    sp.dma_start(KS[1 - p][ROW_MASK:ROW_MASK + NT, :, :],
                                 bass.AP(scr_mask.tensor, at + NT * L, [[L, NT], [0, H], [1, L]])).then_inc(s("qs_loaded"), 16)
                    sp.dma_start(QS[1 - p][0:ROWS, :, :], scr_q[1 - p]).then_inc(s("qs_loaded"), 16)
                    for j in range(2):
                        rows = slice(ROWS // 2 * j, ROWS // 2 * (j + 1))
                        sp.dma_start(KS[1 - p][rows, :, :].rearrange("r (g j) l -> r g j l", j=2)[:, :, j, :],
                                     scr_k[1 - p, rows]).then_inc(s("qs_loaded"), 16)
                if PROBS in on:
                    sp.wait_ge(s("den_ready"), 1)
                    sp.sem_inc(s("den_ready"), -1)
                    sp.dma_start(scr_r[1 - p].rearrange("h (r l) -> (h r) l", l=32), den32[:]).then_inc(s("den_written"), 16)
                    sp.wait_ge(s("den_written"), 16)
                    sp.sem_inc(s("den_written"), -16)
                    sp.dma_start(o_den[:], bass.AP(scr_r.tensor, (1 - p) * H * L, [[L, H], [0, HD], [1, L]])
                                 ).then_inc(s("o_nat_loaded"), 16)

            runs(iteration, sp)

        @block.gpsimd
        def _(pool):
            pool.memset(ident[:], 0.0)
            pool.memset(ident16[:], 0.0)
            pool.memset(genes[:], 0.0)
            pool.memset(half_neg[:], -0.5)
            pool.memset(one_rows[:], 1.0)
            pool.drain().then_inc(s("genes_clear"), 1)
            for m in (ident, ident16):
                pool.affine_select(out=m[:], in_=m[:], compare_op=ALU.not_equal, fill=1.0, base=0,
                                   pattern=[[-1, P]], channel_multiplier=1)
            rows = one_rows[:].rearrange("r (g j) l -> r g j l", j=2)
            pool.affine_select(out=rows[:, :, 0, :], in_=rows[:, :, 0, :], compare_op=ALU.is_ge, fill=0.0, base=2,
                               pattern=[[0, GRP], [0, L]], channel_multiplier=-1)
            pool.affine_select(out=rows[:, :, 1, :], in_=rows[:, :, 1, :], compare_op=ALU.is_ge, fill=0.0, base=-3,
                               pattern=[[0, GRP], [0, L]], channel_multiplier=1)
            pool.drain().then_inc(s("ident_ready"), 1)
            for k in range(2):
                pool.memset(KS[k][:].bitcast(U32), 0)
                pool.memset(v_aug[k][:], 0.0)
            pool.memset(s6[:], 0.0)
            pool.memset(b6[:], 0.0)
            pool.memset(wduT[:], 0.0)
            pool.drain()
            for k in range(2):
                pool.memset(v_aug[k][:, :, :, HD:HD + 1], 1.0)
            pool.drain().then_inc(s("clear_act"), 1)
            pool.sem_inc(s("clear_dve"), 1)
            pool.sem_inc(s("clear_sp"), 1)
            pool.wait_ge(s("toep_row_in"), 32)
            pool.sem_inc(s("toep_row_in"), -32)
            pool.tensor_tensor(toep_row[:, P:P + 1], toep_row[:, P:P + 1], d_col[:], ALU.add).then_inc(
                s("toep_row_ready"), 1)
            pool.wait_ge(s("abs_sum_ready"), 1)
            pool.sem_inc(s("abs_sum_ready"), -1)
            pool.partition_all_reduce(gammas[:], abs_sum[:], P, bass.bass_isa.ReduceOp.add).then_inc(
                s("gamma_sum_ready"), 1)

            pool.wait_ge(s("var_all_ready"), 1)
            pool.sem_inc(s("var_all_ready"), -1)
            pool.tensor_scalar(rstd_all[:], mv_all[:, :, 1], LN_EPS, 1.0, ALU.add, ALU.mult)
            pool.drain()
            pool.tensor_tensor(rstd_all[:], rstd_all[:], half_neg[:], ALU.pow).then_inc(s("rstd_all_ready"), 1)
            pool.wait_ge(s("seq_all_ready"), 1)
            pool.sem_inc(s("seq_all_ready"), -1)
            with pool.Fori(0, H // 2) as i:
                for k in range(2):
                    pool.wait_ge(s(f"kv{k}_free"), 1)
                    pool.sem_inc(s(f"kv{k}_free"), -1)
                    kh = cT[:].rearrange("p s b c -> p (s b) c")[:, :, bass.ds((2 * i + k) * HD, HD)]
                    shape = [P, KL * B, HD, HD]
                    pool.tensor_tensor(kv[k][:], kh.unsqueeze(3).broadcast_to(shape),
                                       kh.unsqueeze(2).broadcast_to(shape), ALU.mult).then_inc(s(f"kv{k}_ready"), 1)

            pool.wait_ge(s("mask_rows_in"), 16)
            pool.sem_inc(s("mask_rows_in"), -16)
            pool.tensor_scalar(aug[:, 0, :], mask_rows[:], -NEG, 0.0, ALU.mult, ALU.add)
            pool.tensor_scalar(aug[:, 1, :], mask_rows[:], -1.0, 1.0, ALU.mult, ALU.add)
            pool.drain()
            split3(pool, aug[:], aug_rest[:], [aug_parts[:, :, n, :] for n in range(3)])
            pool.drain()
            for t in range(NT):
                pool.tensor_copy(aug_terms[:, 0, t, :], aug_parts[:, 0, TERM_Q[t], :])
                pool.tensor_copy(aug_terms[:, 1, t, :], aug_parts[:, 1, TERM_K[t], :])
            pool.drain().then_inc(s("mask_terms_ready"), 1)
            pool.wait_ge(s("bias_in"), 32)
            pool.sem_inc(s("bias_in"), -32)
            pool.wait_ge(s("gammas_ready"), 1)
            pool.sem_inc(s("gammas_ready"), -1)
            for n in range(2):
                pool.tensor_scalar(bias_row[:, n, :], bias_row[:, n, :], inv_gammas[0:1, n:n + 1], 1.0, ALU.mult, ALU.mult)
            pool.drain()
            flat = bias_row[:].rearrange("p n h -> p (n h)")
            pool.wait_ge(s("weights_done"), 1)
            pool.sem_inc(s("weights_done"), -1)
            split3(pool, flat, flat, [bias_parts[:, n, :] for n in range(3)])
            pool.drain().then_inc(s("bias_parts_ready"), 1)

            pool.sem_inc(s("ctx_b_free"), 1)
            pool.sem_inc(s("o_nat_free"), 1)

            def rstd(var, out_col, done):
                pool.tensor_scalar(col(out_col), col(var), LN_EPS, 1.0, ALU.add, ALU.mult)
                pool.drain()
                pool.tensor_tensor(col(out_col), col(out_col), half_neg[:, 0:1], ALU.pow).then_inc(s(done), 1)

            def iteration(d, p, on):
                if FFN1 in on:
                    pool.wait_ge(s("var_ready"), 1)
                    pool.sem_inc(s("var_ready"), -1)
                    rstd(VAR3, RSTD3, "rstd_ready")
                    pool.wait_ge(s("sq_ready"), 1)
                    pool.sem_inc(s("sq_ready"), -1)
                    pool.tensor_scalar(col(RR), col(SQ), 1.0 / L, RMS_EPS, ALU.mult, ALU.add)
                    pool.drain()
                    pool.tensor_tensor(col(RR), col(RR), half_neg[:, 0:1], ALU.pow).then_inc(s("rr_ready"), 1)
                if FFN0 in on:
                    pool.wait_ge(s("var_ready"), 1)
                    pool.sem_inc(s("var_ready"), -1)
                    rstd(VAR1, RSTD1, "rstd_ready")
                    pool.tensor_tensor(x1b[:], x1[:], out_b[:], ALU.add).then_inc(s("x1b_ready"), 1)
                    pool.wait_ge(s("sx_ready"), 1)
                    pool.sem_inc(s("sx_ready"), -1)
                    pool.tensor_copy(s6[:, 0:3], col(SX).broadcast_to([P, 3]))
                    pool.drain()
                    pool.tensor_tensor(col(R0), col(SX), s6[:, 0:1], ALU.subtract)
                    pool.drain()
                    pool.tensor_copy(s6[:, 3:5], col(R0).broadcast_to([P, 2]))
                    pool.drain()
                    pool.tensor_tensor(s6[:, 5:6], col(R0), s6[:, 3:4], ALU.subtract).then_inc(s("s6_ready"), 1)
                if PROJ in on:
                    pool.wait_ge(s("qk_ready"), 1)
                    pool.sem_inc(s("qk_ready"), -1)
                    pool.wait_ge(s("qk_parts_free"), 1)
                    pool.sem_inc(s("qk_parts_free"), -1)
                    split3(pool, qk[:], qk_rest[:], [qk_parts[:, n, :, :] for n in range(3)])
                    pool.drain().then_inc(s("qk_parts_ready"), 1)
                if FFN0 in on:
                    pool.wait_ge(s("ctx_b_loaded"), 16)
                    pool.sem_inc(s("ctx_b_loaded"), -16)
                    pool.wait_ge(s("mask_b_loaded"), 16)
                    pool.sem_inc(s("mask_b_loaded"), -16)
                    pool.wait_ge(s("ctx_m_free"), 1)
                    pool.sem_inc(s("ctx_m_free"), -1)
                    pool.tensor_tensor(ctx_m[:], ctx_b[:], mask_b[:], ALU.mult).then_inc(s("ctx_b_free"), 1)
                    pool.tensor_scalar(mask_q[:], mask_b[:], QK_SCALE, 1.0, ALU.mult, ALU.mult)
                    pool.drain().then_inc(s("ctx_m_ready"), 1)
                if MAXIMA in on:
                    pool.wait_ge(s("neg_max_ready"), 1)
                    pool.sem_inc(s("neg_max_ready"), -1)
                    split3(pool, neg_max[:].rearrange("p t (g j) -> p t j g", j=2),
                           nm_rest[:].rearrange("p t (g j) -> p t j g", j=2), [nm_parts[:, :, :, n, :] for n in range(3)])
                    pool.drain().then_inc(s("nm_parts_ready"), 1)
                if FFN0 in on:
                    pool.wait_ge(s("var_ready"), 1)
                    pool.sem_inc(s("var_ready"), -1)
                    rstd(VAR2, RSTD2, "rstd_ready")
                if PROBS in on:
                    pool.wait_ge(s("o_nat_loaded"), 32)
                    pool.sem_inc(s("o_nat_loaded"), -32)
                    pool.wait_ge(s("attn_free"), 1)
                    pool.sem_inc(s("attn_free"), -1)
                    pool.tensor_tensor(attn[:], o_nat[:], o_den[:], ALU.mult).then_inc(s("attn_ready"), 1)
                    pool.drain().then_inc(s("o_nat_free"), 1)

            runs(iteration, pool)

        @block.scalar
        def _(act):
            for name in ("seq_T0_taken", "seq_T1_taken", "scores0_free", "scores1_free", "o_bank_free", "bank5_free",
                         "bank6_free", "bank7_free"):
                act.sem_inc(s(name), 1)
            act.wait_ge(s("clear_act"), 1)
            act.sem_inc(s("clear_act"), -1)
            for n in range(3):
                for half in range(2):
                    act.wait_ge(s("w_T_ready"), 1)
                    act.sem_inc(s("w_T_ready"), -1)
                    src = bank16[half][:, :].rearrange("p (k c) -> p k c", c=P)
                    if n < 2:
                        for dk in range(KL):
                            dst = wgvT[:, dk, HID * n + 512 * half:HID * n + 512 * (half + 1)]
                            act.activation(dst.rearrange("p (k c) -> p k c", c=P), src[:, 4 * dk:4 * dk + 4, :], ACT.Copy)
                    else:
                        dst = woT[:, 4 * half:4 * half + 4, :].rearrange("p k (o c) -> p (k o) c", c=P)
                        act.activation(dst, src, ACT.Copy)
                    act.drain().then_inc(s("w_T_taken"), 1)
            act.wait_ge(s("small_T_ready"), 1)
            act.sem_inc(s("small_T_ready"), -1)
            act.activation(wqkvT[:].rearrange("p n c -> p (n c)"), banks[2][:, 0:3 * P], ACT.Copy)
            for dk in range(KL):
                act.activation(wcT[:, dk, :], banks[3 + dk][:], ACT.Copy)
            act.activation(wduT[0:GD, :], banks[5][0:GD, :], ACT.Copy)
            act.drain().then_inc(s("small_T_taken"), 1)
            with act.Fori(0, B // 2) as i:
                for k in range(2):
                    act.wait_ge(s(f"seq_T{k}_ready"), 1)
                    act.sem_inc(s(f"seq_T{k}_ready"), -1)
                    src = banks[6 + k][:].rearrange("p (w s c) -> p w s c", w=2, c=C)
                    act.activation(cT[:, :, 2 * i + k, :], src[:, 0], ACT.Copy)
                    act.activation(qT[:, :, 2 * i + k, :], src[:, 1], ACT.Copy)
                    act.drain().then_inc(s(f"seq_T{k}_taken"), 1)
            act.sem_inc(s("seq_all_ready"), 1)
            act.sem_inc(s("seq_all_dve"), 1)

            def exps(first, last):
                for n in range(first, last):
                    act.wait_ge(s(f"scores{n % 2}_ready"), 1)
                    act.sem_inc(s(f"scores{n % 2}_ready"), -1)
                    act.wait_ge(s("probs_free"), 1)
                    act.sem_inc(s("probs_free"), -1)
                    act.activation(probs[n % 8][:], SC[n % 2][:], ACT.Exp).then_inc(s(f"scores{n % 2}_free"), 1)

            def collect(q):
                act.wait_ge(s("o_bank_ready"), 1)
                act.sem_inc(s("o_bank_ready"), -1)
                if q == 0:
                    act.wait_ge(s("o_quad_free"), 1)
                    act.sem_inc(s("o_quad_free"), -1)
                act.activation(o_quad[:, q, :], O[:, 0:L], ACT.Copy).then_inc(s("o_bank_free"), 1)

            def iteration(d, p, on):
                ffn0, probs_on, maxima, ffn1 = FFN0 in on, PROBS in on, MAXIMA in on, FFN1 in on
                if ffn1:
                    act.wait_ge(s("xn3_ready"), 1)
                    act.sem_inc(s("xn3_ready"), -1)
                    act.activation(xn3_sq[:], xn3[:], ACT.Square, accum_out=col(SQ))
                    act.drain().then_inc(s("sq_ready"), 1)
                    act.wait_ge(s("bank7_filled"), 1)
                    act.sem_inc(s("bank7_filled"), -1)
                    act.activation(xrT[:].rearrange("p k t -> p (k t)"), X7[:, 0:L], ACT.Copy).then_inc(s("bank7_copied"), 1)
                if probs_on:
                    exps(0, 2)
                if ffn1:
                    act.wait_ge(s("bank7_filled"), 1)
                    act.sem_inc(s("bank7_filled"), -1)
                    act.activation(logits[:], X7[:], ACT.Copy).then_inc(s("logits_ready"), 1)
                if probs_on:
                    exps(2, 6)
                if ffn0:
                    act.wait_ge(s("banks56_filled"), 1)
                    act.sem_inc(s("banks56_filled"), -1)
                    act.activation(xqT[:].rearrange("p k t -> p (k t)"), X6[:, 0:L], ACT.Copy, bias=-MAGIC).then_inc(
                        s("banks56_copied"), 1)
                    act.wait_ge(s("banks56_filled"), 1)
                    act.sem_inc(s("banks56_filled"), -1)
                    act.activation(s6T[:], bank16[5][:, 0:P], ACT.Copy).then_inc(s("banks56_copied"), 1)
                if probs_on:
                    collect(0)
                    exps(6, 8)
                if ffn1:
                    act.wait_ge(s("nb_ready"), 1)
                    act.sem_inc(s("nb_ready"), -1)
                    act.drain()
                    act.activation(e_all[:], logits[:], ACT.Exp, bias=col(NB), scale=temp_scale[:, 0:1]).then_inc(
                        s("e_ready"), 1)
                if probs_on:
                    exps(8, 10)
                    collect(1)
                if ffn0:
                    tanh_gate(0)
                if probs_on:
                    exps(10, 14)
                    collect(2)
                if ffn0:
                    tanh_gate(1)
                if probs_on:
                    exps(14, 16)
                    collect(3)
                    act.drain()
                    for jj in range(4):
                        act.dma_start(scr_o[1 - p, 4 * jj:4 * jj + 4].rearrange("q d l -> d q l"),
                                      o_quad[32 * jj:32 * jj + HD + 1, :, :]).then_inc(s("o_written"), 16)
                if ffn0:
                    act.wait_ge(s("sh_ready"), 1)
                    act.sem_inc(s("sh_ready"), -1)
                    act.activation(hid[:], hid[:], ACT.Copy, scale=col(SH), bias=MAGIC).then_inc(s("hq_ready"), 1)
                    for half, bank in enumerate((X5, X6)):
                        act.wait_ge(s("banks56_filled"), 1)
                        act.sem_inc(s("banks56_filled"), -1)
                        act.activation(hqT[:, 4 * half:4 * half + 4, :].rearrange("p k t -> p (k t)"), bank[:], ACT.Copy,
                                       bias=-MAGIC).then_inc(s("banks56_copied"), 1)
                if ffn1:
                    act.wait_ge(s("bank7_filled"), 1)
                    act.sem_inc(s("bank7_filled"), -1)
                    act.activation(wT[:].rearrange("p k t -> p (k t)"), X7[:], ACT.Copy).then_inc(s("bank7_copied"), 1)
                    act.wait_ge(s("bank7_filled"), 1)
                    act.sem_inc(s("bank7_filled"), -1)
                    act.activation(exprT[:], X7[:, 0:P], ACT.Copy).then_inc(s("bank7_copied"), 1)
                    act.wait_ge(s("bank7_filled"), 1)
                    act.sem_inc(s("bank7_filled"), -1)
                    act.wait_ge(s("rs_ready"), 1)
                    act.sem_inc(s("rs_ready"), -1)
                    act.activation(down[:], X7[:, 0:L], ACT.Tanh, scale=col(RS)).then_inc(s("down_ready"), 1)
                if maxima:
                    act.wait_ge(s("bank7_filled"), 1)
                    act.sem_inc(s("bank7_filled"), -1)
                    act.activation(nm_rows[:], bank16[7][0:6 * GRP, 0:L], ACT.Copy).then_inc(s("bank7_free"), 1)
                    act.drain()
                    act.dma_start(QS[p][ROW_MAX:ROW_MAX + 6, :, :], nm_rows[:]).then_inc(s("max_rows_loaded"), 16)
                if ffn1:
                    act.wait_ge(s("res_ready"), 1)
                    act.sem_inc(s("res_ready"), -1)
                    act.dma_start(out[d], res[:]).then_inc(s("res_out"), 16)

            def tanh_gate(half):
                act.wait_ge(s("banks56_filled"), 1)
                act.sem_inc(s("banks56_filled"), -1)
                act.wait_ge(s("tanh_free"), 1)
                act.sem_inc(s("tanh_free"), -1)
                if half == 0:
                    act.wait_ge(s("sg_ready"), 1)
                    act.sem_inc(s("sg_ready"), -1)
                act.activation(tanh_g[:], X5[:], ACT.Tanh, scale=col(SG)).then_inc(s("tanh_ready"), 1)

            runs(iteration, act)
            act.wait_ge(s("res_out"), 16)
            act.sem_inc(s("res_out"), -16)

        @block.tensor
        def _(pe):
            for name in ("ctx_in0_free", "ctx_in1_free", "xn_in0_free", "xn_in1_free", "toep0_free", "toep1_free", "kv0_free",
                         "kv1_free", "y_in_free", "ctx_m_free"):
                pe.sem_inc(s(name), 1)
            for name in ("qs_free", "v_aug_free"):
                pe.sem_inc(s(name), 2)
            pe.sem_inc(s("probs_free"), 8)
            pe.wait_ge(s("ident_ready"), 1)
            pe.sem_inc(s("ident_ready"), -1)
            for n in range(3):
                pe.wait_ge(s("w_int_ready"), 1)
                pe.sem_inc(s("w_int_ready"), -1)
                for half in range(2):
                    if n > 0:
                        pe.wait_ge(s("w_T_taken"), 1)
                        pe.sem_inc(s("w_T_taken"), -1)
                    for m in range(8):
                        if n < 2:
                            src = w_int[:, (4 * half + m % 4) * L + (m // 4) * P:(4 * half + m % 4) * L + (m // 4 + 1) * P]
                        else:
                            at = (m % 2) * HID + (4 * half + m // 2) * P
                            src = w_int[:, at:at + P]
                        mm = pe.transpose(bank16[half][:, m * P:(m + 1) * P], src, ident16[:])
                    mm.then_inc(s("w_T_ready"), 1)
                pe.drain().then_inc(s("w_int_free"), 1)
            pe.wait_ge(s("w_T_taken"), 2)
            pe.sem_inc(s("w_T_taken"), -2)
            pe.wait_ge(s("small_in"), 16 * 6)
            pe.sem_inc(s("small_in"), -(16 * 6))
            for n in range(3):
                pe.transpose(banks[2][:, n * P:(n + 1) * P], small_raw[:, n, :], ident[:])
            for dk in range(KL):
                for k in range(KG):
                    pe.transpose(banks[3 + dk][:, k * P:(k + 1) * P], wc_raw[:, k, dk * P:(dk + 1) * P], ident[:])
            for n in range(2):
                for k in range(2):
                    mm = pe.transpose(banks[5][0:GD, (2 * n + k) * P:(2 * n + k + 1) * P], wdu_raw[:, n, k, :], ident[:])
            mm.then_inc(s("small_T_ready"), 1)
            with pe.Fori(0, B // 2) as i:
                for k in range(2):
                    pe.wait_ge(s(f"seq_T{k}_taken"), 1)
                    pe.sem_inc(s(f"seq_T{k}_taken"), -1)
                    pe.wait_ge(s(f"ctx_in{k}_loaded"), 16)
                    pe.sem_inc(s(f"ctx_in{k}_loaded"), -16)
                    for sh in range(KL):
                        pe.transpose(banks[6 + k][:, sh * P:(sh + 1) * P], ctx_in[k][:, sh * P:(sh + 1) * P], ident[:])
                    pe.wait_ge(s(f"xn_in{k}_ready"), 1)
                    pe.sem_inc(s(f"xn_in{k}_ready"), -1)
                    for sh in range(KL):
                        mm = pe.transpose(banks[6 + k][:, (2 + sh) * P:(3 + sh) * P], xn_in[k][:, sh * P:(sh + 1) * P], ident[:])
                    mm.then_inc(s(f"seq_T{k}_ready"), 1)
                    pe.drain().then_inc(s(f"ctx_in{k}_free"), 1)
                    pe.sem_inc(s(f"xn_in{k}_free"), 1)
            for k in range(2):
                pe.wait_ge(s(f"seq_T{k}_taken"), 1)
                pe.sem_inc(s(f"seq_T{k}_taken"), -1)
            pe.wait_ge(s("small_T_taken"), 1)
            pe.sem_inc(s("small_T_taken"), -1)
            with pe.Fori(0, H // 2) as i:
                for k in range(2):
                    pe.wait_ge(s(f"toep{k}_loaded"), 16)
                    pe.sem_inc(s(f"toep{k}_loaded"), -16)
                    pe.wait_ge(s(f"kv{k}_ready"), 1)
                    pe.sem_inc(s(f"kv{k}_ready"), -1)
                    pe.wait_ge(s(f"conv{k}_free"), 1)
                    pe.sem_inc(s(f"conv{k}_free"), -1)
                    rhs = kv[k][:].rearrange("p (s b) j i -> p s (b j i)", b=B)
                    for lh in range(KL):
                        for bh in range(2):
                            cols = slice(512 * bh, 512 * (bh + 1))
                            for sh in range(lh + 1):
                                mm = pe.matmul(banks[4 * k + 2 * lh + bh][:], toep[k][:, (lh - sh) * P:(lh - sh + 1) * P],
                                               rhs[:, sh, cols], start=(sh == 0), stop=(sh == lh))
                    mm.then_inc(s(f"conv{k}_ready"), 1)
                    pe.drain().then_inc(s(f"toep{k}_free"), 1)
                    pe.sem_inc(s(f"kv{k}_free"), 1)
            for k in range(2):
                pe.wait_ge(s(f"conv{k}_free"), 1)
                pe.sem_inc(s(f"conv{k}_free"), -1)
            pe.wait_ge(s("mask_nat_in"), 16)
            pe.sem_inc(s("mask_nat_in"), -16)
            pe.transpose(banks[5][:, 0:KL * B], mask_nat[:], ident[0:KL * B, 0:KL * B]).then_inc(s("mask_T_ready"), 1)
            pe.wait_ge(s("mask_T_taken"), 1)
            pe.sem_inc(s("mask_T_taken"), -1)
            pe.wait_ge(s("b6_ready"), 1)
            pe.sem_inc(s("b6_ready"), -1)
            pe.wait_ge(s("genes_in"), 16)
            pe.sem_inc(s("genes_in"), -16)

            def maxima(p, *ns):
                for h in ns:
                    pe.wait_ge(s(f"max{h % 2}_free"), 1)
                    pe.sem_inc(s(f"max{h % 2}_free"), -1)
                    for th in range(KL):
                        mm = pe.matmul(M[h % 2][:, th * L:(th + 1) * L], QS[p][0:K_MAX, h // 2, th * P:(th + 1) * P],
                                       KS[p][0:K_MAX, h, :], start=True, stop=True)
                    mm.then_inc(s(f"max{h % 2}_ready"), 1)

            def scores(p, *ns):
                for n in ns:
                    h = heads[n]
                    pe.wait_ge(s(f"scores{n % 2}_free"), 1)
                    pe.sem_inc(s(f"scores{n % 2}_free"), -1)
                    for sh in range(KL):
                        mm = pe.matmul(SC[n % 2][:, sh * L:(sh + 1) * L], KS[1 - p][0:K_ALL, h, sh * P:(sh + 1) * P],
                                       QS[1 - p][0:K_ALL, h // 2, :], start=True, stop=True)
                    mm.then_inc(s(f"scores{n % 2}_ready"), 1)

            def values(p, q):
                pe.wait_ge(s("o_bank_free"), 1)
                pe.sem_inc(s("o_bank_free"), -1)
                for sh in range(KL):
                    for jj in range(4):
                        mm = pe.matmul(O[32 * jj:32 * jj + 32, 0:L], v_aug[1 - p][:, sh, heads[4 * q + jj], :],
                                       probs[(4 * q + jj) % 8][:, sh * L:(sh + 1) * L], start=(sh == 0), stop=(sh == 1))
                mm.then_inc(s("o_bank_ready"), 1)
                pe.drain().then_inc(s("probs_free"), 4)

            def gates(half):
                for n, bank in enumerate((X5, X6)):
                    at = HID * n + 512 * half
                    for k in range(KL):
                        pe.matmul(bank[:], xqT[:, k, :], wgvT[:, k, at:at + 512], start=(k == 0), stop=False)
                    mm = pe.matmul(bank[:], s6T[:], b6[:, at:at + 512], start=False, stop=True)
                mm.then_inc(s("banks56_filled"), 1)

            def iteration(d, p, on):
                ffn0, proj, mx, pr, ffn1 = (g in on for g in STAGES)
                if proj:
                    pe.wait_ge(s("ctx_m_ready"), 1)
                    pe.sem_inc(s("ctx_m_ready"), -1)
                    pe.wait_ge(s("xn2_ready"), 1)
                    pe.sem_inc(s("xn2_ready"), -1)
                    pe.wait_ge(s("bank6_free"), 1)
                    pe.sem_inc(s("bank6_free"), -1)
                    pe.matmul(X6[:, L:2 * L], wqkvT[:, 1, :], ctx_m[:], start=True, stop=True)
                    pe.matmul(X6[:, 0:L], wqkvT[:, 0, :], xn2[:], start=True, stop=True).then_inc(s("qk_bank_ready"), 1)
                if ffn0:
                    pe.wait_ge(s("y_in_loaded"), 16)
                    pe.sem_inc(s("y_in_loaded"), -16)
                    pe.wait_ge(s("bank5_free"), 1)
                    pe.sem_inc(s("bank5_free"), -1)
                    for sh in range(KL):
                        mm = pe.transpose(X5[:, sh * P:(sh + 1) * P], y_in[:, sh, :], ident[:])
                    mm.then_inc(s("y_T_ready"), 1)
                    pe.drain().then_inc(s("y_in_free"), 1)
                if mx:
                    pe.wait_ge(s("qs_loaded"), 16 * 5)
                    pe.sem_inc(s("qs_loaded"), -(16 * 5))
                    maxima(p, 0, 1)
                if pr:
                    pe.wait_ge(s("v_aug_ready"), 1)
                    pe.sem_inc(s("v_aug_ready"), -1)
                    pe.wait_ge(s("max_rows_loaded"), 16)
                    pe.sem_inc(s("max_rows_loaded"), -16)
                    scores(p, 0, 1)
                if mx:
                    maxima(p, 2)
                if ffn1:
                    pe.wait_ge(s("xr_ready"), 1)
                    pe.sem_inc(s("xr_ready"), -1)
                    pe.wait_ge(s("bank7_free"), 1)
                    pe.sem_inc(s("bank7_free"), -1)
                    for k in range(KL):
                        mm = pe.transpose(X7[:, k * P:(k + 1) * P], xr[:, k * P:(k + 1) * P], ident[:])
                    mm.then_inc(s("bank7_filled"), 1)
                    pe.wait_ge(s("bank7_copied"), 1)
                    pe.sem_inc(s("bank7_copied"), -1)
                    for k in range(KL):
                        mm = pe.matmul(X7[:], xrT[:, k, :], wcT[:, k, :], start=(k == 0), stop=(k == KL - 1))
                    mm.then_inc(s("bank7_filled"), 1)
                if pr:
                    scores(p, 2, 3)
                if mx:
                    maxima(p, 3)
                if pr:
                    scores(p, 4, 5)
                    values(p, 0)
                if mx:
                    maxima(p, 4)
                if pr:
                    scores(p, 6)
                if ffn0:
                    pe.wait_ge(s("xq_ready"), 1)
                    pe.sem_inc(s("xq_ready"), -1)
                    pe.wait_ge(s("bank6_free"), 1)
                    pe.sem_inc(s("bank6_free"), -1)
                    for k in range(KL):
                        mm = pe.transpose(X6[:, k * P:(k + 1) * P], xq[:, k * P:(k + 1) * P], ident[:])
                    mm.then_inc(s("banks56_filled"), 1)
                    pe.wait_ge(s("s6_ready"), 1)
                    pe.sem_inc(s("s6_ready"), -1)
                    pe.wait_ge(s("bank5_free"), 1)
                    pe.sem_inc(s("bank5_free"), -1)
                    pe.transpose(bank16[5][:, 0:P], s6[:], ident16[:]).then_inc(s("banks56_filled"), 1)
                if pr:
                    scores(p, 7)
                if mx:
                    maxima(p, 5)
                if pr:
                    scores(p, 8, 9)
                    values(p, 1)
                if ffn0:
                    pe.wait_ge(s("banks56_copied"), 1)
                    pe.sem_inc(s("banks56_copied"), -1)
                    pe.wait_ge(s("banks56_copied"), 1)
                    pe.sem_inc(s("banks56_copied"), -1)
                    gates(0)
                if mx:
                    maxima(p, 6)
                if pr:
                    scores(p, 10, 11, 12, 13)
                    values(p, 2)
                if ffn0:
                    pe.wait_ge(s("gate_bank_free"), 1)
                    pe.sem_inc(s("gate_bank_free"), -1)
                    pe.wait_ge(s("val_bank_free"), 1)
                    pe.sem_inc(s("val_bank_free"), -1)
                    gates(1)
                if pr:
                    scores(p, 14, 15)
                    pe.drain().then_inc(s("qs_free"), 1)
                    pe.wait_ge(s("scores0_free"), 1)
                    pe.sem_inc(s("scores0_free"), -1)
                    pe.wait_ge(s("scores1_free"), 1)
                    pe.sem_inc(s("scores1_free"), -1)
                    values(p, 3)
                    pe.sem_inc(s("v_aug_free"), 1)
                    pe.sem_inc(s("scores0_free"), 1)
                    pe.sem_inc(s("scores1_free"), 1)
                if ffn0:
                    pe.wait_ge(s("gate_bank_free"), 1)
                    pe.sem_inc(s("gate_bank_free"), -1)
                    pe.wait_ge(s("val_bank_free"), 1)
                    pe.sem_inc(s("val_bank_free"), -1)
                    pe.wait_ge(s("hq_ready"), 1)
                    pe.sem_inc(s("hq_ready"), -1)
                    for half, bank in enumerate((X5, X6)):
                        for m in range(4):
                            n = 4 * half + m
                            mm = pe.transpose(bank[:, m * P:(m + 1) * P], hid[:, n * P:(n + 1) * P], ident[:])
                        mm.then_inc(s("banks56_filled"), 1)
                if ffn1:
                    pe.wait_ge(s("w_top_ready"), 1)
                    pe.sem_inc(s("w_top_ready"), -1)
                    for k in range(KG):
                        mm = pe.transpose(X7[:, k * P:(k + 1) * P], w_top[:, k * P:(k + 1) * P], ident[:])
                    mm.then_inc(s("bank7_filled"), 1)
                if mx:
                    maxima(p, 7, 8)
                if ffn0:
                    pe.wait_ge(s("banks56_copied"), 2)
                    pe.sem_inc(s("banks56_copied"), -2)
                    pe.sem_inc(s("bank6_free"), 1)
                    for k in range(KH):
                        mm = pe.matmul(X5[:, 0:L], hqT[:, k, :], woT[:, k, :], start=(k == 0), stop=(k == KH - 1))
                    mm.then_inc(s("ffn_ready"), 1)
                if ffn1:
                    pe.wait_ge(s("bank7_copied"), 1)
                    pe.sem_inc(s("bank7_copied"), -1)
                    for k in range(KG):
                        mm = pe.matmul(X7[:, 0:P], genes[:, k, :], wT[:, k, :], start=(k == 0), stop=(k == KG - 1))
                    mm.then_inc(s("bank7_filled"), 1)
                if proj:
                    pe.wait_ge(s("bank6_free"), 1)
                    pe.sem_inc(s("bank6_free"), -1)
                    for sh in range(KL):
                        mm = pe.matmul(X6[:, sh * P:(sh + 1) * P], ctx_m[:, sh * P:(sh + 1) * P], wqkvT[:, 2, :],
                                       start=True, stop=True)
                    mm.then_inc(s("v_bank_ready"), 1)
                    pe.drain().then_inc(s("ctx_m_free"), 1)
                if mx:
                    maxima(p, 9, 10)
                if ffn1:
                    pe.wait_ge(s("bank7_copied"), 1)
                    pe.sem_inc(s("bank7_copied"), -1)
                    pe.matmul(X7[:], exprT[:], wduT[:], start=True, stop=True).then_inc(s("bank7_filled"), 1)
                if mx:
                    maxima(p, 11, 12, 13, 14, 15)
                    pe.wait_ge(s("nm_parts_ready"), 1)
                    pe.sem_inc(s("nm_parts_ready"), -1)
                    pe.wait_ge(s("bank7_free"), 1)
                    pe.sem_inc(s("bank7_free"), -1)
                    for th in range(KL):
                        mm = pe.transpose(bank16[7][0:6 * GRP, th * P:(th + 1) * P],
                                          nm_parts[:, th].rearrange("p j n g -> p (j n g)"), ident16[:])
                    mm.then_inc(s("bank7_filled"), 1)

            runs(iteration, pe)

        @block.vector
        def _(dve):
            for name in ("conv0_free", "conv1_free", "x_b_free", "mask_b_free", "mask32_free", "attn_free", "tanh_free",
                         "max0_free", "max1_free"):
                dve.sem_inc(s(name), 1)
            dve.wait_ge(s("weights_in"), 48)
            dve.sem_inc(s("weights_in"), -48)
            for n in range(3):
                dve.tensor_reduce(abs_sum[:, n:n + 1], w_raw[:, n, :], AX.X, ALU.add, apply_absolute_value=True)
            dve.drain().then_inc(s("abs_sum_ready"), 1)
            for k in range(2):
                dve.sem_inc(s(f"x_in{k}_free"), 1)
            dve.wait_ge(s("gamma_sum_ready"), 1)
            dve.sem_inc(s("gamma_sum_ready"), -1)
            dve.tensor_scalar(gammas[:], gammas[:], 1.0 / (HID * L), 1e-5, ALU.mult, ALU.max)
            dve.drain()
            dve.reciprocal(inv_gammas[:], gammas[:])
            dve.drain().then_inc(s("gammas_ready"), 1)
            for n in range(3):
                dve.tensor_scalar(w_raw[:, n, :], w_raw[:, n, :], inv_gammas[:, n:n + 1], 1.0, ALU.mult, ALU.min)
                dve.drain()
                dve.tensor_scalar(w_raw[:, n, :], w_raw[:, n, :], -1.0, MAGIC, ALU.max, ALU.add)
                dve.drain()
                if n > 0:
                    dve.wait_ge(s("w_int_free"), 1)
                    dve.sem_inc(s("w_int_free"), -1)
                dve.tensor_scalar(w_int[:], w_raw[:, n, :], -MAGIC, None, ALU.add).then_inc(s("w_int_ready"), 1)
            dve.drain().then_inc(s("weights_done"), 1)
            dve.wait_ge(s("vectors_in"), 16 * 7)
            dve.sem_inc(s("vectors_in"), -(16 * 7))
            dve.tensor_scalar(temp_scale[:, 0:1], temp_scale[:, 0:1], 0.1, None, ALU.max)
            dve.drain()
            dve.reciprocal(temp_scale[:, 0:1], temp_scale[:, 0:1])
            with dve.Fori(0, B // 2) as i:
                for k in range(2):
                    dve.wait_ge(s(f"x_in{k}_loaded"), 16)
                    dve.sem_inc(s(f"x_in{k}_loaded"), -16)
                    dve.bn_stats(stat6[:], x_in[k][:])
                    dve.drain().then_inc(s(f"x_in{k}_free"), 1)
                    dve.bn_aggr(stat2[:], stat6[:])
                    dve.drain()
                    dve.tensor_copy(mv_all[:, 2 * i + k, :], stat2[:])
            dve.drain().then_inc(s("var_all_ready"), 1)
            dve.wait_ge(s("rstd_all_ready"), 1)
            dve.sem_inc(s("rstd_all_ready"), -1)
            with dve.Fori(0, B // 2) as i:
                for k in range(2):
                    dve.wait_ge(s(f"x_in{k}_loaded"), 16)
                    dve.sem_inc(s(f"x_in{k}_loaded"), -16)
                    dve.wait_ge(s(f"xn_in{k}_free"), 1)
                    dve.sem_inc(s(f"xn_in{k}_free"), -1)
                    dve.tensor_scalar(xn_in[k][:], x_in[k][:], mv_all[:, 2 * i + k, 0:1], rstd_all[:, bass.ds(2 * i + k, 1)],
                                      ALU.subtract, ALU.mult).then_inc(s(f"xn_in{k}_ready"), 1)
                    dve.drain().then_inc(s(f"x_in{k}_free"), 1)
            dve.wait_ge(s("seq_all_dve"), 1)
            dve.sem_inc(s("seq_all_dve"), -1)
            with dve.Fori(0, H // 2) as i:
                for k in range(2):
                    dve.wait_ge(s(f"conv{k}_ready"), 1)
                    dve.sem_inc(s(f"conv{k}_ready"), -1)
                    q = qT[:].rearrange("p s b c -> p (s b) c")[:, :, bass.ds((2 * i + k) * HD, HD)]
                    n = 2 * k
                    for lh in range(KL):
                        for bh in range(2):
                            r = slice(lh * B + bh * (B // 2), lh * B + (bh + 1) * (B // 2))
                            dve.tensor_tensor(prod[:, r], banks[4 * k + 2 * lh + bh][:].rearrange("p (b j i) -> p b j i", j=HD, i=HD),
                                              q[:, r, :].unsqueeze(2).broadcast_to([P, B // 2, HD, HD]), ALU.mult)
                    dve.drain().then_inc(s(f"conv{k}_free"), 1)
                    dve.tensor_reduce(yT[:].rearrange("p s b c -> p (s b) c")[:, :, bass.ds((2 * i + k) * HD, HD)], prod,
                                      AX.X, ALU.add)
                    dve.drain()
            dve.sem_inc(s("y_all_ready"), 1)
            dve.wait_ge(s("clear_dve"), 1)
            dve.sem_inc(s("clear_dve"), -1)
            dve.wait_ge(s("mask_T_ready"), 1)
            dve.sem_inc(s("mask_T_ready"), -1)
            dve.tensor_copy(mask_cols[:].rearrange("p b k -> p (b k)"), banks[5][:, 0:KL * B])
            dve.drain().then_inc(s("mask_T_taken"), 1)

            def statistics(src, mean, done):
                dve.drain()
                dve.bn_stats(st6[:], src)
                dve.drain()
                dve.bn_aggr(col(mean, 2), st6[:]).then_inc(s(done), 1)

            def maxima(*ns):
                for h in ns:
                    dve.wait_ge(s(f"max{h % 2}_ready"), 1)
                    dve.sem_inc(s(f"max{h % 2}_ready"), -1)
                    dve.tensor_reduce(neg_max[:, :, h:h + 1], M[h % 2][:].rearrange("p (t s) -> p t s", s=L), AX.X,
                                      ALU.max, negate=True).then_inc(s(f"max{h % 2}_free"), 1)

            def topk_round():
                dve.drain()
                dve.match_replace(left[:], best[:], left[:], GONE)
                dve.drain()
                dve.max(best[:], left[:])

            def gate_times_value(half):
                dve.wait_ge(s("tanh_ready"), 1)
                dve.sem_inc(s("tanh_ready"), -1)
                dve.scalar_tensor_tensor(u_g[:], tanh_g[:], 1.0, X5[:], ALU.add, ALU.mult).then_inc(s("gate_bank_free"), 1)
                dve.drain().then_inc(s("tanh_free"), 1)
                dve.tensor_tensor(hid[:, 512 * half:512 * (half + 1)], u_g[:], X6[:], ALU.mult).then_inc(
                    s("val_bank_free"), 1)

            def iteration(d, p, on):
                ffn0, proj, mx, pr, ffn1 = (g in on for g in STAGES)
                if ffn1:
                    dve.wait_ge(s("attn_ready"), 1)
                    dve.sem_inc(s("attn_ready"), -1)
                    dve.drain()
                    dve.tensor_tensor(x3[:].rearrange("p (k l) -> p k l", l=P), x2_all[:, :, d + FFN1, :],
                                      attn[:].rearrange("p (k l) -> p k l", l=P), ALU.add).then_inc(s("attn_free"), 1)
                    statistics(x3[:], MEAN3, "var_ready")
                if proj:
                    dve.wait_ge(s("qk_bank_ready"), 1)
                    dve.sem_inc(s("qk_bank_ready"), -1)
                    dve.scalar_tensor_tensor(qk[:, 1, :], mask_b[:], bqk[:, 1:2], X6[:, L:2 * L], ALU.mult, ALU.add)
                    dve.scalar_tensor_tensor(qk[:, 0, :], X6[:, 0:L], bqk[:, 0:1], mask_q[:], ALU.add, ALU.mult
                                             ).then_inc(s("qk_ready"), 1)
                    dve.drain().then_inc(s("bank6_free"), 1)
                    dve.sem_inc(s("mask_b_free"), 1)
                if ffn1:
                    dve.wait_ge(s("rstd_ready"), 1)
                    dve.sem_inc(s("rstd_ready"), -1)
                    dve.tensor_scalar(xn3[:], x3[:], col(MEAN3), col(RSTD3), ALU.subtract, ALU.mult).then_inc(
                        s("xn3_ready"), 1)
                if mx:
                    maxima(0, 1)
                if ffn0:
                    dve.wait_ge(s("y_T_ready"), 1)
                    dve.sem_inc(s("y_T_ready"), -1)
                    dve.wait_ge(s("x_b_loaded"), 16)
                    dve.sem_inc(s("x_b_loaded"), -16)
                    dve.tensor_tensor(x1[:], X5[:, 0:L], x_b[:], ALU.add).then_inc(s("bank5_free"), 1)
                    dve.drain().then_inc(s("x_b_free"), 1)
                    statistics(x1[:], MEAN1, "var_ready")
                if ffn1:
                    dve.wait_ge(s("rr_ready"), 1)
                    dve.sem_inc(s("rr_ready"), -1)
                    dve.scalar_tensor_tensor(xr[:], xn3[:], col(RR), norm_w[:], ALU.mult, ALU.mult).then_inc(s("xr_ready"), 1)
                if mx:
                    maxima(2)
                if ffn0:
                    dve.wait_ge(s("rstd_ready"), 1)
                    dve.sem_inc(s("rstd_ready"), -1)
                    dve.tensor_scalar(xq[:], x1[:], col(MEAN1), col(RSTD1), ALU.subtract, ALU.mult)
                    dve.drain()
                    dve.tensor_reduce(col(QX), xq[:], AX.X, ALU.max, apply_absolute_value=True)
                    dve.drain()
                    dve.tensor_scalar(col(QX), col(QX), 1e-5, 1.0 / 127.0, ALU.max, ALU.mult)
                    dve.drain()
                    dve.reciprocal(col(SX), col(QX)).then_inc(s("sx_ready"), 1)
                    dve.tensor_scalar(col(SG), col(QX), gammas[:, 0:1], 0.5, ALU.mult, ALU.mult)
                    dve.tensor_scalar(col(KAPPA), col(QX), gammas[:, 1:2], None, ALU.mult)
                    dve.drain().then_inc(s("sg_ready"), 1)
                    dve.tensor_scalar(xq[:], xq[:], col(SX), MAGIC, ALU.mult, ALU.add).then_inc(s("xq_ready"), 1)
                    dve.tensor_tensor(col(KAPPA), col(KAPPA), col(SG), ALU.mult)
                if mx:
                    maxima(3, 4)
                if ffn1:
                    dve.wait_ge(s("logits_ready"), 1)
                    dve.sem_inc(s("logits_ready"), -1)
                    dve.max(best[:], logits[:])
                    dve.drain()
                    dve.tensor_scalar(col(NB), best[:, 0:1], temp_scale[:, 0:1], -1.0, ALU.mult, ALU.mult).then_inc(
                        s("nb_ready"), 1)
                    dve.match_replace(left[:], best[:], logits[:], GONE)
                    dve.drain()
                    dve.max(best[:], left[:])
                if ffn0:
                    gate_times_value(0)
                if ffn1:
                    topk_round()
                if ffn0:
                    dve.drain()
                    gate_times_value(1)
                    dve.drain()
                    dve.tensor_reduce(col(QH), hid[:], AX.X, ALU.max, apply_absolute_value=True)
                    dve.drain()
                    dve.tensor_scalar(col(QH), col(QH), col(KAPPA), 1e-5, ALU.mult, ALU.max)
                    dve.drain()
                    dve.reciprocal(col(RH), col(QH))
                    dve.tensor_scalar(col(SO), col(QH), gammas[:, 2:3], 1.0 / 127.0, ALU.mult, ALU.mult)
                    dve.drain()
                    dve.tensor_scalar(col(SH), col(RH), col(KAPPA), 127.0, ALU.mult, ALU.mult).then_inc(s("sh_ready"), 1)
                if ffn1:
                    topk_round()
                    dve.drain()
                    dve.match_replace(left[:], best[:], left[:], GONE)
                    dve.drain()
                    dve.wait_ge(s("e_ready"), 1)
                    dve.sem_inc(s("e_ready"), -1)
                    dve.scalar_tensor_tensor(w_top[:], left[:], GONE, e_all[:], ALU.is_equal, ALU.mult,
                                             accum_out=col(WS))
                    dve.drain().then_inc(s("w_top_ready"), 1)
                    dve.reciprocal(col(RS), col(WS)).then_inc(s("rs_ready"), 1)
                if mx:
                    maxima(5, 6, 7, 8, 9, 10)
                if pr:
                    dve.wait_ge(s("den_loaded"), 32)
                    dve.sem_inc(s("den_loaded"), -32)
                    dve.reciprocal(den32[:], den32[:])
                    dve.drain()
                    dve.tensor_tensor(den32[:], den32[:], mask32[:], ALU.mult).then_inc(s("den_ready"), 1)
                    dve.drain().then_inc(s("mask32_free"), 1)
                if mx:
                    maxima(11, 12, 13, 14, 15)
                    dve.drain().then_inc(s("neg_max_ready"), 1)
                if ffn0:
                    b = d + FFN0
                    dve.wait_ge(s("ffn_ready"), 1)
                    dve.sem_inc(s("ffn_ready"), -1)
                    dve.wait_ge(s("x1b_ready"), 1)
                    dve.sem_inc(s("x1b_ready"), -1)
                    x2 = x2_all[:, :, b, :]
                    dve.scalar_tensor_tensor(x2, X5[:, 0:L].rearrange("p (k l) -> p k l", l=P), col(SO),
                                             x1b[:].rearrange("p (k l) -> p k l", l=P), ALU.mult, ALU.add).then_inc(
                                                 s("bank5_free"), 1)
                    statistics(x2, MEAN2, "var_ready")
                if proj:
                    dve.wait_ge(s("v_bank_ready"), 1)
                    dve.sem_inc(s("v_bank_ready"), -1)
                    dve.wait_ge(s("v_aug_free"), 1)
                    dve.sem_inc(s("v_aug_free"), -1)
                    for sh in range(KL):
                        mm = dve.scalar_tensor_tensor(v_aug[1 - p][:, sh, :, 0:HD], bv[:].rearrange("p (h d) -> p h d", d=HD),
                                                      mask_cols[:, d + PROJ, sh:sh + 1],
                                                      X6[:, sh * P:(sh + 1) * P].rearrange("p (h d) -> p h d", d=HD),
                                                      ALU.mult, ALU.add)
                    mm.then_inc(s("bank6_free"), 1)
                    dve.drain().then_inc(s("v_aug_ready"), 1)
                if ffn1:
                    dve.drain()
                    dve.tensor_scalar(col(RSS), col(RS), temp_scale[:, 1:2], None, ALU.mult)
                    dve.wait_ge(s("down_ready"), 1)
                    dve.sem_inc(s("down_ready"), -1)
                    dve.tensor_tensor(dx[:], down[:], xr[:], ALU.mult)
                    dve.drain()
                    dve.scalar_tensor_tensor(dx[:], X7[:, L:2 * L], col(RSS), dx[:], ALU.mult, ALU.mult).then_inc(
                        s("bank7_free"), 1)
                    dve.drain()
                    dve.wait_ge(s("res_out"), 16)
                    dve.sem_inc(s("res_out"), -16)
                    dve.tensor_tensor(res[:], dx[:], x3[:], ALU.add).then_inc(s("res_ready"), 1)
                if ffn0:
                    dve.wait_ge(s("rstd_ready"), 1)
                    dve.sem_inc(s("rstd_ready"), -1)
                    dve.tensor_scalar(xn2[:].rearrange("p (k l) -> p k l", l=P), x2, col(MEAN2), col(RSTD2), ALU.subtract,
                                      ALU.mult).then_inc(s("xn2_ready"), 1)

            dve.sem_inc(s("res_out"), 16)
            runs(iteration, dve)


_IN = dict(x="x", ctx_2048="ctx", mask_Bx1x2048_fk1="mask", L0_xattn_ssm_kernel="ssm", L0_xattn_D="d",
           L0_ffn_gate_w="gate_w", L0_ffn_gate_b="gate_b", L0_ffn_val_w="val_w", L0_ffn_val_b="val_b",
           L0_ffn_out_w="out_w", L0_ffn_out_b="out_b", L1_xattn_Wq="wq", L1_xattn_bq="bq", L1_xattn_Wk="wk",
           L1_xattn_bk="bk", L1_xattn_Wv="wv", L1_xattn_bv="bv", L1_ffn_Wc="wc", L1_ffn_temperature="temperature",
           L1_ffn_genes="genes", L1_ffn_Wd="wd", L1_ffn_Wu="wu", L1_ffn_norm_w="norm_w", L1_ffn_scale="scale")


def kernel(**inputs):
    import numpy as np
    import concourse.bacc as bacc
    from concourse.bass_utils import run_bass_kernel_spmd

    nc = bacc.Bacc("TRN2", target_bir_lowering=False, num_devices=1)
    arrays, aps = {}, {}
    for name, short in _IN.items():
        v = np.ascontiguousarray(inputs[name])
        if v.ndim == 0:
            v = v.reshape(1)
        if short == "ssm":
            v = np.concatenate([np.zeros((v.shape[0], P), v.dtype), v], axis=1)
        arrays["in_" + short] = v
        aps[short] = nc.dram_tensor("in_" + short, v.shape, mybir.dt.from_np(v.dtype), kind="ExternalInput").ap()
    shape = inputs["x"].shape
    out = nc.dram_tensor("out_x", shape, F32, kind="ExternalOutput").ap()
    build(nc, aps, out)
    r = run_bass_kernel_spmd(nc, [arrays], core_ids=[0])
    return r.results[0]["out_x"]
```

```python
from contextlib import ExitStack

import concourse.bass as bass
from concourse import mybir

F32 = mybir.dt.float32
BF16 = mybir.dt.bfloat16
U32 = mybir.dt.uint32
ALU = mybir.AluOpType
ACT = mybir.ActivationFunctionType
AX = mybir.AxisListType

P = 128
MAGIC = 12582912.0
LN_EPS = 1e-5
RMS_EPS = 1.1920928955078125e-07
NEG = 1000000.0
GONE = -3.0e38
TOPK = 32


def split3(eng, whole, rest, parts):
    eng.tensor_copy(parts[0], whole)
    eng.drain()
    eng.tensor_tensor(rest, whole, parts[0], ALU.subtract)
    eng.drain()
    eng.tensor_copy(parts[1], rest)
    eng.drain()
    eng.tensor_tensor(parts[2], rest, parts[1], ALU.subtract)


def build(nc, a, out):
    B, C, L = a["x"].shape
    H, HD = a["ssm"].shape[0], C // a["ssm"].shape[0]
    HID = a["gate_w"].shape[0]
    G, GD = a["genes"].shape
    KL, KH, KG = L // P, HID // P, G // P
    QK_SCALE = 1.0 / float(HD) ** 0.5
    TERM_Q, TERM_K = (0, 0, 0, 1, 1, 2), (0, 1, 2, 0, 1, 0)
    NT = len(TERM_Q)
    ROWS, GRP = 2 * HD * NT, H // 2
    ROW_MASK, ROW_MAX = ROWS, ROWS + NT
    K_MAX, K_ALL = ROWS + NT, ROWS + NT + 6
    assert C == P and L == 2 * P and HD == 8 and K_ALL <= P

    scr_toep = nc.dram_tensor("scr_toep", [H, P + L], F32, kind="Internal").ap()
    scr_toeps = nc.dram_tensor("scr_toeps", [H, P, L], F32, kind="Internal").ap()
    scr_q = nc.dram_tensor("scr_q", [2, P, NT, L], BF16, kind="Internal").ap()
    scr_k = nc.dram_tensor("scr_k", [2, P, NT, L], BF16, kind="Internal").ap()
    scr_mask = nc.dram_tensor("scr_mask", [B, 2, NT, L], BF16, kind="Internal").ap()
    scr_o = nc.dram_tensor("scr_o", [2, H, HD + 1, L], F32, kind="Internal").ap()
    scr_r = nc.dram_tensor("scr_r", [2, H, L], F32, kind="Internal").ap()

    with ExitStack() as ctx:
        def sb(name, shape, dt=F32):
            return ctx.enter_context(nc.sbuf_tensor(name, shape, dt))

        banks = [ctx.enter_context(nc.psum_tensor(f"bank{i}", [P, 512], F32)) for i in range(8)]

        ident = sb("ident", [P, P])
        ident16 = sb("ident16", [P, P], BF16)
        half_neg = sb("half_neg", [P, 16])
        wgvT = sb("wgvT", [P, KL, 2 * HID], BF16)
        woT = sb("woT", [P, KH, L], BF16)
        wqkvT = sb("wqkvT", [P, 3, P])
        wcT = sb("wcT", [P, KL, G])
        wduT = sb("wduT", [P, 2 * L])
        genes = sb("genes", [P, KG, P])
        b6 = sb("b6", [P, 2 * HID], BF16)
        gammas = sb("gammas", [P, 3])
        inv_gammas = sb("inv_gammas", [P, 3])
        out_b = sb("out_b", [P, L])
        norm_w = sb("norm_w", [P, L])
        bv = sb("bv", [P, C])
        bqk = sb("bqk", [P, 2])
        temp_scale = sb("temp_scale", [P, 2])
        mask_cols = sb("mask_cols", [P, B, KL])
        yT = sb("yT", [P, KL, B, C])

        w_raw = sb("w_raw", [P, 3, KH * L])
        w_int = [sb(f"w_int{n}", [P, KH * L], BF16) for n in range(3)]
        small_raw = sb("small_raw", [P, 3, P])
        wc_raw = sb("wc_raw", [P, KG, L])
        wdu_raw = sb("wdu_raw", [P, 2, 2, GD])
        bias_nat = sb("bias_nat", [16, 2, HID // 16])
        bias_parts = sb("bias_parts", [16, 3, 2, HID // 16], BF16)
        toep_row = sb("toep_row", [H, P + L])
        d_col = sb("d_col", [H, 1])
        mask_nat = sb("mask_nat", [2 * B, P])
        mask_rows = sb("mask_rows", [B, L])
        aug = sb("aug", [B, 2, L])
        aug_rest = sb("aug_rest", [B, 2, L])
        aug_parts = sb("aug_parts", [B, 2, 3, L], BF16)
        abs_sum = sb("abs_sum", [P, 3])
        one_rows = sb("one_rows", [6, H, L], BF16)
        stat6_all = sb("stat6_all", [P, B, 6])
        mv_all = sb("mv_all", [P, B, 2])
        rstd_all = sb("rstd_all", [P, B])
        cT = sb("cT", [P, KL, B, C])
        qT = sb("qT", [P, KL, B, C])
        toep = [sb(f"toep{k}", [P, L]) for k in range(2)]
        kv = [sb(f"kv{k}", [P, KL * B, HD, HD]) for k in range(2)]
        x_all = yT[:].rearrange("p s b c -> p (s b c)").rearrange("p (b l) -> p b l", l=L)
        ctx_all = [kv[k][:].rearrange("p s j i -> p (s j i)").rearrange("p (b l) -> p b l", l=L) for k in range(2)]
        prod = w_raw[:].rearrange("p a n -> p (a n)")[:, 0:KL * B * HD * HD].rearrange(
            "p (s j i) -> p s j i", j=HD, i=HD)

        spare = {"w_raw": w_raw[:].rearrange("p a n -> p (a n)"), "cT": cT[:].rearrange("p s b c -> p (s b c)"),
                 "qT": qT[:].rearrange("p s b c -> p (s b c)"),
                 "kv0": kv[0][:].rearrange("p s j i -> p (s j i)"), "kv1": kv[1][:].rearrange("p s j i -> p (s j i)")}
        used = dict.fromkeys(spare, 0)

        def inside(tile, shape, dt=F32):
            n = 1
            for m in shape[1:]:
                n *= m
            words = n if dt == F32 else n // 2
            view = spare[tile][:, used[tile]:used[tile] + words]
            used[tile] += words
            assert used[tile] <= spare[tile].shape[1]
            view = view if dt == F32 else view.bitcast(dt)
            names = "abc"[:len(shape) - 1]
            if len(names) == 1:
                return view
            return view.rearrange(f"p ({' '.join(names)}) -> p {' '.join(names)}", **dict(zip(names, shape[1:])))

        x_b = sb("x_b", [P, L])
        y_in = sb("y_in", [P, KL, P])
        x1 = [inside("qT", [P, L]), sb("x1_odd", [P, L])]
        x1b = [inside("qT", [P, L]), sb("x1b_odd", [P, L])]
        xq = [inside("qT", [P, L]), sb("xq_odd", [P, L])]
        xqT = inside("qT", [P, KL, P], BF16)
        st6 = sb("st6", [P, 3, 6])
        st = sb("st", [P, 26])
        s6 = [sb(f"s6_{k}", [P, P], BF16) for k in range(2)]
        s6T = inside("qT", [P, P], BF16)
        tanh_g = inside("qT", [P, 512])
        hid = inside("w_raw", [P, HID])
        hqT = inside("w_raw", [P, KH, P], BF16)
        xn2 = inside("qT", [P, L])
        xn1 = sb("xn1", [P, L])
        x2 = sb("x2", [P, L])
        ctx_b = sb("ctx_b", [P, L])
        mask_b = sb("mask_b", [P, L])
        mask_q = sb("mask_q", [P, L])
        ctx_m = sb("ctx_m", [P, L])
        qk = inside("kv1", [P, 2, L])
        qk_rest = inside("kv1", [P, 2, L])
        qk_parts = inside("kv1", [P, 3, 2, L], BF16)
        v_aug = [sb(f"v_aug{k}", [P, KL, H, 32]) for k in range(2)]
        QS = [inside("w_raw", [P, GRP, L], BF16) for k in range(2)]
        KS = [sb(f"KS{k}", [P, H, L], BF16) for k in range(2)]
        neg_max = sb("neg_max", [P, KL, H])
        nm_rest = sb("nm_rest", [P, KL, H])
        nm_parts = sb("nm_parts", [P, KL, 2, 3, GRP], BF16)
        nm_rows = sb("nm_rows", [6 * GRP, L], BF16)
        probs = [inside("cT", [P, L * KL]) for k in range(8)]
        o_quad = inside("kv0", [P, 4, L])
        o_nat = inside("kv0", [P, L])
        o_den = inside("kv0", [P, L])
        attn = inside("kv0", [P, L])
        den32 = sb("den32", [P, 32])
        mask32_all = sb("mask32_all", [P, B, 32])
        x3 = [inside("qT", [P, L]), sb("x3_odd", [P, L])]
        xn3 = inside("qT", [P, L])
        xn3_sq = inside("w_raw", [P, L])
        xr = [inside("qT", [P, L]), sb("xr_odd", [P, L])]
        xrT = inside("kv0", [P, KL, P])
        logits = [inside("w_raw", [P, G]), sb("logits_odd", [P, G])]
        left = inside("w_raw", [P, G])
        best = sb("best", [P, 8])
        e_all = inside("w_raw", [P, G])
        w_top = inside("qT", [P, G])
        wT = inside("w_raw", [P, KG, P])
        exprT = inside("qT", [P, P])
        down = inside("kv1", [P, L])
        dx = inside("qT", [P, L])
        dxu = sb("dxu", [P, L])
        xw = sb("xw", [P, L])
        res = sb("res", [P, L])

        made = {}

        def s(name):
            if name not in made:
                made[name] = ctx.enter_context(nc.semaphore(name))
            return made[name]

        (MEAN1, VAR1, RSTD1, MEAN2, VAR2, RSTD2, MEAN3, VAR3, RSTD3, QX, SX, QH, RH, SH, SO, SQ, RR, NB, WS, RS,
         RSS, R0) = range(22)
        SG, KAPPA = 22, 24

        def col(n, m=1):
            return st[:, n:n + m]

        bank16 = [b[:].bitcast(BF16) for b in banks]
        M, SC, O, X5, X6, X7 = banks[0:2], banks[2:4], banks[4], banks[5], banks[6], banks[7]
        x2_all = yT

        LEAD = 6
        assert B == 16

        heads = [4 * jj + q for q in range(4) for jj in range(4)]

        block = ctx.enter_context(nc.Block())

        @block.sync
        def _(sp):
            sp.sem_inc(s("qk_parts_free"), 1)
            sp.sem_inc(s("o_quad_free"), 1)
            sp.dma_start(toep_row[:], a["ssm"]).then_inc(s("toep_row_in"), 16)
            sp.dma_start(d_col[:], a["d"].rearrange("(h o) -> h o", o=1)).then_inc(s("toep_row_in"), 16)
            halves = (slice(0, B // 2), slice(B // 2, B))
            sp.dma_start(x_all[:, halves[0], :], a["x"][halves[0]].rearrange("b c l -> c b l")).then_inc(s("x_half0_in"), 16)
            sp.dma_start(x_all[:, halves[1], :], a["x"][halves[1]].rearrange("b c l -> c b l")).then_inc(s("x_half1_in"), 16)
            sp.dma_start(w_raw[:, 0, :].rearrange("p (k d) -> p k d", d=L),
                         a["gate_w"].rearrange("(k p) d -> p k d", p=P)).then_inc(s("gate_w_in"), 16)
            sp.dma_start(mask_rows[:], a["mask"].rearrange("b o l -> (b o) l")).then_inc(s("mask_rows_in"), 16)
            sp.dma_start(w_raw[:, 1, :].rearrange("p (k d) -> p k d", d=L),
                         a["val_w"].rearrange("(k p) d -> p k d", p=P)).then_inc(s("val_w_in"), 16)
            for n, b in enumerate((a["gate_b"], a["val_b"])):
                sp.dma_start(bias_nat[:, n, :], b.rearrange("(p n) -> p n", p=16)).then_inc(s("bias_in"), 16)
            sp.dma_start(w_raw[:, 2, :].rearrange("p (k d) -> p k d", d=HID),
                         a["out_w"].rearrange("(k p) d -> p k d", p=P)).then_inc(s("out_w_in"), 16)
            for n, w in enumerate((a["wq"], a["wk"], a["wv"])):
                sp.dma_start(small_raw[:, n, :], w).then_inc(s("small_in"), 16)
            sp.dma_start(wc_raw[:], a["wc"].rearrange("(k p) d -> p k d", p=P)).then_inc(s("small_in"), 16)
            for n, w in enumerate((a["wd"], a["wu"])):
                sp.dma_start(wdu_raw[:, n, :, :], w.rearrange("(k p) g -> p k g", p=P)).then_inc(s("small_in"), 16)
            sp.dma_start(mask_nat[:], a["mask"].rearrange("b o (k l) -> (b o k) l", l=P)).then_inc(s("small_in"), 16)
            for k in range(2):
                sp.dma_start(ctx_all[k], a["ctx"][halves[k]].rearrange("b c l -> c b l")).then_inc(s(f"ctx_half{k}_in"), 16)
            for k in range(2):
                sp.wait_ge(s(f"toep{k}_free"), 1)
                sp.sem_inc(s(f"toep{k}_free"), -1)
            sp.wait_ge(s("toeps_written"), 16)
            sp.sem_inc(s("toeps_written"), -16)
            for k in range(2):
                sp.dma_start(toep[k][:], scr_toeps[k]).then_inc(s(f"toep{k}_loaded"), 16)
            for h in range(H):
                sp.dma_start(mask32_all[8 * h:8 * h + 8, :, :], a["mask"].rearrange("b o (r l) -> (o r) b l", l=32)
                             ).then_inc(s("mask32_in"), 16)
            for tile, src in ((out_b, a["out_b"]), (norm_w, a["norm_w"]), (bv, a["bv"])):
                n = src.shape[0]
                sp.dma_start(tile[:], bass.AP(src.tensor, 0, [[0, P], [1, n]])).then_inc(s("vectors_in"), 16)
            for n, src in enumerate((a["bq"], a["bk"])):
                sp.dma_start(bqk[:, n:n + 1], src.rearrange("(p o) -> p o", o=1)).then_inc(s("vectors_in"), 16)
            for n, src in enumerate((a["temperature"], a["scale"])):
                sp.dma_start(temp_scale[:, n:n + 1], bass.AP(src.tensor, 0, [[0, P], [1, 1]])).then_inc(s("vectors_in"), 16)
            sp.wait_ge(s("genes_clear"), 1)
            sp.sem_inc(s("genes_clear"), -1)
            sp.dma_start(genes[:, :, 0:GD], a["genes"].rearrange("(k p) c -> p k c", p=P)).then_inc(s("genes_in"), 16)
            with sp.Fori(0, H // 2 - 1) as i:
                for k in range(2):
                    sp.wait_ge(s(f"toep{k}_free"), 1)
                    sp.sem_inc(s(f"toep{k}_free"), -1)
                    sp.dma_start(toep[k][:], scr_toeps[2 * i + 2 + k]).then_inc(s(f"toep{k}_loaded"), 16)
            sp.wait_ge(s("clear_sp"), 1)
            sp.sem_inc(s("clear_sp"), -1)
            sp.wait_ge(s("bias_parts_ready"), 1)
            sp.sem_inc(s("bias_parts_ready"), -1)
            for r in range(NT):
                for n in range(2):
                    sp.dma_start(b6[r:r + 1, HID * n:HID * (n + 1)], bias_parts[:, TERM_K[r], n, :]).then_inc(
                        s("b6_loaded"), 16)
            sp.wait_ge(s("mask_parts_ready"), 1)
            sp.sem_inc(s("mask_parts_ready"), -1)
            first = 0
            for run in (3, 2, 1):
                terms = slice(first, first + run)
                sp.dma_start(scr_mask[:, 0, terms, :], aug_parts[:, 0, TERM_Q[first]:TERM_Q[first] + 1, :].broadcast_to([B, run, L])
                             ).then_inc(s("mask_terms_written"), 16)
                sp.dma_start(scr_mask[:, 1, terms, :], aug_parts[:, 1, 0:run, :]).then_inc(s("mask_terms_written"), 16)
                first += run
            for k in range(2):
                sp.dma_start(KS[k][ROW_MAX:ROW_MAX + 6, :, :], one_rows[:]).then_inc(s("ks_ones_in"), 16)
            sp.wait_ge(s("mask_terms_written"), 16 * 6)
            sp.sem_inc(s("mask_terms_written"), -(16 * 6))
            sp.wait_ge(s("ks_ones_in"), 32)
            sp.sem_inc(s("ks_ones_in"), -32)
            sp.wait_ge(s("b6_loaded"), 16 * 2 * NT)
            sp.sem_inc(s("b6_loaded"), -(16 * 2 * NT))
            sp.sem_inc(s("b6_ready"), 1)
            sp.wait_ge(s("y_all_ready"), 1)
            sp.sem_inc(s("y_all_ready"), -1)

            def load_x(b):
                sp.wait_ge(s("x_b_free"), 1)
                sp.sem_inc(s("x_b_free"), -1)
                sp.dma_start(x_b[:], a["x"][b]).then_inc(s("x_b_loaded"), 16)
                sp.dma_start(y_in[:], yT[:, :, b, :]).then_inc(s("y_in_loaded"), 16)

            def load_context(b):
                sp.wait_ge(s("ctx_b_free"), 1)
                sp.sem_inc(s("ctx_b_free"), -1)
                sp.dma_start(ctx_b[:], a["ctx"][b]).then_inc(s("ctx_b_loaded"), 16)
                sp.wait_ge(s("mask_b_free"), 1)
                sp.sem_inc(s("mask_b_free"), -1)
                sp.dma_start(mask_b[:], bass.AP(a["mask"].tensor, b * L, [[0, P], [1, L]])).then_inc(
                    s("mask_b_loaded"), 16)

            def write_qk_parts(k):
                sp.wait_ge(s("qk_parts_ready"), 1)
                sp.sem_inc(s("qk_parts_ready"), -1)
                first = 0
                for run in (3, 2, 1):
                    terms = slice(first, first + run)
                    sp.dma_start(scr_q[k, :, terms, :], qk_parts[:, TERM_Q[first], 0:1, :].broadcast_to([P, run, L])
                                 ).then_inc(s("parts_written"), 16)
                    sp.dma_start(scr_k[k, :, terms, :], qk_parts[:, 0:run, 1, :]).then_inc(s("parts_written"), 16)
                    first += run

            def write_attention(k):
                sp.wait_ge(s("o_quad_ready"), 1)
                sp.sem_inc(s("o_quad_ready"), -1)
                for jj in range(4):
                    sp.dma_start(scr_o[k, 4 * jj:4 * jj + 4].rearrange("q d l -> d q l"),
                                 o_quad[32 * jj:32 * jj + HD + 1, :, :]).then_inc(s("o_written"), 16)

            def load_attention(k):
                sp.wait_ge(s("o_written"), 64)
                sp.sem_inc(s("o_written"), -64)
                sp.sem_inc(s("o_quad_free"), 1)
                at = k * H * (HD + 1) * L + HD * L
                sp.dma_start(den32[:], bass.AP(scr_o.tensor, at, [[(HD + 1) * L, H], [32, L // 32], [1, 32]])
                             ).then_inc(s("den_loaded"), 16)
                sp.wait_ge(s("o_nat_free"), 1)
                sp.sem_inc(s("o_nat_free"), -1)
                sp.dma_start(o_nat[:], scr_o[k, :, 0:HD, :]).then_inc(s("o_nat_loaded"), 16)

            def load_stacked_qk(b, k):
                sp.wait_ge(s("parts_written"), 16 * 6)
                sp.sem_inc(s("parts_written"), -(16 * 6))
                sp.sem_inc(s("qk_parts_free"), 1)
                sp.wait_ge(s("qs_free"), 1)
                sp.sem_inc(s("qs_free"), -1)
                at = b * (2 * NT * L)
                sp.dma_start(QS[k][ROW_MASK:ROW_MASK + NT, :, :],
                             bass.AP(scr_mask.tensor, at, [[L, NT], [0, GRP], [1, L]])).then_inc(s("qs_loaded"), 16)
                sp.dma_start(KS[k][ROW_MASK:ROW_MASK + NT, :, :],
                             bass.AP(scr_mask.tensor, at + NT * L, [[L, NT], [0, H], [1, L]])).then_inc(s("qs_loaded"), 16)
                stacked = "(g c) t l -> (c t) g l"
                sp.dma_start(QS[k][0:ROWS, :, :], scr_q[k].rearrange(stacked, g=GRP)).then_inc(s("qs_loaded"), 16)
                for j in range(2):
                    rows = slice(ROWS // 2 * j, ROWS // 2 * (j + 1))
                    sp.dma_start(KS[k][rows, :, :].rearrange("r (g j) l -> r g j l", j=2)[:, :, j, :],
                                 scr_k[k].rearrange(stacked, g=GRP)[rows]).then_inc(s("qs_loaded"), 16)

            def spread_inverses(k):
                sp.wait_ge(s("den_ready"), 1)
                sp.sem_inc(s("den_ready"), -1)
                sp.dma_start(scr_r[k].rearrange("h (r l) -> (h r) l", l=32), den32[:]).then_inc(s("den_written"), 16)
                sp.wait_ge(s("den_written"), 16)
                sp.sem_inc(s("den_written"), -16)
                sp.dma_start(o_den[:], bass.AP(scr_r.tensor, k * H * L, [[L, H], [0, HD], [1, L]])
                             ).then_inc(s("o_nat_loaded"), 16)

            def load_max_rows(k):
                sp.wait_ge(s("nm_rows_ready"), 1)
                sp.sem_inc(s("nm_rows_ready"), -1)
                sp.dma_start(QS[k][ROW_MAX:ROW_MAX + 6, :, :], nm_rows[:]).then_inc(s("max_rows_loaded"), 16)

            def write_result(b):
                sp.wait_ge(s("res_ready"), 1)
                sp.sem_inc(s("res_ready"), -1)
                sp.dma_start(out[b], res[:]).then_inc(s("res_out"), 16)

            load_x(0)
            load_x(1)
            load_context(0)
            load_x(2)
            load_context(1)
            write_qk_parts(0)
            load_stacked_qk(0, 0)
            load_x(3)
            load_context(2)
            write_qk_parts(1)
            load_stacked_qk(1, 1)
            load_max_rows(0)
            load_x(4)
            load_context(3)
            write_attention(0)
            write_qk_parts(0)
            load_attention(0)
            load_stacked_qk(2, 0)
            spread_inverses(0)
            load_max_rows(1)
            load_x(5)
            load_context(4)
            write_attention(1)
            write_qk_parts(1)
            load_attention(1)
            load_stacked_qk(3, 1)
            spread_inverses(1)
            load_max_rows(0)
            with sp.Fori(0, (B - LEAD) // 2) as i:
                load_x(2 * i + 6)
                load_context(2 * i + 5)
                write_attention(0)
                write_qk_parts(0)
                load_attention(0)
                load_stacked_qk(2 * i + 4, 0)
                spread_inverses(0)
                load_max_rows(1)
                write_result(2 * i)
                load_x(2 * i + 7)
                load_context(2 * i + 6)
                write_attention(1)
                write_qk_parts(1)
                load_attention(1)
                load_stacked_qk(2 * i + 5, 1)
                spread_inverses(1)
                load_max_rows(0)
                write_result(2 * i + 1)
            load_context(15)
            write_attention(0)
            write_qk_parts(0)
            load_attention(0)
            load_stacked_qk(14, 0)
            spread_inverses(0)
            load_max_rows(1)
            write_result(10)
            write_attention(1)
            write_qk_parts(1)
            load_attention(1)
            load_stacked_qk(15, 1)
            spread_inverses(1)
            load_max_rows(0)
            write_result(11)
            write_attention(0)
            load_attention(0)
            spread_inverses(0)
            load_max_rows(1)
            write_result(12)
            write_attention(1)
            load_attention(1)
            spread_inverses(1)
            write_result(13)
            write_result(14)
            write_result(15)

            sp.wait_ge(s("res_out"), 16)

        @block.gpsimd
        def _(pool):
            pool.memset(ident[:], 0.0)
            pool.memset(ident16[:], 0.0)
            pool.memset(genes[:], 0.0)
            pool.memset(half_neg[:], -0.5)
            pool.memset(one_rows[:], 1.0)
            pool.drain().then_inc(s("genes_clear"), 1)
            pool.wait_ge(s("toep_row_in"), 32)
            pool.sem_inc(s("toep_row_in"), -32)
            pool.tensor_tensor(toep_row[:, P:P + 1], toep_row[:, P:P + 1], d_col[:], ALU.add).then_inc(
                s("toep_row_ready"), 1)
            for m in (ident, ident16):
                pool.affine_select(out=m[:], in_=m[:], compare_op=ALU.not_equal, fill=1.0, base=0,
                                   pattern=[[-1, P]], channel_multiplier=1)
            rows = one_rows[:].rearrange("r (g j) l -> r g j l", j=2)
            pool.affine_select(out=rows[:, :, 0, :], in_=rows[:, :, 0, :], compare_op=ALU.is_ge, fill=0.0, base=2,
                               pattern=[[0, GRP], [0, L]], channel_multiplier=-1)
            pool.affine_select(out=rows[:, :, 1, :], in_=rows[:, :, 1, :], compare_op=ALU.is_ge, fill=0.0, base=-3,
                               pattern=[[0, GRP], [0, L]], channel_multiplier=1)
            pool.drain().then_inc(s("ident_ready"), 1)
            for k in range(2):
                pool.memset(KS[k][:].bitcast(U32), 0)
                pool.memset(v_aug[k][:], 0.0)
            for k in range(2):
                pool.memset(s6[k][:], 0.0)
            pool.memset(b6[:], 0.0)
            pool.memset(wduT[:], 0.0)
            pool.drain()
            for k in range(2):
                pool.memset(v_aug[k][:, :, :, HD:HD + 1], 1.0)
            pool.drain().then_inc(s("clear_act"), 1)
            pool.sem_inc(s("clear_dve"), 1)
            pool.sem_inc(s("clear_sp"), 1)
            pool.wait_ge(s("var_all_ready"), 1)
            pool.sem_inc(s("var_all_ready"), -1)
            pool.tensor_scalar(rstd_all[:], mv_all[:, :, 1], LN_EPS, 1.0, ALU.add, ALU.mult)
            pool.drain()
            pool.tensor_tensor(rstd_all[:], rstd_all[:], half_neg[:], ALU.pow).then_inc(s("rstd_all_ready"), 1)
            pool.wait_ge(s("mask_rows_in"), 16)
            pool.sem_inc(s("mask_rows_in"), -16)
            pool.tensor_scalar(aug[:, 0, :], mask_rows[:], -NEG, 0.0, ALU.mult, ALU.add)
            pool.tensor_scalar(aug[:, 1, :], mask_rows[:], -1.0, 1.0, ALU.mult, ALU.add)
            pool.drain()
            split3(pool, aug[:], aug_rest[:], [aug_parts[:, :, n, :] for n in range(3)])
            pool.drain().then_inc(s("mask_parts_ready"), 1)
            pool.wait_ge(s("abs_sum_ready"), 1)
            pool.sem_inc(s("abs_sum_ready"), -1)
            pool.partition_all_reduce(gammas[:], abs_sum[:], P, bass.bass_isa.ReduceOp.add).then_inc(
                s("gamma_sum_ready"), 1)
            pool.wait_ge(s("bias_in"), 32)
            pool.sem_inc(s("bias_in"), -32)
            pool.wait_ge(s("gammas_ready"), 1)
            pool.sem_inc(s("gammas_ready"), -1)
            for n in range(2):
                pool.tensor_scalar(bias_nat[:, n, :], bias_nat[:, n, :], inv_gammas[0:16, n:n + 1], 1.0, ALU.mult, ALU.mult)
            pool.drain()
            split3(pool, bias_nat[:], bias_nat[:], [bias_parts[:, n] for n in range(3)])
            pool.drain().then_inc(s("bias_parts_ready"), 1)

            pool.wait_ge(s("seq_all_ready"), 1)
            pool.sem_inc(s("seq_all_ready"), -1)
            with pool.Fori(0, H // 2) as i:
                for k in range(2):
                    pool.wait_ge(s(f"kv{k}_free"), 1)
                    pool.sem_inc(s(f"kv{k}_free"), -1)
                    kh = cT[:].rearrange("p s b c -> p (s b) c")[:, :, bass.ds((2 * i + k) * HD, HD)]
                    shape = [P, KL * B, HD, HD]
                    pool.tensor_tensor(kv[k][:], kh.unsqueeze(3).broadcast_to(shape),
                                       kh.unsqueeze(2).broadcast_to(shape), ALU.mult).then_inc(s(f"kv{k}_ready"), 1)

            pool.sem_inc(s("ctx_b_free"), 1)
            pool.sem_inc(s("o_nat_free"), 1)
            pool.sem_inc(s("x2_free"), 1)
            pool.sem_inc(s("res_out"), 16)

            def normalise(src, dst, mean, var, out_col, done):
                pool.tensor_scalar(col(out_col), col(var), LN_EPS, 1.0, ALU.add, ALU.mult)
                pool.drain()
                pool.tensor_tensor(col(out_col), col(out_col), half_neg[:, 0:1], ALU.pow)
                pool.drain()
                pool.tensor_scalar(dst, src, col(mean), col(out_col), ALU.subtract, ALU.mult).then_inc(s(done), 1)

            def add_attention(b, k):
                pool.wait_ge(s("o_nat_loaded"), 32)
                pool.sem_inc(s("o_nat_loaded"), -32)
                pool.tensor_tensor(attn[:], o_nat[:], o_den[:], ALU.mult)
                pool.drain().then_inc(s("o_nat_free"), 1)
                pool.tensor_tensor(x3[k][:].rearrange("p (k l) -> p k l", l=P), x2_all[:, :, b, :],
                                   attn[:].rearrange("p (k l) -> p k l", l=P), ALU.add).then_inc(s("x3_ready"), 1)

            def normalise_x1(k):
                pool.wait_ge(s("var1_ready"), 1)
                pool.sem_inc(s("var1_ready"), -1)
                normalise(x1[k][:], xn1[:], MEAN1, VAR1, RSTD1, "xn1_ready")
                pool.tensor_tensor(x1b[k][:], x1[k][:], out_b[:], ALU.add)

            def normalise_x3(k):
                pool.wait_ge(s("var3_ready"), 1)
                pool.sem_inc(s("var3_ready"), -1)
                normalise(x3[k][:], xn3[:], MEAN3, VAR3, RSTD3, "xn3_ready")
                pool.drain()
                pool.tensor_tensor(xw[:], xn3[:], norm_w[:], ALU.mult)

            def rms_of_xn3(k):
                pool.wait_ge(s("sq_ready"), 1)
                pool.sem_inc(s("sq_ready"), -1)
                pool.tensor_scalar(col(RR), col(SQ), 1.0 / L, RMS_EPS, ALU.mult, ALU.add)
                pool.drain()
                pool.tensor_tensor(col(RR), col(RR), half_neg[:, 0:1], ALU.pow)
                pool.drain()
                pool.tensor_scalar(xr[k][:], xw[:], col(RR), 1.0, ALU.mult, ALU.mult).then_inc(s("xr_ready"), 1)

            def scale_parts(k):
                pool.wait_ge(s("sx_ready"), 1)
                pool.sem_inc(s("sx_ready"), -1)
                pool.tensor_scalar(col(SG + k), col(QX), gammas[:, 0:1], 0.5, ALU.mult, ALU.mult)
                pool.drain()
                pool.tensor_scalar(col(KAPPA + k), col(QX), gammas[:, 1:2], col(SG + k), ALU.mult, ALU.mult).then_inc(s("sg_ready"), 1)
                pool.tensor_copy(s6[k][:, 0:3], col(SX).broadcast_to([P, 3]))
                pool.drain()
                pool.tensor_tensor(col(R0), col(SX), s6[k][:, 0:1], ALU.subtract)
                pool.drain()
                pool.tensor_copy(s6[k][:, 3:5], col(R0).broadcast_to([P, 2]))
                pool.drain()
                pool.tensor_tensor(s6[k][:, 5:6], col(R0), s6[k][:, 3:4], ALU.subtract).then_inc(s("s6_ready"), 1)

            def split_qk():
                pool.wait_ge(s("qk_ready"), 1)
                pool.sem_inc(s("qk_ready"), -1)
                pool.sem_inc(s("mask_b_free"), 1)
                pool.wait_ge(s("qk_parts_free"), 1)
                pool.sem_inc(s("qk_parts_free"), -1)
                split3(pool, qk[:], qk_rest[:], [qk_parts[:, n, :, :] for n in range(3)])
                pool.drain().then_inc(s("qk_parts_ready"), 1)

            def mask_context():
                pool.wait_ge(s("ctx_b_loaded"), 16)
                pool.sem_inc(s("ctx_b_loaded"), -16)
                pool.wait_ge(s("mask_b_loaded"), 16)
                pool.sem_inc(s("mask_b_loaded"), -16)
                pool.wait_ge(s("ctx_m_free"), 1)
                pool.sem_inc(s("ctx_m_free"), -1)
                pool.tensor_tensor(ctx_m[:], ctx_b[:], mask_b[:], ALU.mult).then_inc(s("ctx_b_free"), 1)
                pool.tensor_scalar(mask_q[:], mask_b[:], QK_SCALE, 1.0, ALU.mult, ALU.mult)
                pool.drain().then_inc(s("ctx_m_ready"), 1)

            def output_scale():
                pool.wait_ge(s("qh_ready"), 1)
                pool.sem_inc(s("qh_ready"), -1)
                pool.tensor_scalar(col(SO), col(QH), gammas[:, 2:3], 1.0 / 127.0, ALU.mult, ALU.mult).then_inc(s("so_ready"), 1)

            def normalise_x2(b):
                pool.wait_ge(s("var2_ready"), 1)
                pool.sem_inc(s("var2_ready"), -1)
                normalise(x2[:], xn2[:], MEAN2, VAR2, RSTD2, "xn2_ready")
                pool.tensor_copy(x2_all[:, :, b, :], x2[:].rearrange("p (k l) -> p k l", l=P)).then_inc(s("x2_free"), 1)

            def down_times_xr(k):
                pool.wait_ge(s("down_ready"), 1)
                pool.sem_inc(s("down_ready"), -1)
                pool.tensor_scalar(col(RSS), col(RS), temp_scale[:, 1:2], 1.0, ALU.mult, ALU.mult)
                pool.tensor_tensor(dx[:], down[:], xr[k][:], ALU.mult).then_inc(s("dx_ready"), 1)

            def final_sum(k):
                pool.wait_ge(s("up_ready"), 1)
                pool.sem_inc(s("up_ready"), -1)
                pool.wait_ge(s("res_out"), 16)
                pool.sem_inc(s("res_out"), -16)
                pool.tensor_tensor(res[:], dxu[:], x3[k][:], ALU.add)
                pool.drain().then_inc(s("res_ready"), 1)

            def split_maxima():
                pool.wait_ge(s("neg_max_ready"), 1)
                pool.sem_inc(s("neg_max_ready"), -1)
                split3(pool, neg_max[:].rearrange("p t (g j) -> p t j g", j=2),
                       nm_rest[:].rearrange("p t (g j) -> p t j g", j=2), [nm_parts[:, :, :, n, :] for n in range(3)])
                pool.drain().then_inc(s("nm_parts_ready"), 1)

            normalise_x1(0)
            scale_parts(0)
            normalise_x1(1)
            mask_context()
            output_scale()
            normalise_x2(0)
            scale_parts(1)
            normalise_x1(0)
            split_qk()
            mask_context()
            output_scale()
            normalise_x2(1)
            scale_parts(0)
            normalise_x1(1)
            split_qk()
            mask_context()
            output_scale()
            normalise_x2(2)
            split_maxima()
            scale_parts(1)
            normalise_x1(0)
            split_qk()
            mask_context()
            output_scale()
            normalise_x2(3)
            split_maxima()
            scale_parts(0)
            add_attention(0, 0)
            normalise_x3(0)
            rms_of_xn3(0)
            normalise_x1(1)
            split_qk()
            mask_context()
            output_scale()
            normalise_x2(4)
            split_maxima()
            scale_parts(1)
            with pool.Fori(0, (B - LEAD) // 2) as i:
                add_attention(2 * i + 1, 1)
                normalise_x3(1)
                rms_of_xn3(1)
                normalise_x1(0)
                split_qk()
                mask_context()
                output_scale()
                normalise_x2(2 * i + 5)
                down_times_xr(0)
                split_maxima()
                final_sum(0)
                scale_parts(0)
                add_attention(2 * i + 2, 0)
                normalise_x3(0)
                rms_of_xn3(0)
                normalise_x1(1)
                split_qk()
                mask_context()
                output_scale()
                normalise_x2(2 * i + 6)
                down_times_xr(1)
                split_maxima()
                final_sum(1)
                scale_parts(1)
            add_attention(11, 1)
            normalise_x3(1)
            rms_of_xn3(1)
            split_qk()
            mask_context()
            output_scale()
            normalise_x2(15)
            down_times_xr(0)
            split_maxima()
            final_sum(0)
            add_attention(12, 0)
            normalise_x3(0)
            rms_of_xn3(0)
            split_qk()
            down_times_xr(1)
            split_maxima()
            final_sum(1)
            add_attention(13, 1)
            normalise_x3(1)
            rms_of_xn3(1)
            down_times_xr(0)
            split_maxima()
            final_sum(0)
            add_attention(14, 0)
            normalise_x3(0)
            rms_of_xn3(0)
            down_times_xr(1)
            final_sum(1)
            add_attention(15, 1)
            normalise_x3(1)
            rms_of_xn3(1)
            down_times_xr(0)
            final_sum(0)
            down_times_xr(1)
            final_sum(1)


        @block.scalar
        def _(act):
            for name in ("seq_T0_taken", "seq_T1_taken", "o_bank_free", "bank5_free",
                         "bank6_free", "bank7_free"):
                act.sem_inc(s(name), 1)
            act.wait_ge(s("toep_row_ready"), 1)
            act.sem_inc(s("toep_row_ready"), -1)
            act.dma_start(scr_toep, toep_row[:]).then_inc(s("toep_written"), 16)
            act.wait_ge(s("toep_written"), 16)
            act.sem_inc(s("toep_written"), -16)
            act.dma_start(scr_toeps, bass.AP(scr_toep.tensor, P, [[P + L, H], [-1, P], [1, L]])).then_inc(
                s("toeps_written"), 16)
            for n, w in enumerate(("gate", "val", "out")):
                act.wait_ge(s(f"{w}_w_in"), 16)
                act.sem_inc(s(f"{w}_w_in"), -16)
                act.activation(w_int[n][:], w_raw[:, n, :], ACT.Abs, accum_out=abs_sum[:, n:n + 1])
            act.drain().then_inc(s("abs_sum_ready"), 1)

            def sequence(dst, n):
                act.wait_ge(s(f"x_T{n % 2}_ready"), 1)
                act.sem_inc(s(f"x_T{n % 2}_ready"), -1)
                act.activation(dst[:, :, 2 * n:2 * n + 2, :].rearrange("p s b c -> p b s c"),
                               banks[6 + n % 2][:].rearrange("p (b s c) -> p b s c", b=2, c=C), ACT.Copy
                               ).then_inc(s(f"seq_T{n % 2}_taken"), 1)

            for n in range(B // 2):
                sequence(qT, n)
            for n in range(3):
                for half in range(2):
                    act.wait_ge(s("w_T_ready"), 1)
                    act.sem_inc(s("w_T_ready"), -1)
                    src = bank16[2 * n + half][:, :].rearrange("p (k c) -> p k c", c=P)
                    if n < 2:
                        for dk in range(KL):
                            dst = wgvT[:, dk, HID * n + 512 * half:HID * n + 512 * (half + 1)]
                            act.activation(dst.rearrange("p (k c) -> p k c", c=P), src[:, 4 * dk:4 * dk + 4, :], ACT.Copy)
                    else:
                        dst = woT[:, 4 * half:4 * half + 4, :].rearrange("p k (o c) -> p (k o) c", c=P)
                        act.activation(dst, src, ACT.Copy)
                if n == 1:
                    act.drain().then_inc(s("w_T_taken"), 1)
            act.wait_ge(s("small_T_ready"), 1)
            act.sem_inc(s("small_T_ready"), -1)
            act.activation(wqkvT[:].rearrange("p n c -> p (n c)"), banks[0][:, 0:3 * P], ACT.Copy)
            act.activation(mask_cols[:].rearrange("p b k -> p (b k)"), banks[0][:, 3 * P:3 * P + KL * B], ACT.Copy)
            for dk in range(KL):
                act.activation(wcT[:, dk, :], banks[1 + dk][:], ACT.Copy)
            act.wait_ge(s("clear_act"), 1)
            act.sem_inc(s("clear_act"), -1)
            act.activation(wduT[0:GD, :], banks[3][0:GD, :], ACT.Copy)
            act.drain().then_inc(s("small_T_taken"), 1)

            def exps(*ns):
                for n in ns:
                    act.wait_ge(s(f"scores{n % 2}_ready"), 1)
                    act.sem_inc(s(f"scores{n % 2}_ready"), -1)
                    if n == 15:
                        act.sem_inc(s("qs_free"), 1)
                    act.activation(probs[n % 8][:], SC[n % 2][:], ACT.Exp).then_inc(s(f"scores{n % 2}_free"), 1)

            def collect(q):
                act.wait_ge(s("o_bank_ready"), 1)
                act.sem_inc(s("o_bank_ready"), -1)
                if q == 0:
                    act.wait_ge(s("o_quad_free"), 1)
                    act.sem_inc(s("o_quad_free"), -1)
                act.activation(o_quad[:, q, :], O[:, 0:L], ACT.Copy).then_inc(s("o_bank_free"), 1)

            def tanh_gate(k, half):
                act.wait_ge(s("gate_ready"), 1)
                act.sem_inc(s("gate_ready"), -1)
                act.wait_ge(s("tanh_free"), 1)
                act.sem_inc(s("tanh_free"), -1)
                if half == 0:
                    act.wait_ge(s("sg_ready"), 1)
                    act.sem_inc(s("sg_ready"), -1)
                act.activation(tanh_g[:], X5[:], ACT.Tanh, scale=col(SG + k)).then_inc(s("tanh_ready"), 1)

            def square_xn3():
                act.wait_ge(s("xn3_ready"), 1)
                act.sem_inc(s("xn3_ready"), -1)
                act.activation(xn3_sq[:], xn3[:], ACT.Square, accum_out=col(SQ)).then_inc(s("sq_ready"), 1)

            def copy_xqT():
                act.wait_ge(s("banks56_filled"), 1)
                act.sem_inc(s("banks56_filled"), -1)
                act.activation(xqT[:].rearrange("p k t -> p (k t)"), X5[:, 0:L], ACT.Copy, bias=-MAGIC).then_inc(
                    s("banks56_copied"), 1)

            def copy_xrT():
                act.wait_ge(s("bank7_filled"), 1)
                act.sem_inc(s("bank7_filled"), -1)
                act.activation(xrT[:].rearrange("p k t -> p (k t)"), X7[:, 0:L], ACT.Copy).then_inc(s("bank7_copied"), 1)

            def copy_s6T():
                act.wait_ge(s("banks56_filled"), 1)
                act.sem_inc(s("banks56_filled"), -1)
                act.activation(s6T[:], bank16[5][:, 0:P], ACT.Copy).then_inc(s("banks56_copied"), 1)

            def copy_logits(k):
                act.wait_ge(s("bank7_filled"), 1)
                act.sem_inc(s("bank7_filled"), -1)
                act.activation(logits[k][:], X7[:], ACT.Copy).then_inc(s("logits_ready"), 1)
                act.drain().then_inc(s("bank7_free"), 1)

            def quantise_hidden():
                act.wait_ge(s("sh_ready"), 1)
                act.sem_inc(s("sh_ready"), -1)
                for half in range(2):
                    cols = slice(512 * half, 512 * (half + 1))
                    act.activation(hid[:, cols], hid[:, cols], ACT.Copy, scale=col(SH), bias=MAGIC).then_inc(s("hq_ready"), 1)

            def exp_logits(k):
                act.wait_ge(s("nb_ready"), 1)
                act.sem_inc(s("nb_ready"), -1)
                act.activation(e_all[:], logits[k][:], ACT.Exp, bias=col(NB), scale=temp_scale[:, 0:1]).then_inc(
                    s("e_ready"), 1)

            def copy_hidden_T():
                for half, bank in enumerate((X5, X6)):
                    act.wait_ge(s("banks56_filled"), 1)
                    act.sem_inc(s("banks56_filled"), -1)
                    act.activation(hqT[:, 4 * half:4 * half + 4, :].rearrange("p k t -> p (k t)"), bank[:], ACT.Copy,
                                   bias=-MAGIC).then_inc(s("banks56_copied"), 1)

            def finish_attention():
                collect(3)
                act.sem_inc(s("v_aug_free"), 1)
                act.drain().then_inc(s("o_quad_ready"), 1)

            def copy_wT():
                act.wait_ge(s("gene_bank_filled"), 1)
                act.sem_inc(s("gene_bank_filled"), -1)
                act.activation(wT[:].rearrange("p k t -> p (k t)"), X7[:], ACT.Copy).then_inc(s("gene_bank_copied"), 1)

            def copy_exprT():
                act.wait_ge(s("gene_bank_filled"), 1)
                act.sem_inc(s("gene_bank_filled"), -1)
                act.activation(exprT[:], X7[:, 0:P], ACT.Copy).then_inc(s("gene_bank_copied"), 1)

            def tanh_down():
                act.wait_ge(s("gene_bank_filled"), 1)
                act.sem_inc(s("gene_bank_filled"), -1)
                act.wait_ge(s("rs_ready"), 1)
                act.sem_inc(s("rs_ready"), -1)
                act.activation(down[:], X7[:, 0:L], ACT.Tanh, scale=col(RS)).then_inc(s("down_ready"), 1)

            def copy_max_rows():
                act.wait_ge(s("nm_T_ready"), 1)
                act.sem_inc(s("nm_T_ready"), -1)
                act.activation(nm_rows[:], bank16[0][0:6 * GRP, 0:L], ACT.Copy).then_inc(s("max0_free"), 1)
                act.drain().then_inc(s("nm_rows_ready"), 1)

            copy_xqT()
            copy_s6T()
            tanh_gate(0, 0)
            tanh_gate(0, 1)
            quantise_hidden()
            copy_hidden_T()
            copy_xqT()
            copy_s6T()
            tanh_gate(1, 0)
            tanh_gate(1, 1)
            quantise_hidden()
            copy_hidden_T()
            copy_xqT()
            copy_s6T()
            tanh_gate(0, 0)
            tanh_gate(0, 1)
            quantise_hidden()
            copy_hidden_T()
            copy_max_rows()
            copy_xqT()
            exps(0, 1)
            exps(2, 3)
            exps(4, 5)
            copy_s6T()
            collect(0)
            exps(6, 7)
            tanh_gate(1, 0)
            exps(8, 9)
            collect(1)
            exps(10, 11)
            tanh_gate(1, 1)
            exps(12, 13)
            collect(2)
            exps(14, 15)
            finish_attention()
            quantise_hidden()
            copy_hidden_T()
            copy_max_rows()
            copy_xqT()
            exps(0, 1)
            exps(2, 3)
            exps(4, 5)
            copy_s6T()
            square_xn3()
            collect(0)
            exps(6, 7)
            tanh_gate(0, 0)
            exps(8, 9)
            collect(1)
            exps(10, 11)
            copy_xrT()
            tanh_gate(0, 1)
            exps(12, 13)
            collect(2)
            exps(14, 15)
            copy_logits(0)
            finish_attention()
            quantise_hidden()
            copy_hidden_T()
            copy_max_rows()
            with act.Fori(0, (B - LEAD) // 2) as i:
                copy_xqT()
                exps(0, 1)
                exps(2, 3)
                exps(4, 5)
                copy_s6T()
                square_xn3()
                collect(0)
                exps(6, 7)
                tanh_gate(1, 0)
                exps(8, 9)
                collect(1)
                exps(10, 11)
                copy_xrT()
                tanh_gate(1, 1)
                exps(12, 13)
                collect(2)
                exps(14, 15)
                exp_logits(0)
                copy_logits(1)
                finish_attention()
                quantise_hidden()
                copy_hidden_T()
                copy_wT()
                copy_exprT()
                tanh_down()
                copy_max_rows()
                copy_xqT()
                exps(0, 1)
                exps(2, 3)
                exps(4, 5)
                copy_s6T()
                square_xn3()
                collect(0)
                exps(6, 7)
                tanh_gate(0, 0)
                exps(8, 9)
                collect(1)
                exps(10, 11)
                copy_xrT()
                tanh_gate(0, 1)
                exps(12, 13)
                collect(2)
                exps(14, 15)
                exp_logits(1)
                copy_logits(0)
                finish_attention()
                quantise_hidden()
                copy_hidden_T()
                copy_wT()
                copy_exprT()
                tanh_down()
                copy_max_rows()
            copy_xqT()
            exps(0, 1)
            exps(2, 3)
            exps(4, 5)
            copy_s6T()
            square_xn3()
            collect(0)
            exps(6, 7)
            tanh_gate(1, 0)
            exps(8, 9)
            collect(1)
            exps(10, 11)
            copy_xrT()
            tanh_gate(1, 1)
            exps(12, 13)
            collect(2)
            exps(14, 15)
            exp_logits(0)
            copy_logits(1)
            finish_attention()
            quantise_hidden()
            copy_hidden_T()
            copy_wT()
            copy_exprT()
            tanh_down()
            copy_max_rows()
            exps(0, 1)
            exps(2, 3)
            exps(4, 5)
            square_xn3()
            collect(0)
            exps(6, 7)
            exps(8, 9)
            collect(1)
            exps(10, 11)
            copy_xrT()
            exps(12, 13)
            collect(2)
            exps(14, 15)
            exp_logits(1)
            copy_logits(0)
            finish_attention()
            copy_wT()
            copy_exprT()
            tanh_down()
            copy_max_rows()
            exps(0, 1)
            exps(2, 3)
            exps(4, 5)
            square_xn3()
            collect(0)
            exps(6, 7)
            exps(8, 9)
            collect(1)
            exps(10, 11)
            copy_xrT()
            exps(12, 13)
            collect(2)
            exps(14, 15)
            exp_logits(0)
            copy_logits(1)
            finish_attention()
            copy_wT()
            copy_exprT()
            tanh_down()
            copy_max_rows()
            exps(0, 1)
            exps(2, 3)
            exps(4, 5)
            square_xn3()
            collect(0)
            exps(6, 7)
            exps(8, 9)
            collect(1)
            exps(10, 11)
            copy_xrT()
            exps(12, 13)
            collect(2)
            exps(14, 15)
            exp_logits(1)
            copy_logits(0)
            finish_attention()
            copy_wT()
            copy_exprT()
            tanh_down()
            square_xn3()
            copy_xrT()
            exp_logits(0)
            copy_logits(1)
            copy_wT()
            copy_exprT()
            tanh_down()
            exp_logits(1)
            copy_wT()
            copy_exprT()
            tanh_down()


        @block.tensor
        def _(pe):
            for name in ("toep0_free", "toep1_free", "ctx_m_free"):
                pe.sem_inc(s(name), 1)
            for name in ("qs_free", "v_aug_free"):
                pe.sem_inc(s(name), 2)
            pe.wait_ge(s("ident_ready"), 1)
            pe.sem_inc(s("ident_ready"), -1)

            def sequence(src, n, of_x):
                pe.wait_ge(s(f"seq_T{n % 2}_taken"), 1)
                pe.sem_inc(s(f"seq_T{n % 2}_taken"), -1)
                for b in range(2):
                    for sh in range(KL):
                        at = (KL * b + sh) * P
                        mm = pe.transpose(banks[6 + n % 2][:, at:at + P], src[:, b, sh * P:(sh + 1) * P], ident[:])
                mm.then_inc(s(f"x_T{n % 2}_ready") if of_x else s(f"ctx_T{n % 2}_ready"), 1)

            for n in range(B // 2):
                pe.wait_ge(s("xn_ready"), 1)
                pe.sem_inc(s("xn_ready"), -1)
                sequence(x_all[:, 2 * n:2 * n + 2, :], n, True)
            for n in range(3):
                pe.wait_ge(s("w_int_ready"), 1)
                pe.sem_inc(s("w_int_ready"), -1)
                for half in range(2):
                    for m in range(8):
                        if n < 2:
                            at = (4 * half + m % 4) * L + (m // 4) * P
                        else:
                            at = (m % 2) * HID + (4 * half + m // 2) * P
                        mm = pe.transpose(bank16[2 * n + half][:, m * P:(m + 1) * P], w_int[n][:, at:at + P], ident16[:])
                    mm.then_inc(s("w_T_ready"), 1)
            for n in range(B // 2):
                if n % (B // 4) == 0:
                    pe.wait_ge(s(f"ctx_half{n // (B // 4)}_in"), 16)
                    pe.sem_inc(s(f"ctx_half{n // (B // 4)}_in"), -16)
                at = 2 * n % (B // 2)
                sequence(ctx_all[n // (B // 4)][:, at:at + 2, :], n, False)
            pe.drain().then_inc(s("kv0_free"), 1)
            pe.sem_inc(s("kv1_free"), 1)
            pe.wait_ge(s("small_in"), 16 * 7)
            pe.sem_inc(s("small_in"), -(16 * 7))
            pe.wait_ge(s("w_T_taken"), 1)
            pe.sem_inc(s("w_T_taken"), -1)
            for n in range(3):
                pe.transpose(banks[0][:, n * P:(n + 1) * P], small_raw[:, n, :], ident[:])
            pe.transpose(banks[0][:, 3 * P:3 * P + KL * B], mask_nat[:], ident[0:KL * B, 0:KL * B])
            for dk in range(KL):
                for k in range(KG):
                    pe.transpose(banks[1 + dk][:, k * P:(k + 1) * P], wc_raw[:, k, dk * P:(dk + 1) * P], ident[:])
            for n in range(2):
                for k in range(2):
                    mm = pe.transpose(banks[3][0:GD, (2 * n + k) * P:(2 * n + k + 1) * P], wdu_raw[:, n, k, :], ident[:])
            mm.then_inc(s("small_T_ready"), 1)
            for k in range(2):
                pe.wait_ge(s(f"seq_T{k}_taken"), 1)
                pe.sem_inc(s(f"seq_T{k}_taken"), -1)
            pe.wait_ge(s("small_T_taken"), 1)
            pe.sem_inc(s("small_T_taken"), -1)
            def operands(k):
                pe.wait_ge(s(f"toep{k}_loaded"), 16)
                pe.sem_inc(s(f"toep{k}_loaded"), -16)
                pe.wait_ge(s(f"kv{k}_ready"), 1)
                pe.sem_inc(s(f"kv{k}_ready"), -1)
                pe.wait_ge(s(f"conv{k}_free"), 1)
                pe.sem_inc(s(f"conv{k}_free"), -1)

            def convolve(k, last):
                rhs = kv[k][:].rearrange("p (s b) j i -> p s (b j i)", b=B)
                for lh in range(KL):
                    for bh in range(2):
                        cols = slice(512 * bh, 512 * (bh + 1))
                        for sh in range(lh + 1):
                            mm = pe.matmul(banks[4 * k + 2 * lh + bh][:], toep[k][:, (lh - sh) * P:(lh - sh + 1) * P],
                                           rhs[:, sh, cols], start=(sh == 0), stop=(sh == lh))
                mm.then_inc(s(f"conv{k}_ready"), 1)
                if not last:
                    operands(1 - k)
                pe.drain().then_inc(s(f"kv{k}_free"), 1)
                pe.sem_inc(s(f"toep{k}_free"), 1)

            operands(0)
            with pe.Fori(0, H // 4 - 1) as i:
                for k in (0, 1, 0, 1):
                    convolve(k, last=False)
            for n in range(4):
                convolve(n % 2, last=(n == 3))
            for k in range(2):
                pe.wait_ge(s(f"conv{k}_free"), 1)
                pe.sem_inc(s(f"conv{k}_free"), -1)
            pe.wait_ge(s("b6_ready"), 1)
            pe.sem_inc(s("b6_ready"), -1)
            pe.wait_ge(s("genes_in"), 16)
            pe.sem_inc(s("genes_in"), -16)

            def maxima(k, *ns):
                for h in ns:
                    pe.wait_ge(s(f"max{h % 2}_free"), 1)
                    pe.sem_inc(s(f"max{h % 2}_free"), -1)
                    for th in range(KL):
                        mm = pe.matmul(M[h % 2][:, th * L:(th + 1) * L], QS[k][0:K_MAX, h // 2, th * P:(th + 1) * P],
                                       KS[k][0:K_MAX, h, :], start=True, stop=True)
                    mm.then_inc(s(f"max{h % 2}_ready"), 1)

            def scores(k, *ns):
                for n in ns:
                    h = heads[n]
                    if n >= 2:
                        pe.wait_ge(s(f"scores{n % 2}_free"), 1)
                        pe.sem_inc(s(f"scores{n % 2}_free"), -1)
                    for sh in range(KL):
                        mm = pe.matmul(SC[n % 2][:, sh * L:(sh + 1) * L], KS[k][0:K_ALL, h, sh * P:(sh + 1) * P],
                                       QS[k][0:K_ALL, h // 2, :], start=True, stop=True)
                    mm.then_inc(s(f"scores{n % 2}_ready"), 1)

            def values(k, q):
                pe.wait_ge(s("o_bank_free"), 1)
                pe.sem_inc(s("o_bank_free"), -1)
                for sh in range(KL):
                    for jj in range(4):
                        mm = pe.matmul(O[32 * jj:32 * jj + 32, 0:L], v_aug[k][:, sh, heads[4 * q + jj], :],
                                       probs[(4 * q + jj) % 8][:, sh * L:(sh + 1) * L], start=(sh == 0), stop=(sh == 1))
                mm.then_inc(s("o_bank_ready"), 1)

            def gates(half):
                for n, bank in enumerate((X5, X6)):
                    at = HID * n + 512 * half
                    if half == 1 and n == 0:
                        pe.wait_ge(s("gate_bank_free"), 1)
                        pe.sem_inc(s("gate_bank_free"), -1)
                    if half == 0 and n == 1:
                        pe.wait_ge(s("bank6_free"), 1)
                        pe.sem_inc(s("bank6_free"), -1)
                    if half == 1 and n == 1:
                        pe.wait_ge(s("val_bank_free"), 1)
                        pe.sem_inc(s("val_bank_free"), -1)
                    for k in range(KL):
                        pe.matmul(bank[:], xqT[:, k, :], wgvT[:, k, at:at + 512], start=(k == 0), stop=False)
                    pe.matmul(bank[:], s6T[:], b6[:, at:at + 512], start=False, stop=True).then_inc(
                        s("gate_ready") if n == 0 else s("value_ready"), 1)

            def transpose_y():
                pe.wait_ge(s("y_in_loaded"), 16)
                pe.sem_inc(s("y_in_loaded"), -16)
                pe.wait_ge(s("bank7_free"), 1)
                pe.sem_inc(s("bank7_free"), -1)
                for sh in range(KL):
                    mm = pe.transpose(X7[:, sh * P:(sh + 1) * P], y_in[:, sh, :], ident[:])
                mm.then_inc(s("y_T_ready"), 1)

            def first_maxima(k):
                pe.wait_ge(s("qs_loaded"), 16 * 5)
                pe.sem_inc(s("qs_loaded"), -(16 * 5))
                maxima(k, 0)

            def project_qk():
                pe.wait_ge(s("ctx_m_ready"), 1)
                pe.sem_inc(s("ctx_m_ready"), -1)
                pe.wait_ge(s("xn2_ready"), 1)
                pe.sem_inc(s("xn2_ready"), -1)
                pe.wait_ge(s("bank6_free"), 1)
                pe.sem_inc(s("bank6_free"), -1)
                pe.matmul(X6[:, L:2 * L], wqkvT[:, 1, :], ctx_m[:], start=True, stop=True)
                pe.matmul(X6[:, 0:L], wqkvT[:, 0, :], xn2[:], start=True, stop=True).then_inc(s("qk_bank_ready"), 1)

            def first_scores(k):
                pe.wait_ge(s("v_aug_ready"), 1)
                pe.sem_inc(s("v_aug_ready"), -1)
                pe.wait_ge(s("max_rows_loaded"), 16)
                pe.sem_inc(s("max_rows_loaded"), -16)
                scores(k, 0)

            def transpose_xq(k):
                pe.wait_ge(s("xq_ready"), 1)
                pe.sem_inc(s("xq_ready"), -1)
                pe.wait_ge(s("bank5_free"), 1)
                pe.sem_inc(s("bank5_free"), -1)
                for n in range(KL):
                    mm = pe.transpose(X5[:, n * P:(n + 1) * P], xq[k][:, n * P:(n + 1) * P], ident[:])
                mm.then_inc(s("banks56_filled"), 1)

            def transpose_s6(k):
                pe.wait_ge(s("s6_ready"), 1)
                pe.sem_inc(s("s6_ready"), -1)
                pe.wait_ge(s("banks56_copied"), 1)
                pe.sem_inc(s("banks56_copied"), -1)
                pe.transpose(bank16[5][:, 0:P], s6[k][:], ident16[:]).then_inc(s("banks56_filled"), 1)

            def transpose_xr(k):
                pe.wait_ge(s("xr_ready"), 1)
                pe.sem_inc(s("xr_ready"), -1)
                pe.wait_ge(s("bank7_free"), 1)
                pe.sem_inc(s("bank7_free"), -1)
                for n in range(KL):
                    mm = pe.transpose(X7[:, n * P:(n + 1) * P], xr[k][:, n * P:(n + 1) * P], ident[:])
                mm.then_inc(s("bank7_filled"), 1)

            def gates0():
                pe.wait_ge(s("banks56_copied"), 1)
                pe.sem_inc(s("banks56_copied"), -1)
                gates(0)

            def logits_product():
                pe.wait_ge(s("bank7_copied"), 1)
                pe.sem_inc(s("bank7_copied"), -1)
                for k in range(KL):
                    mm = pe.matmul(X7[:], xrT[:, k, :], wcT[:, k, :], start=(k == 0), stop=(k == KL - 1))
                mm.then_inc(s("bank7_filled"), 1)

            def transpose_hidden():
                pe.wait_ge(s("gate_bank_free"), 1)
                pe.sem_inc(s("gate_bank_free"), -1)
                pe.wait_ge(s("val_bank_free"), 1)
                pe.sem_inc(s("val_bank_free"), -1)
                for half, bank in enumerate((X5, X6)):
                    pe.wait_ge(s("hq_ready"), 1)
                    pe.sem_inc(s("hq_ready"), -1)
                    for m in range(4):
                        n = 4 * half + m
                        mm = pe.transpose(bank[:, m * P:(m + 1) * P], hid[:, n * P:(n + 1) * P], ident[:])
                    mm.then_inc(s("banks56_filled"), 1)

            def ffn_product():
                for half in range(2):
                    pe.wait_ge(s("banks56_copied"), 1)
                    pe.sem_inc(s("banks56_copied"), -1)
                    for k in range(KH // 2 * half, KH // 2 * (half + 1)):
                        mm = pe.matmul(X5[:, 0:L], hqT[:, k, :], woT[:, k, :], start=(k == 0), stop=(k == KH - 1))
                mm.then_inc(s("ffn_ready"), 1)
                pe.sem_inc(s("bank6_free"), 1)

            def last_values(k):
                pe.wait_ge(s("scores0_free"), 1)
                pe.sem_inc(s("scores0_free"), -1)
                pe.wait_ge(s("scores1_free"), 1)
                pe.sem_inc(s("scores1_free"), -1)
                values(k, 3)

            def project_v():
                pe.wait_ge(s("bank7_free"), 1)
                pe.sem_inc(s("bank7_free"), -1)
                for sh in range(KL):
                    mm = pe.matmul(X7[:, sh * P:(sh + 1) * P], ctx_m[:, sh * P:(sh + 1) * P], wqkvT[:, 2, :],
                                   start=True, stop=True)
                mm.then_inc(s("v_bank_ready"), 1)
                pe.drain().then_inc(s("ctx_m_free"), 1)

            def transpose_weights():
                pe.wait_ge(s("w_top_ready"), 1)
                pe.sem_inc(s("w_top_ready"), -1)
                pe.wait_ge(s("bank7_free"), 1)
                pe.sem_inc(s("bank7_free"), -1)
                for k in range(KG):
                    mm = pe.transpose(X7[:, k * P:(k + 1) * P], w_top[:, k * P:(k + 1) * P], ident[:])
                mm.then_inc(s("gene_bank_filled"), 1)

            def expressed():
                pe.wait_ge(s("gene_bank_copied"), 1)
                pe.sem_inc(s("gene_bank_copied"), -1)
                for k in range(KG):
                    mm = pe.matmul(X7[:, 0:P], genes[:, k, :], wT[:, k, :], start=(k == 0), stop=(k == KG - 1))
                mm.then_inc(s("gene_bank_filled"), 1)

            def down_up():
                pe.wait_ge(s("gene_bank_copied"), 1)
                pe.sem_inc(s("gene_bank_copied"), -1)
                pe.matmul(X7[:], exprT[:], wduT[:], start=True, stop=True).then_inc(s("gene_bank_filled"), 1)

            def transpose_maxima():
                pe.wait_ge(s("nm_parts_ready"), 1)
                pe.sem_inc(s("nm_parts_ready"), -1)
                pe.wait_ge(s("max0_free"), 1)
                pe.sem_inc(s("max0_free"), -1)
                for th in range(KL):
                    mm = pe.transpose(bank16[0][0:6 * GRP, th * P:(th + 1) * P],
                                      nm_parts[:, th].rearrange("p j n g -> p (j n g)"), ident16[:])
                mm.then_inc(s("nm_T_ready"), 1)

            transpose_y()
            transpose_xq(0)
            transpose_s6(0)
            transpose_y()
            gates0()
            gates(1)
            transpose_hidden()
            ffn_product()
            transpose_xq(1)
            project_qk()
            transpose_s6(1)
            transpose_y()
            gates0()
            gates(1)
            project_v()
            transpose_hidden()
            ffn_product()
            transpose_xq(0)
            project_qk()
            first_maxima(0)
            maxima(0, 1, 2)
            transpose_s6(0)
            maxima(0, 3)
            transpose_y()
            maxima(0, 4, 5)
            gates0()
            maxima(0, 6, 7)
            gates(1)
            project_v()
            maxima(0, 8, 9)
            transpose_hidden()
            ffn_product()
            maxima(0, 10, 11)
            maxima(0, 12, 13)
            maxima(0, 14, 15)
            transpose_maxima()
            transpose_xq(1)
            project_qk()
            first_maxima(1)
            maxima(1, 1)
            first_scores(0)
            maxima(1, 2)
            scores(0, 1)
            transpose_s6(1)
            scores(0, 2)
            maxima(1, 3)
            transpose_y()
            scores(0, 3)
            maxima(1, 4)
            scores(0, 4)
            maxima(1, 5)
            scores(0, 5)
            values(0, 0)
            scores(0, 6, 7)
            gates0()
            scores(0, 8, 9)
            maxima(1, 6)
            values(0, 1)
            scores(0, 10, 11)
            maxima(1, 7)
            gates(1)
            scores(0, 12, 13)
            values(0, 2)
            scores(0, 14, 15)
            last_values(0)
            project_v()
            maxima(1, 8, 9)
            transpose_hidden()
            ffn_product()
            maxima(1, 10, 11)
            maxima(1, 12, 13)
            maxima(1, 14, 15)
            transpose_maxima()
            transpose_xq(0)
            project_qk()
            first_maxima(0)
            maxima(0, 1)
            first_scores(1)
            maxima(0, 2)
            scores(1, 1)
            transpose_s6(0)
            scores(1, 2)
            maxima(0, 3)
            scores(1, 3)
            transpose_y()
            maxima(0, 4)
            scores(1, 4)
            maxima(0, 5)
            scores(1, 5)
            values(1, 0)
            scores(1, 6, 7)
            gates0()
            scores(1, 8, 9)
            maxima(0, 6)
            values(1, 1)
            scores(1, 10, 11)
            maxima(0, 7)
            transpose_xr(0)
            gates(1)
            scores(1, 12, 13)
            values(1, 2)
            scores(1, 14, 15)
            logits_product()
            last_values(1)
            maxima(0, 8, 9)
            project_v()
            transpose_hidden()
            ffn_product()
            maxima(0, 10, 11)
            maxima(0, 12, 13)
            maxima(0, 14, 15)
            transpose_maxima()
            with pe.Fori(0, (B - LEAD) // 2) as i:
                transpose_xq(1)
                project_qk()
                first_maxima(1)
                maxima(1, 1)
                first_scores(0)
                maxima(1, 2)
                scores(0, 1)
                transpose_s6(1)
                scores(0, 2)
                maxima(1, 3)
                scores(0, 3)
                maxima(1, 4)
                scores(0, 4)
                transpose_y()
                maxima(1, 5)
                scores(0, 5)
                values(0, 0)
                scores(0, 6, 7)
                gates0()
                scores(0, 8)
                maxima(1, 6)
                scores(0, 9)
                values(0, 1)
                scores(0, 10, 11)
                maxima(1, 7)
                transpose_xr(1)
                gates(1)
                scores(0, 12, 13)
                values(0, 2)
                scores(0, 14, 15)
                logits_product()
                last_values(0)
                project_v()
                maxima(1, 8, 9)
                transpose_hidden()
                ffn_product()
                maxima(1, 10, 11)
                transpose_weights()
                expressed()
                maxima(1, 12, 13)
                down_up()
                maxima(1, 14, 15)
                transpose_maxima()
                transpose_xq(0)
                project_qk()
                first_maxima(0)
                maxima(0, 1)
                first_scores(1)
                maxima(0, 2)
                scores(1, 1)
                transpose_s6(0)
                scores(1, 2)
                maxima(0, 3)
                scores(1, 3)
                maxima(0, 4)
                scores(1, 4)
                transpose_y()
                maxima(0, 5)
                scores(1, 5)
                values(1, 0)
                scores(1, 6, 7)
                gates0()
                scores(1, 8)
                maxima(0, 6)
                scores(1, 9)
                values(1, 1)
                scores(1, 10, 11)
                maxima(0, 7)
                transpose_xr(0)
                gates(1)
                scores(1, 12, 13)
                values(1, 2)
                scores(1, 14, 15)
                logits_product()
                last_values(1)
                project_v()
                maxima(0, 8, 9)
                transpose_hidden()
                ffn_product()
                maxima(0, 10, 11)
                transpose_weights()
                expressed()
                maxima(0, 12, 13)
                down_up()
                maxima(0, 14, 15)
                transpose_maxima()
            transpose_xq(1)
            project_qk()
            first_maxima(1)
            maxima(1, 1)
            first_scores(0)
            maxima(1, 2)
            scores(0, 1)
            transpose_s6(1)
            scores(0, 2)
            maxima(1, 3)
            scores(0, 3)
            maxima(1, 4)
            scores(0, 4)
            maxima(1, 5)
            scores(0, 5)
            values(0, 0)
            scores(0, 6, 7)
            gates0()
            scores(0, 8, 9)
            maxima(1, 6)
            values(0, 1)
            scores(0, 10, 11)
            maxima(1, 7)
            transpose_xr(1)
            gates(1)
            scores(0, 12, 13)
            values(0, 2)
            scores(0, 14, 15)
            logits_product()
            last_values(0)
            project_v()
            maxima(1, 8, 9)
            transpose_hidden()
            ffn_product()
            maxima(1, 10, 11)
            transpose_weights()
            expressed()
            maxima(1, 12)
            down_up()
            maxima(1, 13, 14, 15)
            transpose_maxima()
            project_qk()
            first_maxima(0)
            maxima(0, 1)
            first_scores(1)
            maxima(0, 2)
            scores(1, 1, 2)
            maxima(0, 3)
            scores(1, 3)
            maxima(0, 4)
            scores(1, 4)
            maxima(0, 5)
            scores(1, 5)
            values(1, 0)
            scores(1, 6, 7)
            scores(1, 8, 9)
            maxima(0, 6)
            values(1, 1)
            scores(1, 10, 11)
            maxima(0, 7)
            transpose_xr(0)
            scores(1, 12, 13)
            values(1, 2)
            scores(1, 14, 15)
            logits_product()
            last_values(1)
            project_v()
            maxima(0, 8, 9)
            maxima(0, 10, 11)
            transpose_weights()
            expressed()
            maxima(0, 12, 13)
            down_up()
            maxima(0, 14, 15)
            transpose_maxima()
            first_maxima(1)
            maxima(1, 1)
            first_scores(0)
            maxima(1, 2)
            scores(0, 1, 2)
            maxima(1, 3)
            scores(0, 3)
            maxima(1, 4)
            scores(0, 4)
            maxima(1, 5)
            scores(0, 5)
            values(0, 0)
            scores(0, 6, 7)
            scores(0, 8, 9)
            maxima(1, 6)
            values(0, 1)
            scores(0, 10, 11)
            maxima(1, 7)
            transpose_xr(1)
            scores(0, 12, 13)
            values(0, 2)
            scores(0, 14, 15)
            logits_product()
            last_values(0)
            maxima(1, 8, 9)
            maxima(1, 10, 11)
            transpose_weights()
            expressed()
            maxima(1, 12, 13)
            down_up()
            maxima(1, 14, 15)
            transpose_maxima()
            first_scores(1)
            scores(1, 1, 2)
            scores(1, 3, 4, 5)
            values(1, 0)
            scores(1, 6, 7)
            scores(1, 8, 9)
            values(1, 1)
            scores(1, 10, 11)
            transpose_xr(0)
            scores(1, 12, 13)
            values(1, 2)
            scores(1, 14, 15)
            logits_product()
            last_values(1)
            transpose_weights()
            expressed()
            down_up()
            transpose_xr(1)
            logits_product()
            transpose_weights()
            expressed()
            down_up()
            transpose_weights()
            expressed()
            down_up()


        @block.vector
        def _(dve):
            for name in ("conv0_free", "conv1_free", "x_b_free", "mask_b_free", "tanh_free",
                         "max0_free", "max1_free"):
                dve.sem_inc(s(name), 1)
            for k in range(2):
                dve.wait_ge(s(f"x_half{k}_in"), 16)
                dve.sem_inc(s(f"x_half{k}_in"), -16)
                for b in range(B // 2 * k, B // 2 * (k + 1)):
                    dve.bn_stats(stat6_all[:, b, :], x_all[:, b, :])
            dve.drain()
            for b in range(B):
                dve.bn_aggr(mv_all[:, b, :], stat6_all[:, b, :])
            dve.drain().then_inc(s("var_all_ready"), 1)
            dve.wait_ge(s("rstd_all_ready"), 1)
            dve.sem_inc(s("rstd_all_ready"), -1)
            for n in range(B // 2):
                for b in (2 * n, 2 * n + 1):
                    mm = dve.tensor_scalar(x_all[:, b, :], x_all[:, b, :], mv_all[:, b, 0:1], rstd_all[:, b:b + 1],
                                           ALU.subtract, ALU.mult)
                mm.then_inc(s("xn_ready"), 1)
            dve.wait_ge(s("gamma_sum_ready"), 1)
            dve.sem_inc(s("gamma_sum_ready"), -1)
            dve.tensor_scalar(gammas[:], gammas[:], 1.0 / (HID * L), 1e-5, ALU.mult, ALU.max)
            dve.drain()
            dve.reciprocal(inv_gammas[:], gammas[:])
            dve.drain().then_inc(s("gammas_ready"), 1)
            for n in range(3):
                dve.tensor_scalar(w_raw[:, n, :], w_raw[:, n, :], inv_gammas[:, n:n + 1], 1.0, ALU.mult, ALU.min)
                dve.drain()
                dve.tensor_scalar(w_raw[:, n, :], w_raw[:, n, :], -1.0, MAGIC, ALU.max, ALU.add)
                dve.drain()
                dve.tensor_scalar(w_int[n][:], w_raw[:, n, :], -MAGIC, None, ALU.add).then_inc(s("w_int_ready"), 1)
            for n in range(B // 2):
                dve.wait_ge(s(f"ctx_T{n % 2}_ready"), 1)
                dve.sem_inc(s(f"ctx_T{n % 2}_ready"), -1)
                dve.tensor_copy(cT[:, :, 2 * n:2 * n + 2, :].rearrange("p s b c -> p b s c"),
                                banks[6 + n % 2][:].rearrange("p (b s c) -> p b s c", b=2, c=C)
                                ).then_inc(s(f"seq_T{n % 2}_taken"), 1)
            dve.drain().then_inc(s("seq_all_ready"), 1)
            with dve.Fori(0, H // 4) as i:
                for n in range(4):
                    k = n % 2
                    dve.wait_ge(s(f"conv{k}_ready"), 1)
                    dve.sem_inc(s(f"conv{k}_ready"), -1)
                    q = qT[:].rearrange("p s b c -> p (s b) c")[:, :, bass.ds((4 * i + n) * HD, HD)]
                    for lh in range(KL):
                        for bh in range(2):
                            r = slice(lh * B + bh * (B // 2), lh * B + (bh + 1) * (B // 2))
                            dve.tensor_tensor(prod[:, r], banks[4 * k + 2 * lh + bh][:].rearrange("p (b j i) -> p b j i", j=HD, i=HD),
                                              q[:, r, :].unsqueeze(2).broadcast_to([P, B // 2, HD, HD]), ALU.mult)
                    dve.drain().then_inc(s(f"conv{k}_free"), 1)
                    dve.tensor_reduce(yT[:].rearrange("p s b c -> p (s b) c")[:, :, bass.ds((4 * i + n) * HD, HD)], prod,
                                      AX.X, ALU.add)
                    dve.drain()
            dve.sem_inc(s("y_all_ready"), 1)
            dve.wait_ge(s("clear_dve"), 1)
            dve.sem_inc(s("clear_dve"), -1)
            dve.wait_ge(s("vectors_in"), 16 * 7)
            dve.sem_inc(s("vectors_in"), -(16 * 7))
            dve.wait_ge(s("mask32_in"), 16 * H)
            dve.sem_inc(s("mask32_in"), -(16 * H))
            dve.tensor_scalar(temp_scale[:, 0:1], temp_scale[:, 0:1], 0.1, None, ALU.max)
            dve.drain()
            dve.reciprocal(temp_scale[:, 0:1], temp_scale[:, 0:1])

            def statistics(src, n, mean, done):
                dve.bn_stats(st6[:, n, :], src)
                dve.drain()
                dve.bn_aggr(col(mean, 2), st6[:, n, :]).then_inc(s(done), 1)

            def maxima(*ns):
                for h in ns:
                    dve.wait_ge(s(f"max{h % 2}_ready"), 1)
                    dve.sem_inc(s(f"max{h % 2}_ready"), -1)
                    dve.tensor_reduce(neg_max[:, :, h:h + 1], M[h % 2][:].rearrange("p (t s) -> p t s", s=L), AX.X,
                                      ALU.max, negate=True).then_inc(s(f"max{h % 2}_free"), 1)

            def topk_round():
                dve.drain()
                dve.match_replace(left[:], best[:], left[:], GONE)
                dve.drain()
                dve.max(best[:], left[:])

            def gate_times_value(half):
                dve.wait_ge(s("tanh_ready"), 1)
                dve.sem_inc(s("tanh_ready"), -1)
                h = hid[:, 512 * half:512 * (half + 1)]
                dve.scalar_tensor_tensor(h, tanh_g[:], 1.0, X5[:], ALU.add, ALU.mult).then_inc(s("gate_bank_free"), 1)
                dve.drain().then_inc(s("tanh_free"), 1)
                dve.wait_ge(s("value_ready"), 1)
                dve.sem_inc(s("value_ready"), -1)
                dve.tensor_tensor(h, h, X6[:], ALU.mult).then_inc(s("val_bank_free"), 1)

            def first_sum(k):
                dve.wait_ge(s("y_T_ready"), 1)
                dve.sem_inc(s("y_T_ready"), -1)
                dve.wait_ge(s("x_b_loaded"), 16)
                dve.sem_inc(s("x_b_loaded"), -16)
                dve.tensor_tensor(x1[k][:], X7[:, 0:L], x_b[:], ALU.add).then_inc(s("bank7_free"), 1)
                dve.drain().then_inc(s("x_b_free"), 1)
                statistics(x1[k][:], 0, MEAN1, "var1_ready")

            def statistics_x3(k):
                dve.wait_ge(s("x3_ready"), 1)
                dve.sem_inc(s("x3_ready"), -1)
                statistics(x3[k][:], 1, MEAN3, "var3_ready")

            def bias_and_mask_qk():
                dve.wait_ge(s("qk_bank_ready"), 1)
                dve.sem_inc(s("qk_bank_ready"), -1)
                dve.scalar_tensor_tensor(qk[:, 1, :], mask_b[:], bqk[:, 1:2], X6[:, L:2 * L], ALU.mult, ALU.add)
                dve.scalar_tensor_tensor(qk[:, 0, :], X6[:, 0:L], bqk[:, 0:1], mask_q[:], ALU.add, ALU.mult
                                         ).then_inc(s("qk_ready"), 1)
                dve.drain().then_inc(s("bank6_free"), 1)

            def quantise_x(k):
                dve.wait_ge(s("xn1_ready"), 1)
                dve.sem_inc(s("xn1_ready"), -1)
                dve.tensor_reduce(col(QX), xn1[:], AX.X, ALU.max, apply_absolute_value=True)
                dve.drain()
                dve.tensor_scalar(col(QX), col(QX), 1e-5, 1.0 / 127.0, ALU.max, ALU.mult)
                dve.drain()
                dve.reciprocal(col(SX), col(QX)).then_inc(s("sx_ready"), 1)
                dve.drain()
                dve.tensor_scalar(xq[k][:], xn1[:], col(SX), MAGIC, ALU.mult, ALU.add).then_inc(s("xq_ready"), 1)

            def top_first(k):
                dve.wait_ge(s("logits_ready"), 1)
                dve.sem_inc(s("logits_ready"), -1)
                dve.max(best[:], logits[k][:])
                dve.drain()
                dve.tensor_scalar(col(NB), best[:, 0:1], temp_scale[:, 0:1], -1.0, ALU.mult, ALU.mult).then_inc(
                    s("nb_ready"), 1)
                dve.match_replace(left[:], best[:], logits[k][:], GONE)

            def top_next():
                dve.drain()
                dve.max(best[:], left[:])

            def hidden_scales(k):
                dve.drain()
                dve.tensor_reduce(col(QH), hid[:], AX.X, ALU.max, apply_absolute_value=True)
                dve.drain()
                dve.tensor_scalar(col(QH), col(QH), col(KAPPA + k), 1e-5, ALU.mult, ALU.max).then_inc(s("qh_ready"), 1)
                dve.drain()
                dve.reciprocal(col(RH), col(QH))
                dve.drain()
                dve.tensor_scalar(col(SH), col(RH), col(KAPPA + k), 127.0, ALU.mult, ALU.mult).then_inc(s("sh_ready"), 1)

            def top_weights():
                dve.drain()
                dve.match_replace(left[:], best[:], left[:], GONE)
                dve.wait_ge(s("e_ready"), 1)
                dve.sem_inc(s("e_ready"), -1)
                dve.drain()
                dve.scalar_tensor_tensor(w_top[:], left[:], GONE, e_all[:], ALU.is_equal, ALU.mult,
                                         accum_out=col(WS))
                dve.drain().then_inc(s("w_top_ready"), 1)
                dve.reciprocal(col(RS), col(WS)).then_inc(s("rs_ready"), 1)

            def second_sum(k):
                dve.wait_ge(s("ffn_ready"), 1)
                dve.sem_inc(s("ffn_ready"), -1)
                dve.wait_ge(s("so_ready"), 1)
                dve.sem_inc(s("so_ready"), -1)
                dve.wait_ge(s("x2_free"), 1)
                dve.sem_inc(s("x2_free"), -1)
                dve.scalar_tensor_tensor(x2[:], X5[:, 0:L], col(SO), x1b[k][:], ALU.mult, ALU.add).then_inc(s("bank5_free"), 1)
                dve.drain()
                statistics(x2[:], 2, MEAN2, "var2_ready")

            def value_operand(b, k):
                dve.wait_ge(s("v_bank_ready"), 1)
                dve.sem_inc(s("v_bank_ready"), -1)
                dve.wait_ge(s("v_aug_free"), 1)
                dve.sem_inc(s("v_aug_free"), -1)
                for sh in range(KL):
                    mm = dve.scalar_tensor_tensor(v_aug[k][:, sh, :, 0:HD], bv[:].rearrange("p (h d) -> p h d", d=HD),
                                                  mask_cols[:, b, sh:sh + 1],
                                                  X7[:, sh * P:(sh + 1) * P].rearrange("p (h d) -> p h d", d=HD),
                                                  ALU.mult, ALU.add)
                mm.then_inc(s("bank7_free"), 1)
                dve.drain().then_inc(s("v_aug_ready"), 1)

            def inverse_denominators(b):
                dve.wait_ge(s("den_loaded"), 16)
                dve.sem_inc(s("den_loaded"), -16)
                dve.reciprocal(den32[:], den32[:])
                dve.drain()
                dve.tensor_tensor(den32[:], den32[:], mask32_all[:, b, :], ALU.mult).then_inc(s("den_ready"), 1)

            def last_maximum():
                maxima(15)
                dve.drain().then_inc(s("neg_max_ready"), 1)

            def down_times_up():
                dve.wait_ge(s("dx_ready"), 1)
                dve.sem_inc(s("dx_ready"), -1)
                dve.scalar_tensor_tensor(dxu[:], X7[:, L:2 * L], col(RSS), dx[:], ALU.mult, ALU.mult).then_inc(
                    s("bank7_free"), 1)
                dve.drain().then_inc(s("up_ready"), 1)

            first_sum(0)
            quantise_x(0)
            first_sum(1)
            gate_times_value(0)
            gate_times_value(1)
            quantise_x(1)
            hidden_scales(0)
            second_sum(0)
            bias_and_mask_qk()
            first_sum(0)
            gate_times_value(0)
            gate_times_value(1)
            quantise_x(0)
            hidden_scales(1)
            value_operand(0, 0)
            second_sum(1)
            maxima(0, 1)
            maxima(2, 3)
            bias_and_mask_qk()
            maxima(4, 5)
            first_sum(1)
            gate_times_value(0)
            maxima(6, 7)
            gate_times_value(1)
            quantise_x(1)
            hidden_scales(0)
            maxima(8, 9)
            value_operand(1, 1)
            second_sum(0)
            maxima(10, 11)
            maxima(12, 13, 14)
            last_maximum()
            maxima(0, 1)
            maxima(2, 3)
            bias_and_mask_qk()
            maxima(4, 5)
            first_sum(0)
            gate_times_value(0)
            maxima(6, 7)
            gate_times_value(1)
            quantise_x(0)
            hidden_scales(1)
            maxima(8, 9)
            value_operand(2, 0)
            second_sum(1)
            maxima(10, 11)
            maxima(12, 13)
            inverse_denominators(0)
            maxima(14)
            last_maximum()
            maxima(0, 1)
            statistics_x3(0)
            maxima(2, 3)
            bias_and_mask_qk()
            maxima(4, 5)
            first_sum(1)
            gate_times_value(0)
            maxima(6, 7)
            gate_times_value(1)
            quantise_x(1)
            hidden_scales(0)
            maxima(8, 9)
            value_operand(3, 1)
            second_sum(0)
            maxima(10, 11)
            maxima(12, 13)
            inverse_denominators(1)
            maxima(14)
            last_maximum()
            with dve.Fori(0, (B - LEAD) // 2) as i:
                top_first(0)
                top_next()
                topk_round()
                maxima(0, 1)
                statistics_x3(1)
                maxima(2, 3)
                bias_and_mask_qk()
                maxima(4, 5)
                topk_round()
                first_sum(0)
                gate_times_value(0)
                maxima(6, 7)
                quantise_x(0)
                gate_times_value(1)
                hidden_scales(1)
                top_weights()
                maxima(8, 9)
                value_operand(2 * i + 4, 0)
                second_sum(1)
                maxima(10, 11)
                maxima(12, 13)
                inverse_denominators(2 * i + 2)
                maxima(14)
                last_maximum()
                down_times_up()
                top_first(1)
                top_next()
                topk_round()
                maxima(0, 1)
                statistics_x3(0)
                maxima(2, 3)
                bias_and_mask_qk()
                maxima(4, 5)
                topk_round()
                first_sum(1)
                gate_times_value(0)
                maxima(6, 7)
                quantise_x(1)
                gate_times_value(1)
                hidden_scales(0)
                top_weights()
                maxima(8, 9)
                value_operand(2 * i + 5, 1)
                second_sum(0)
                maxima(10, 11)
                maxima(12, 13)
                inverse_denominators(2 * i + 3)
                maxima(14)
                last_maximum()
                down_times_up()
            top_first(0)
            top_next()
            topk_round()
            maxima(0, 1)
            statistics_x3(1)
            maxima(2, 3)
            bias_and_mask_qk()
            maxima(4, 5)
            topk_round()
            gate_times_value(0)
            maxima(6, 7)
            gate_times_value(1)
            hidden_scales(1)
            top_weights()
            maxima(8, 9)
            value_operand(14, 0)
            second_sum(1)
            maxima(10, 11)
            maxima(12, 13)
            inverse_denominators(12)
            maxima(14)
            last_maximum()
            down_times_up()
            top_first(1)
            top_next()
            topk_round()
            maxima(0, 1)
            statistics_x3(0)
            maxima(2, 3)
            bias_and_mask_qk()
            maxima(4, 5)
            topk_round()
            maxima(6, 7)
            top_weights()
            maxima(8, 9)
            value_operand(15, 1)
            maxima(10, 11)
            maxima(12, 13)
            inverse_denominators(13)
            maxima(14)
            last_maximum()
            down_times_up()
            top_first(0)
            top_next()
            topk_round()
            maxima(0, 1)
            statistics_x3(1)
            maxima(2, 3)
            maxima(4, 5)
            topk_round()
            maxima(6, 7)
            top_weights()
            maxima(8, 9)
            maxima(10, 11)
            maxima(12, 13)
            inverse_denominators(14)
            maxima(14)
            last_maximum()
            down_times_up()
            top_first(1)
            top_next()
            topk_round()
            statistics_x3(0)
            topk_round()
            top_weights()
            inverse_denominators(15)
            down_times_up()
            top_first(0)
            top_next()
            topk_round()
            statistics_x3(1)
            topk_round()
            top_weights()
            down_times_up()
            top_first(1)
            top_next()
            topk_round()
            topk_round()
            top_weights()
            down_times_up()



_IN = dict(x="x", ctx_2048="ctx", mask_Bx1x2048_fk1="mask", L0_xattn_ssm_kernel="ssm", L0_xattn_D="d",
           L0_ffn_gate_w="gate_w", L0_ffn_gate_b="gate_b", L0_ffn_val_w="val_w", L0_ffn_val_b="val_b",
           L0_ffn_out_w="out_w", L0_ffn_out_b="out_b", L1_xattn_Wq="wq", L1_xattn_bq="bq", L1_xattn_Wk="wk",
           L1_xattn_bk="bk", L1_xattn_Wv="wv", L1_xattn_bv="bv", L1_ffn_Wc="wc", L1_ffn_temperature="temperature",
           L1_ffn_genes="genes", L1_ffn_Wd="wd", L1_ffn_Wu="wu", L1_ffn_norm_w="norm_w", L1_ffn_scale="scale")


def kernel(**inputs):
    import numpy as np
    import concourse.bacc as bacc
    from concourse.bass_utils import run_bass_kernel_spmd

    nc = bacc.Bacc("TRN2", target_bir_lowering=False, num_devices=1)
    arrays, aps = {}, {}
    for name, short in _IN.items():
        v = np.ascontiguousarray(inputs[name])
        if v.ndim == 0:
            v = v.reshape(1)
        if short == "ssm":
            v = np.concatenate([np.zeros((v.shape[0], P), v.dtype), v], axis=1)
        arrays["in_" + short] = v
        aps[short] = nc.dram_tensor("in_" + short, v.shape, mybir.dt.from_np(v.dtype), kind="ExternalInput").ap()
    shape = inputs["x"].shape
    out = nc.dram_tensor("out_x", shape, F32, kind="ExternalOutput").ap()
    build(nc, aps, out)
    r = run_bass_kernel_spmd(nc, [arrays], core_ids=[0])
    return r.results[0]["out_x"]
```
